# Optimizing a Trainium2 kernel written in Bass

```python
import numpy as np
import jax
import jax.numpy as jnp

def _softmax(x, axis=-1):
    return jax.nn.softmax(x, axis=axis)

def _gelu(x):
    return jax.nn.gelu(x, approximate=True)

def _silu(x):
    return jax.nn.silu(x)

def _sigmoid(x):
    return jax.nn.sigmoid(x)

def _layernorm(x, axis=-1, eps=1e-05):
    m = jnp.mean(x, axis=axis, keepdims=True)
    v = jnp.var(x, axis=axis, keepdims=True)
    return (x - m) / jnp.sqrt(v + eps)

def _scatter_add(tgt, idx, src, axis=0):
    return tgt.at[idx].add(src)

def _segment_sum(src, seg, n):
    return jax.ops.segment_sum(src, seg, n)
kernel_name = 'mk_gnn_preln_d4_gnn_r64_0ad8f8'

def setup_inputs(seed: int=0):
    np.random.seed(seed)
    _w = jnp.asarray

    def _rec_inputs():
        import jax
        import jax.numpy as jnp
        _gk = jax.random.key(seed)
        x = -0.000202 + 1 * jax.random.normal(jax.random.fold_in(_gk, 1), (50000, 128), jnp.float32)
        src = jax.random.randint(jax.random.fold_in(_gk, 2), (12500,), 0, 50000, jnp.int32)
        dst = jnp.minimum((50000 * jax.random.uniform(jax.random.fold_in(_gk, 3), (12500,)) ** 2.0).astype(jnp.int32), 49999)
        _o = jnp.argsort(dst, stable=True)
        src = src[_o]
        dst = dst[_o]
        return (x, src, dst)
    x, src, dst = _rec_inputs()

    def _L0_gnn_setup():
        import jax, jax.numpy as jnp
        import numpy as np
        N_NODES = 50000
        N_EDGES = 25000
        D = 128

        def _sage_conv(x, src, dst, W_l, b_l, W_r, n_nodes):
            msgs = x[src]
            summed = jax.ops.segment_sum(msgs, dst, num_segments=n_nodes)
            deg = jax.ops.segment_sum(jnp.ones((src.shape[0],), x.dtype), dst, num_segments=n_nodes)
            mean = summed / jnp.maximum(deg, 1.0)[:, None]
            return mean @ W_l + b_l + x @ W_r
        key = jax.random.key(seed)
        ks = jax.random.split(key, 7)
        s = 1.0 / np.sqrt(D)
        x = jax.random.normal(ks[0], (N_NODES, D), dtype=jnp.float32)
        edge_index = jax.random.randint(ks[1], (2, N_EDGES), 0, N_NODES, dtype=jnp.int64)
        W1_l = jax.random.normal(ks[2], (D, D), dtype=jnp.float32) * s
        b1 = jnp.zeros((D,), dtype=jnp.float32)
        W1_r = jax.random.normal(ks[3], (D, D), dtype=jnp.float32) * s
        W2_l = jax.random.normal(ks[4], (D, D), dtype=jnp.float32) * s
        b2 = jnp.zeros((D,), dtype=jnp.float32)
        W2_r = jax.random.normal(ks[5], (D, D), dtype=jnp.float32) * s
        return {'x': x, 'edge_index': edge_index, 'W1_l': W1_l, 'b1': b1, 'W1_r': W1_r, 'W2_l': W2_l, 'b2': b2, 'W2_r': W2_r}
    _L0_gnn_all = _L0_gnn_setup()
    _L0_gnn_in = {k: v for k, v in _L0_gnn_all.items() if k in ('W1_l', 'b1', 'W1_r', 'W2_l', 'b2', 'W2_r')}
    del _L0_gnn_all

    def _L1_gnn_setup():
        import jax, jax.numpy as jnp
        import numpy as np
        N_NODES = 50000
        N_EDGES = 9375
        D = 128
        LN_EPS = 1e-05

        def _layer_norm(f, gamma, beta):
            mu = jnp.mean(f, axis=-1, keepdims=True)
            var = jnp.mean(jnp.square(f - mu), axis=-1, keepdims=True)
            return (f - mu) * jax.lax.rsqrt(var + LN_EPS) * gamma + beta
        key = jax.random.key(seed)
        k1, k2, k3, k4 = jax.random.split(key, 4)
        x = jax.random.normal(k1, (N_NODES, D), dtype=jnp.float32)
        edge_index = jax.random.randint(k2, (2, N_EDGES), 0, N_NODES, dtype=jnp.int64)
        scale = 1.0 / np.sqrt(D)
        W_l = jax.random.normal(k3, (D, D), dtype=jnp.float32) * scale
        W_r = jax.random.normal(k4, (D, D), dtype=jnp.float32) * scale
        b_l = jnp.zeros((D,), dtype=jnp.float32)
        gamma = jnp.ones((D,), dtype=jnp.float32)
        beta = jnp.zeros((D,), dtype=jnp.float32)
        return {'x': x, 'edge_index': edge_index, 'W_l': W_l, 'b_l': b_l, 'W_r': W_r, 'gamma': gamma, 'beta': beta}
    _L1_gnn_all = _L1_gnn_setup()
    _L1_gnn_in = {k: v for k, v in _L1_gnn_all.items() if k in ('W_l', 'b_l', 'W_r', 'gamma', 'beta')}
    del _L1_gnn_all

    def _L2_gnn_setup():
        import jax, jax.numpy as jnp
        import numpy as np
        N_NODES = 50000
        N_EDGES = 12500
        IN_DIM = 128
        HID = 32
        HEADS = 4
        OUT_DIM = 128
        NEG_SLOPE = 0.2

        def gat_conv(x, src, dst, W, a_src, a_dst, bias, concat):
            N = x.shape[0]
            H, C = a_src.shape
            h = (x @ W.T).reshape(N, H, C)
            alpha_src = jnp.einsum('nhc,hc->nh', h, a_src)
            alpha_dst = jnp.einsum('nhc,hc->nh', h, a_dst)
            e = jax.nn.leaky_relu(alpha_src[src] + alpha_dst[dst], NEG_SLOPE)
            m = jax.ops.segment_max(e, dst, num_segments=N)
            m = jnp.where(jnp.isfinite(m), m, 0.0)
            p = jnp.exp(e - m[dst])
            s = jax.ops.segment_sum(p, dst, num_segments=N)
            a = p / (s[dst] + 1e-16)
            out = jax.ops.segment_sum(h[src] * a[:, :, None], dst, num_segments=N)
            if concat:
                return out.reshape(N, H * C) + bias
            return out.mean(axis=1) + bias
        key = jax.random.key(seed)
        ks = jax.random.split(key, 12)
        x = jax.random.normal(ks[0], (N_NODES, IN_DIM), dtype=jnp.float32)
        edge_index = jax.random.randint(ks[1], (2, N_EDGES), 0, N_NODES, dtype=jnp.int64)
        W1 = jax.random.normal(ks[2], (HEADS * HID, IN_DIM), dtype=jnp.float32) * (1.0 / np.sqrt(IN_DIM))
        att_src1 = jax.random.normal(ks[3], (HEADS, HID), dtype=jnp.float32) * (1.0 / np.sqrt(HID))
        att_dst1 = jax.random.normal(ks[4], (HEADS, HID), dtype=jnp.float32) * (1.0 / np.sqrt(HID))
        bias1 = jnp.zeros((HEADS * HID,), dtype=jnp.float32)
        W2 = jax.random.normal(ks[5], (OUT_DIM, HEADS * HID), dtype=jnp.float32) * (1.0 / np.sqrt(HEADS * HID))
        att_src2 = jax.random.normal(ks[6], (1, OUT_DIM), dtype=jnp.float32) * (1.0 / np.sqrt(OUT_DIM))
        att_dst2 = jax.random.normal(ks[7], (1, OUT_DIM), dtype=jnp.float32) * (1.0 / np.sqrt(OUT_DIM))
        bias2 = jnp.zeros((OUT_DIM,), dtype=jnp.float32)
        return {'x': x, 'edge_index': edge_index, 'W1': W1, 'att_src1': att_src1, 'att_dst1': att_dst1, 'bias1': bias1, 'W2': W2, 'att_src2': att_src2, 'att_dst2': att_dst2, 'bias2': bias2}
    _L2_gnn_all = _L2_gnn_setup()
    _L2_gnn_in = {k: v for k, v in _L2_gnn_all.items() if k in ('W1', 'att_src1', 'att_dst1', 'bias1', 'W2', 'att_src2', 'att_dst2', 'bias2')}
    del _L2_gnn_all

    def _L3_gnn_setup():
        import jax, jax.numpy as jnp
        import numpy as np
        N, E, D, H, C = (50000, 12500, 128, 256, 128)

        def _ln(x, g, b, eps=1e-05):
            m = jnp.mean(x, axis=-1, keepdims=True)
            v = jnp.mean((x - m) ** 2, axis=-1, keepdims=True)
            return (x - m) * jax.lax.rsqrt(v + eps) * g + b

        def _sage_layer(h, W1, b1, g1, bt1, W2, b2, g2, bt2):
            h = jax.nn.relu(_ln(h @ W1 + b1, g1, bt1))
            h = h @ W2 + b2
            if g2 is not None:
                h = jax.nn.relu(_ln(h, g2, bt2))
            return h
        key = jax.random.key(seed)
        ks = jax.random.split(key, 10)
        w = lambda k, s: jax.random.normal(k, s, jnp.float32) * 0.05
        inp = {'embed': jax.random.normal(ks[0], (N, D), jnp.float32), 'norm': jax.random.uniform(ks[1], (N, 1), jnp.float32), 'src': jax.random.randint(ks[2], (E,), 0, N, jnp.int32), 'dst': jax.random.randint(ks[3], (E,), 0, N, jnp.int32)}
        dims = [(2 * D, H, H, False), (2 * H, H, H, False), (2 * H, H, C, True)]
        for i, (fi, hd, fo, last) in enumerate(dims, start=1):
            kk = jax.random.split(ks[3 + i], 2)
            inp[f'W1_{i}'] = w(kk[0], (fi, hd))
            inp[f'b1_{i}'] = jnp.zeros((hd,), jnp.float32)
            inp[f'g1_{i}'] = jnp.ones((hd,), jnp.float32)
            inp[f'bt1_{i}'] = jnp.zeros((hd,), jnp.float32)
            inp[f'W2_{i}'] = w(kk[1], (hd, fo))
            inp[f'b2_{i}'] = jnp.zeros((fo,), jnp.float32)
            if not last:
                inp[f'g2_{i}'] = jnp.ones((fo,), jnp.float32)
                inp[f'bt2_{i}'] = jnp.zeros((fo,), jnp.float32)
        return inp
    _L3_gnn_all = _L3_gnn_setup()
    _L3_gnn_in = {k: v for k, v in _L3_gnn_all.items() if k in ('W1_1', 'b1_1', 'g1_1', 'bt1_1', 'W2_1', 'b2_1', 'g2_1', 'bt2_1', 'W1_2', 'b1_2', 'g1_2', 'bt1_2', 'W2_2', 'b2_2', 'g2_2', 'bt2_2', 'W1_3', 'b1_3', 'g1_3', 'bt1_3', 'W2_3', 'b2_3')}
    del _L3_gnn_all
    return {'x': x, 'src': src, 'dst': dst, 'L0_gnn_W1_l': _L0_gnn_in['W1_l'], 'L0_gnn_b1': _L0_gnn_in['b1'], 'L0_gnn_W1_r': _L0_gnn_in['W1_r'], 'L0_gnn_W2_l': _L0_gnn_in['W2_l'], 'L0_gnn_b2': _L0_gnn_in['b2'], 'L0_gnn_W2_r': _L0_gnn_in['W2_r'], 'L1_gnn_W_l': _L1_gnn_in['W_l'], 'L1_gnn_b_l': _L1_gnn_in['b_l'], 'L1_gnn_W_r': _L1_gnn_in['W_r'], 'L1_gnn_gamma': _L1_gnn_in['gamma'], 'L1_gnn_beta': _L1_gnn_in['beta'], 'L2_gnn_W1': _L2_gnn_in['W1'], 'L2_gnn_att_src1': _L2_gnn_in['att_src1'], 'L2_gnn_att_dst1': _L2_gnn_in['att_dst1'], 'L2_gnn_bias1': _L2_gnn_in['bias1'], 'L2_gnn_W2': _L2_gnn_in['W2'], 'L2_gnn_att_src2': _L2_gnn_in['att_src2'], 'L2_gnn_att_dst2': _L2_gnn_in['att_dst2'], 'L2_gnn_bias2': _L2_gnn_in['bias2'], 'L3_gnn_W1_1': _L3_gnn_in['W1_1'], 'L3_gnn_b1_1': _L3_gnn_in['b1_1'], 'L3_gnn_g1_1': _L3_gnn_in['g1_1'], 'L3_gnn_bt1_1': _L3_gnn_in['bt1_1'], 'L3_gnn_W2_1': _L3_gnn_in['W2_1'], 'L3_gnn_b2_1': _L3_gnn_in['b2_1'], 'L3_gnn_g2_1': _L3_gnn_in['g2_1'], 'L3_gnn_bt2_1': _L3_gnn_in['bt2_1'], 'L3_gnn_W1_2': _L3_gnn_in['W1_2'], 'L3_gnn_b1_2': _L3_gnn_in['b1_2'], 'L3_gnn_g1_2': _L3_gnn_in['g1_2'], 'L3_gnn_bt1_2': _L3_gnn_in['bt1_2'], 'L3_gnn_W2_2': _L3_gnn_in['W2_2'], 'L3_gnn_b2_2': _L3_gnn_in['b2_2'], 'L3_gnn_g2_2': _L3_gnn_in['g2_2'], 'L3_gnn_bt2_2': _L3_gnn_in['bt2_2'], 'L3_gnn_W1_3': _L3_gnn_in['W1_3'], 'L3_gnn_b1_3': _L3_gnn_in['b1_3'], 'L3_gnn_g1_3': _L3_gnn_in['g1_3'], 'L3_gnn_bt1_3': _L3_gnn_in['bt1_3'], 'L3_gnn_W2_3': _L3_gnn_in['W2_3'], 'L3_gnn_b2_3': _L3_gnn_in['b2_3']}

def reference(x, src, dst, L0_gnn_W1_l, L0_gnn_b1, L0_gnn_W1_r, L0_gnn_W2_l, L0_gnn_b2, L0_gnn_W2_r, L1_gnn_W_l, L1_gnn_b_l, L1_gnn_W_r, L1_gnn_gamma, L1_gnn_beta, L2_gnn_W1, L2_gnn_att_src1, L2_gnn_att_dst1, L2_gnn_bias1, L2_gnn_W2, L2_gnn_att_src2, L2_gnn_att_dst2, L2_gnn_bias2, L3_gnn_W1_1, L3_gnn_b1_1, L3_gnn_g1_1, L3_gnn_bt1_1, L3_gnn_W2_1, L3_gnn_b2_1, L3_gnn_g2_1, L3_gnn_bt2_1, L3_gnn_W1_2, L3_gnn_b1_2, L3_gnn_g1_2, L3_gnn_bt1_2, L3_gnn_W2_2, L3_gnn_b2_2, L3_gnn_g2_2, L3_gnn_bt2_2, L3_gnn_W1_3, L3_gnn_b1_3, L3_gnn_g1_3, L3_gnn_bt1_3, L3_gnn_W2_3, L3_gnn_b2_3):
    import jax
    import jax.numpy as jnp

    def _L0_gnn_ref(x, edge_index, W1_l, b1, W1_r, W2_l, b2, W2_r):
        import jax, jax.numpy as jnp
        import numpy as np
        N_NODES = 50000
        N_EDGES = 25000
        D = 128

        def _sage_conv(x, src, dst, W_l, b_l, W_r, n_nodes):
            msgs = x[src]
            summed = jax.ops.segment_sum(msgs, dst, num_segments=n_nodes)
            deg = jax.ops.segment_sum(jnp.ones((src.shape[0],), x.dtype), dst, num_segments=n_nodes)
            mean = summed / jnp.maximum(deg, 1.0)[:, None]
            return mean @ W_l + b_l + x @ W_r
        src, dst = (edge_index[0], edge_index[1])
        h = jax.nn.relu(_sage_conv(x, src, dst, W1_l, b1, W1_r, x.shape[0]))
        h = jax.nn.relu(_sage_conv(h, src, dst, W2_l, b2, W2_r, x.shape[0]))
        return h

    def _L1_gnn_ref(x, edge_index, W_l, b_l, W_r, gamma, beta):
        import jax, jax.numpy as jnp
        import numpy as np
        N_NODES = 50000
        N_EDGES = 9375
        D = 128
        LN_EPS = 1e-05

        def _layer_norm(f, gamma, beta):
            mu = jnp.mean(f, axis=-1, keepdims=True)
            var = jnp.mean(jnp.square(f - mu), axis=-1, keepdims=True)
            return (f - mu) * jax.lax.rsqrt(var + LN_EPS) * gamma + beta
        n = x.shape[0]
        src, dst = (edge_index[0], edge_index[1])
        agg = jax.ops.segment_sum(x[src], dst, num_segments=n)
        cnt = jax.ops.segment_sum(jnp.ones_like(src, dtype=x.dtype), dst, num_segments=n)
        mean = agg / jnp.maximum(cnt, 1.0)[:, None]
        f = mean @ W_l + b_l + x @ W_r
        f = jax.nn.gelu(f, approximate=False)
        f = _layer_norm(f, gamma, beta)
        return f + x

    def _L2_gnn_ref(x, edge_index, W1, att_src1, att_dst1, bias1, W2, att_src2, att_dst2, bias2):
        import jax, jax.numpy as jnp
        import numpy as np
        N_NODES = 50000
        N_EDGES = 12500
        IN_DIM = 128
        HID = 32
        HEADS = 4
        OUT_DIM = 128
        NEG_SLOPE = 0.2

        def gat_conv(x, src, dst, W, a_src, a_dst, bias, concat):
            N = x.shape[0]
            H, C = a_src.shape
            h = (x @ W.T).reshape(N, H, C)
            alpha_src = jnp.einsum('nhc,hc->nh', h, a_src)
            alpha_dst = jnp.einsum('nhc,hc->nh', h, a_dst)
            e = jax.nn.leaky_relu(alpha_src[src] + alpha_dst[dst], NEG_SLOPE)
            m = jax.ops.segment_max(e, dst, num_segments=N)
            m = jnp.where(jnp.isfinite(m), m, 0.0)
            p = jnp.exp(e - m[dst])
            s = jax.ops.segment_sum(p, dst, num_segments=N)
            a = p / (s[dst] + 1e-16)
            out = jax.ops.segment_sum(h[src] * a[:, :, None], dst, num_segments=N)
            if concat:
                return out.reshape(N, H * C) + bias
            return out.mean(axis=1) + bias
        N = x.shape[0]
        loop = jnp.arange(N, dtype=edge_index.dtype)
        src = jnp.concatenate([edge_index[0], loop])
        dst = jnp.concatenate([edge_index[1], loop])
        h = jax.nn.elu(gat_conv(x, src, dst, W1, att_src1, att_dst1, bias1, True))
        return gat_conv(h, src, dst, W2, att_src2, att_dst2, bias2, False)

    def _L3_gnn_ref(embed, norm, src, dst, W1_1, b1_1, g1_1, bt1_1, W2_1, b2_1, g2_1, bt2_1, W1_2, b1_2, g1_2, bt1_2, W2_2, b2_2, g2_2, bt2_2, W1_3, b1_3, g1_3, bt1_3, W2_3, b2_3):
        import jax, jax.numpy as jnp
        import numpy as np
        N, E, D, H, C = (50000, 12500, 128, 256, 128)

        def _ln(x, g, b, eps=1e-05):
            m = jnp.mean(x, axis=-1, keepdims=True)
            v = jnp.mean((x - m) ** 2, axis=-1, keepdims=True)
            return (x - m) * jax.lax.rsqrt(v + eps) * g + b

        def _sage_layer(h, W1, b1, g1, bt1, W2, b2, g2, bt2):
            h = jax.nn.relu(_ln(h @ W1 + b1, g1, bt1))
            h = h @ W2 + b2
            if g2 is not None:
                h = jax.nn.relu(_ln(h, g2, bt2))
            return h
        n = embed.shape[0]
        params = [(W1_1, b1_1, g1_1, bt1_1, W2_1, b2_1, g2_1, bt2_1), (W1_2, b1_2, g1_2, bt1_2, W2_2, b2_2, g2_2, bt2_2), (W1_3, b1_3, g1_3, bt1_3, W2_3, b2_3, None, None)]
        h = embed
        for p in params:
            agg = jax.ops.segment_sum(h[src], dst, num_segments=n)
            hc = jnp.concatenate([(agg - h) * norm, h], axis=1)
            h = _sage_layer(hc, *p)
        return h
    edge_index = jnp.stack([src, dst])
    deg = jnp.maximum(jax.ops.segment_sum(jnp.ones(dst.shape, jnp.float32), dst, num_segments=50000), 1.0)
    deg_isqrt = deg ** (-0.5)
    h = jnp.maximum(_layernorm(x, axis=-1), 0.0)
    x = x + _L0_gnn_ref(h, edge_index, L0_gnn_W1_l, L0_gnn_b1, L0_gnn_W1_r, L0_gnn_W2_l, L0_gnn_b2, L0_gnn_W2_r)
    h = jnp.maximum(_layernorm(x, axis=-1), 0.0)
    x = x + _L1_gnn_ref(h, edge_index, L1_gnn_W_l, L1_gnn_b_l, L1_gnn_W_r, L1_gnn_gamma, L1_gnn_beta)
    h = jnp.maximum(_layernorm(x, axis=-1), 0.0)
    x = x + _L2_gnn_ref(h, edge_index, L2_gnn_W1, L2_gnn_att_src1, L2_gnn_att_dst1, L2_gnn_bias1, L2_gnn_W2, L2_gnn_att_src2, L2_gnn_att_dst2, L2_gnn_bias2)
    h = jnp.maximum(_layernorm(x, axis=-1), 0.0)
    x = x + _L3_gnn_ref(h, deg_isqrt[:, None], src, dst, L3_gnn_W1_1, L3_gnn_b1_1, L3_gnn_g1_1, L3_gnn_bt1_1, L3_gnn_W2_1, L3_gnn_b2_1, L3_gnn_g2_1, L3_gnn_bt2_1, L3_gnn_W1_2, L3_gnn_b1_2, L3_gnn_g1_2, L3_gnn_bt1_2, L3_gnn_W2_2, L3_gnn_b2_2, L3_gnn_g2_2, L3_gnn_bt2_2, L3_gnn_W1_3, L3_gnn_b1_3, L3_gnn_g1_3, L3_gnn_bt1_3, L3_gnn_W2_3, L3_gnn_b2_3)
    return x

_drawn_inputs = setup_inputs


def setup_inputs(seed=0):
    import zlib

    import numpy as np

    out = dict(_drawn_inputs(seed))
    spreads = {'L0_gnn_b1': (0.0, 0.1),
     'L0_gnn_b2': (0.0, 0.1),
     'L1_gnn_b_l': (0.0, 0.1),
     'L1_gnn_gamma': (1.0, 0.2),
     'L1_gnn_beta': (0.0, 0.1),
     'L2_gnn_bias1': (0.0, 0.1),
     'L2_gnn_bias2': (0.0, 0.1),
     'L3_gnn_b1_1': (0.0, 0.1),
     'L3_gnn_g1_1': (1.0, 0.2),
     'L3_gnn_bt1_1': (0.0, 0.322),
     'L3_gnn_b2_1': (0.0, 0.1),
     'L3_gnn_g2_1': (1.0, 0.2),
     'L3_gnn_bt2_1': (0.0, 0.291),
     'L3_gnn_b1_2': (0.0, 0.1),
     'L3_gnn_g1_2': (1.0, 0.2),
     'L3_gnn_bt1_2': (0.0, 0.305),
     'L3_gnn_b2_2': (0.0, 0.1),
     'L3_gnn_g2_2': (1.0, 0.2),
     'L3_gnn_bt2_2': (0.0, 0.315),
     'L3_gnn_b1_3': (0.0, 0.1),
     'L3_gnn_g1_3': (1.0, 0.2),
     'L3_gnn_bt1_3': (0.0, 0.273),
     'L3_gnn_b2_3': (0.0, 0.1)}
    factors = {'L2_gnn_att_src1': 4.565,
     'L2_gnn_att_dst1': 8.0,
     'L2_gnn_att_src2': 6.469,
     'L2_gnn_att_dst2': 8.0}
    for name, (base, spread) in spreads.items():
        noise = np.random.default_rng([zlib.crc32(name.encode()), seed]).standard_normal(out[name].shape)
        drawn = base * np.exp(spread * noise) if base else spread * noise
        out[name] = jnp.asarray(drawn.astype(out[name].dtype))
    for name, factor in factors.items():
        out[name] = (out[name] * factor).astype(out[name].dtype)
    return out
```

```python
from contextlib import ExitStack

import numpy as np
import concourse.bass as bass
from concourse import mybir

F32 = mybir.dt.float32
BF16 = mybir.dt.bfloat16
I32 = mybir.dt.int32
ALU = mybir.AluOpType
ACT = mybir.ActivationFunctionType
AX = mybir.AxisListType

P = 128
D = 128
H2 = 256
N = 50000
E = 12500
HEADS = 4
HC = D // HEADS
COLS = -(-E // P)
JOINT = COLS
TILES = 104
J = 2
NS = 4
ROWS = P * J
PASS = ROWS * NS
PASSES = -(-N // PASS)
SHIFT = PASSES * PASS - N
SLOT_PASSES = COLS // (J * NS)
TAIL = (0, 1)
GROUPS = 52
NOWHERE = 60000
FAR = 1e30
EPS = 1e-5
GAT1W = D + 2 * HEADS
GAT2W = D + 2


class Ledger:

    def __init__(self, plan):
        self.old, self.new = plan, {"event": {}, "total": {}}
        self.replay, self.i, self.now = False, 0, None
        self.parts = [("setup", 1), ("dense", PASSES)]
        for r in range(8):
            if r in (3, 4):
                self.parts += [(f"alphas{r}", TILES // (J * NS)), (f"weights{r}", 1)]
            self.parts += [(f"round{r} first", 1), (f"round{r}", SLOT_PASSES), (f"round{r} tail", 1)]

    def part(self, name, passes):
        assert (name, passes) in self.parts
        self.now = name

    def _totals(self, signal):
        base = 0
        for name, passes in self.parts:
            if name == self.now:
                break
            base += passes * self.old["total"].get((name, signal), 0)
        return base, self.old["total"].get((self.now, signal), 0)

    def fired(self, signal, key):
        if self.replay:
            return
        k = (self.now, signal)
        n = self.new["total"].get(k, 0) + 1
        self.new["total"][k] = n
        self.new["event"][(self.now, signal, key)] = n

    def value(self, signal, key, i, back=0):
        if not self.old["total"]:
            return 1
        base, per = self._totals(signal)
        n = self.old["event"][(self.now, signal, key)]
        return base + n - back * per + (i * per if not isinstance(i, int) or i else 0)


class Signal:

    def __init__(self, name, sem, ledger, inc=1):
        self.name, self.sem, self.ledger, self.inc = name, sem, ledger, inc

    def counts(self, key):
        self.ledger.fired(self.name, key)
        return self.inc

    def at(self, key, i=0, back=0):
        return self.ledger.value(self.name, key, i, back) * self.inc


def build(nc, d, out, plan):
    led = Ledger(plan)
    ctx = ExitStack()

    def sb(name, shape, dt=F32):
        return ctx.enter_context(nc.sbuf_tensor(name, shape, dt))

    def sig(name, inc=1):
        return Signal(name, ctx.enter_context(nc.semaphore(name)), led, inc)

    def table(name, shape):
        return nc.dram_tensor(name, shape, F32).ap()

    with ctx:
        T = [table("t_h0", (N, D)), table("t_h1", (N, D)), table("t_h2", (N, D)),
             table("t_gat1", (N, GAT1W)), table("t_gat2", (N, GAT2W)), table("t_h5", (N, D)),
             table("t_z6", (N, H2)), table("t_z7", (N, H2)), out]
        WIDTH = [D, D, D, GAT1W, GAT2W, D, H2, H2, D]
        own = table("own", (GROUPS * P, J * H2))
        resid = table("resid", (GROUPS * P, J * D))

        w128 = {n: sb(n, [P, 1, D]) for n in ("w0l1", "w0r1", "w0l2", "w0r2", "w1l", "w1r")}
        wgat1, wgat2 = sb("wgat1", [P, 1, GAT1W]), sb("wgat2", [P, 1, GAT2W])
        w11, w21 = sb("w11", [P, 2, H2]), sb("w21", [P, 2, H2])
        w12, w22 = sb("w12", [P, 4, H2]), sb("w22", [P, 2, H2])
        w13, w23 = sb("w13", [P, 4, H2]), sb("w23", [P, 2, D])
        c11, c12, c13 = sb("c11", [P, 1, H2]), sb("c12", [P, 2, H2]), sb("c13", [P, 2, H2])
        BIASES = [("L0_gnn_b1", D), ("L0_gnn_b2", D), ("L1_gnn_b_l", D), ("L3_gnn_b1_1", H2),
                  ("L3_gnn_b2_1", H2), ("L3_gnn_b1_2", H2), ("L3_gnn_b2_2", H2),
                  ("L3_gnn_b1_3", H2), ("L3_gnn_b2_3", D)]
        at, BIAS_AT = 0, {}
        for name, w in BIASES:
            BIAS_AT[name] = (at, w)
            at += w
        NB = at
        brow = sb("brow", [P, NB], BF16)
        ones = sb("ones", [P, P], BF16)
        bgat1 = sb("bgat1", [P, 1])
        AFF = ["L3_gnn_g1_1", "L3_gnn_bt1_1", "L3_gnn_g2_1", "L3_gnn_bt2_1", "L3_gnn_g1_2",
               "L3_gnn_bt1_2", "L3_gnn_g2_2", "L3_gnn_bt2_2", "L3_gnn_g1_3", "L3_gnn_bt1_3"]
        aff = sb("aff", [P, len(AFF), 2])
        wide = {n: sb("wide_" + n, [P, D]) for n in ("L1_gnn_gamma", "L1_gnn_beta", "L2_gnn_bias2")}
        wide2 = {n: sb("wide_" + n, [P, H2]) for n in
                 ("L3_gnn_g2_1", "L3_gnn_bt2_1", "L3_gnn_g2_2", "L3_gnn_bt2_2")}
        ident = sb("ident", [P, P])
        after = sb("after", [P, P])
        eps = sb("eps", [P, 1])

        src_i, self_i, put_i = sb("src_i", [P, TILES], I32), sb("self_i", [P, TILES], I32), sb("put_i", [P, TILES], I32)
        dst_i = sb("dst_i", [P, 3, COLS], I32)
        dst_f = sb("dst_f", [P, 3, COLS])
        goes_on = sb("goes_on", [P, COLS])
        sel = sb("sel", [P, COLS])
        count = sb("count", [P, TILES])
        rcount, norm = sb("rcount", [P, TILES]), sb("norm", [P, TILES])
        chain = sb("chain", [P, P])
        chain_t = sb("chain_t", [P, P])

        xin = [sb(f"xin{s}", [P, J, D]) for s in range(NS)]
        X = [sb(f"x{s}", [P, J, D]) for s in range(NS)]
        fin = [sb(f"fin{s}", [P, J, D]) for s in range(NS)]
        tmp = [sb(f"tmp{s}", [P, J, D]) for s in range(NS)]
        Pb = [sb(f"pb{s}", [P, J, D]) for s in range(NS)]
        Z = [[sb(f"z{s}_{q}", [P, J, 2 * H2 if q == 0 else H2]) for q in (0, 1)] for s in range(NS)]
        row = [[sb(f"row{s}_{q}", [P, J, (GAT1W, GAT2W)[q]]) for q in (0, 1)] for s in range(NS)]
        hT = [sb(f"hT{s}", [P, 4, ROWS]) for s in range(NS)]
        eb = [sb(f"eb{s}", [P, ROWS]) for s in range(NS)]
        st = [sb(f"st{s}", [P, J, 6]) for s in range(NS)]
        mv = [sb(f"mv{s}", [P, J, 2]) for s in range(NS)]
        lnv = [sb(f"lnv{s}", [P, J]) for s in range(NS)]
        rstd = [sb(f"rstd{s}", [P, J]) for s in range(NS)]
        nmean = [sb(f"nmean{s}", [P, J]) for s in range(NS)]
        msg = [sb(f"msg{s}", [P, J, H2]) for s in range(NS)]
        acc = [sb(f"acc{s}", [P, J, H2]) for s in range(NS)]
        joint = sb("joint", [P, H2])
        bias_f, bias_h = sb("bias_f", [P, NB]), sb("bias_h", [P, NB], BF16)
        att = sb("att", [P, 2 * HEADS + 2])
        same = [sb("same0", [P, COLS]), sb("same1", [P, COLS])]
        cnt = [sb("cnt0", [P, COLS]), sb("cnt1", [P, COLS])]
        col = sb("col", [P, 4])
        alpha = [sb("alpha_src", [P, TILES, 2 * HEADS]), sb("alpha_dst", [P, TILES, 2 * HEADS])]
        weight = [sb("weight_src", [P, TILES, HEADS]), sb("weight_own", [P, TILES, HEADS])]
        top = [sb("top_fwd", [P, COLS, HEADS]), sb("top_bwd", [P, COLS, HEADS]), sb("top_new", [P, COLS, HEADS])]
        edge_top = sb("edge_top", [P, 2, HEADS])
        abuf = [sb(f"abuf{s}", [P, 2, J, 2 * HEADS]) for s in range(NS)]
        den = [sb(f"den{s}", [P, J, HEADS]) for s in range(NS)]
        alpha_i = [[sb(f"alpha_i{k}{q}", [P, TILES], I32) for q in (0, 1)] for k in (0, 1)]
        idx = [sb(f"idx{s}", [P, 3, J], I32) for s in range(NS)]
        O = [ctx.enter_context(nc.psum_tensor(f"o{s}", [P, J, H2], F32)) for s in range(NS)]
        PT = [ctx.enter_context(nc.psum_tensor(f"pt{s}", [P, 2, ROWS], F32)) for s in range(NS)]
        print("sbuf left", nc.sbuf_bytes_remaining) if not plan["total"] else None

        weights_in = [sig(f"weights_in{k}", 16) for k in range(3)]
        x_in = [sig(f"x_in{s}", 16) for s in range(NS)]
        stored = {(k, s): sig(f"stored{k}_{s}", 16) for k in range(9) for s in range(NS)}
        saved = sig("saved")
        means = sig("means")
        logvar = sig("logvar")
        rstds = sig("rstds")
        shift = sig("shift")
        z_dve, z_act = sig("z_dve"), sig("z_act")
        turned = sig("turned")
        flat = sig("flat")
        elu_e = sig("elu_e")
        elu_d = sig("elu_d")
        prod = sig("prod")
        gelu = sig("gelu")
        rows_a = sig("rows_a")
        resid_p = sig("resid_p")
        pool_c = sig("pool_c")
        x_new = sig("x_new")
        done = sig("done")
        vec = sig("vec")
        act_c = sig("act_c")
        pe_c = sig("pe_c")
        gate = sig("gate")
        passed = sig("passed")

        def carry(eng):
            if not isinstance(led.i, int):
                eng.sem_inc(passed.sem, 1)

        scattered = sig("scattered")
        msg_used = sig("msg_used")
        x_got = [sig(f"x_got{s}", 16) for s in range(NS)]
        msg_in = [sig(f"msg_in{s}", 16) for s in range(NS)]
        own_in = [sig(f"own_in{s}", 16) for s in range(NS)]
        scatter_out = [sig(f"scatter_out{s}", 16) for s in range(NS)]
        own_out = [sig(f"own_out{s}", 16) for s in range(NS)]
        resid_out = [sig(f"resid_out{s}", 16) for s in range(NS)]
        alpha_in = [sig(f"alpha_in{s}", 16) for s in range(NS)]
        alpha_at = sig("alpha_at")
        tops = sig("tops")


        def part_end(eng, k):
            eng.drain().then_inc(gate.sem, 1)
            eng.wait_ge(gate.sem, 5 * k)

        def dve_stats(v, s, key, view):
            for j in range(J):
                ins = v.bn_stats(st[s][:, j, :], view(j))
            ins.then_inc(vec.sem, vec.counts(("bn", s, key)))
            v.wait_ge(vec.sem, vec.at(("bn", s, key), led.i))
            if not isinstance(led.i, int):
                carry(v)
            for j in range(J):
                ins = v.bn_aggr(mv[s][:, j, :], st[s][:, j, :])
            ins.then_inc(means.sem, means.counts((s, key)))

        def act_rstd(a, s, key):
            a.wait_ge(means.sem, means.at((s, key), led.i))
            a.activation(lnv[s][:, :], mv[s][:, :, 1], ACT.Ln, bias=eps[:, 0:1]).then_inc(logvar.sem, logvar.counts((s, key)))
            a.wait_ge(logvar.sem, logvar.at((s, key), led.i))
            a.activation(rstd[s][:, :], lnv[s][:, :], ACT.Exp, scale=-0.5).then_inc(rstds.sem, rstds.counts((s, key)))

        def dve_norm(v, s, key, view, dst):
            v.wait_ge(rstds.sem, rstds.at((s, key), led.i))
            for j in range(J):
                ins = v.tensor_scalar(dst(j), view(j), mv[s][:, j, 0:1], rstd[s][:, j:j + 1],
                                      ALU.subtract, ALU.mult)
            return ins

        def dve_shift(v, s, key):
            v.wait_ge(rstds.sem, rstds.at((s, key), led.i))
            v.wait_ge(means.sem, means.at((s, key), led.i))
            v.scalar_tensor_tensor(out=nmean[s][:, :], in0=mv[s][:, :, 0], scalar=-1.0,
                                              in1=rstd[s][:, :], op0=ALU.mult, op1=ALU.mult).then_inc(shift.sem, shift.counts((s, key)))

        def act_norm_relu(a, s, key, view, dst):
            a.wait_ge(shift.sem, shift.at((s, key), led.i))
            for j in range(J):
                ins = a.activation(dst(j), view(j), ACT.Relu, bias=nmean[s][:, j:j + 1],
                                   scale=rstd[s][:, j:j + 1])
            ins.then_inc(z_act.sem, z_act.counts((s, key)))

        def zview(s, q, lo, hi):
            return lambda j: Z[s][q][:, j, lo:hi]

        def layer_pe(t, s, key, ready, chunks, weights, bias, width):
            t.wait_ge(ready.sem, ready.at((s, key), led.i))
            for h in range(0, len(chunks), 2):
                if h:
                    t.wait_ge(flat.sem, flat.at((s, key, h - 2), led.i))
                for c in range(h, min(h + 2, len(chunks))):
                    for j in range(J):
                        ins = t.transpose(PT[s][:, c - h, j * P:(j + 1) * P], chunks[c](j), ident[:, :])
                ins.then_inc(turned.sem, turned.counts((s, key, h)))

        def layer_mm(t, s, key, weights, bias, width, elu=False, order=None):
            h = (len(weights) - 1) // 2 * 2
            ready = elu_d if elu else flat
            t.wait_ge(ready.sem, ready.at((s, key, h), led.i))
            for j in range(J):
                o = O[s][:, j, 0:width]
                if bias:
                    lo, w = BIAS_AT[bias]
                    t.matmul(o, ones[:, :], brow[:, lo:lo + w], start=True, stop=False)
                for c, w in enumerate(weights):
                    ins = t.matmul(o, hT[s][:, c, j * P:(j + 1) * P], w[:, 0:width],
                                   start=(c == 0 and not bias), stop=(c == len(weights) - 1))
            ins.then_inc(prod.sem, prod.counts((s, key)))

        def act_flat(a, s, key, n, affine=None, elu=False):
            for h in range(0, n, 2):
                a.wait_ge(turned.sem, turned.at((s, key, h), led.i))
                if elu:
                    a.activation(eb[s][:, :], PT[s][:, 0, :], ACT.Exp, bias=bgat1[:, 0:1])
                    a.activation(hT[s][:, 0, :], PT[s][:, 0, :], ACT.Relu,
                                            bias=bgat1[:, 0:1]).then_inc(elu_e.sem, elu_e.counts((s, key, h)))
                elif affine is not None:
                    for c in range(h, min(h + 2, n)):
                        ins = a.activation(hT[s][:, c, :], PT[s][:, c - h, :], ACT.Relu,
                                           bias=aff[:, affine + 1, c:c + 1], scale=aff[:, affine, c:c + 1])
                    ins.then_inc(flat.sem, flat.counts((s, key, h)))
                else:
                    k = min(2, n - h)
                    a.activation(hT[s][:, h:h + k, :], PT[s][:, 0:k, :], ACT.Copy).then_inc(flat.sem, flat.counts((s, key, h)))

        def dve_elu(v, s, key):
            v.wait_ge(elu_e.sem, elu_e.at((s, key, 0), led.i))
            v.tensor_scalar(eb[s][:, :], eb[s][:, :], 1.0, -1.0, ALU.min, ALU.add).then_inc(vec.sem, vec.counts(("elu", s, key)))
            v.wait_ge(vec.sem, vec.at(("elu", s, key), led.i))
            v.tensor_tensor(hT[s][:, 0, :], hT[s][:, 0, :], eb[s][:, :], ALU.add).then_inc(elu_d.sem, elu_d.counts((s, key, 0)))

        W = lambda t: [t[:, c, :] for c in range(t.shape[1])]
        DENSE = [
            (0, W(w128["w0r1"]), "L0_gnn_b1", D, None), (1, W(w128["w0r2"]), "L0_gnn_b2", D, None),
            (2, W(w128["w1r"]), "L1_gnn_b_l", D, None), (3, W(wgat1), None, GAT1W, None),
            (4, W(wgat2), None, GAT2W, "elu"), (5, W(c11), "L3_gnn_b1_1", H2, None),
            (6, W(w21), "L3_gnn_b2_1", H2, 0), (7, W(c12), "L3_gnn_b1_2", H2, 2),
            (8, W(w22), "L3_gnn_b2_2", H2, 4), (9, W(c13), "L3_gnn_b1_3", H2, 6),
            (10, W(w23), "L3_gnn_b2_3", D, 8),
        ]
        MADE = {0: (z_act, 0), 1: (z_act, 1), 2: (z_act, 0), 3: (z_act, 1), 4: (rows_a, None),
                5: (z_act, 1), 6: (z_dve, 0), 7: (z_dve, 1), 8: (z_dve, 0), 9: (z_dve, 1), 10: (z_dve, 0)}
        KEPT = {0: 0, 1: 1, 2: 2, 4: 3, 7: 6, 9: 7}

        def chunk_rows(L, s):
            q = MADE[L][1]
            n = len(DENSE[L][1])
            if L == 4:
                return [lambda j: row[s][0][:, j, 0:D]]
            return [(lambda j, c=c: Z[s][q][:, j, c * D:(c + 1) * D]) for c in range(n)]

        def node0(i, s):
            if isinstance(i, int):
                return i * PASS + s * ROWS - (SHIFT if s == NS - 1 and i == PASSES - 1 else 0)
            at = i * PASS + s * ROWS
            if s == NS - 1:
                at = at - (i // (PASSES - 1)) * SHIFT
                at = nc.s_assert_within(at, 0, N - ROWS, skip_runtime_bounds_check_because="loop bounds")
            return at

        def rows_of(t, i, s):
            return t[bass.ds(node0(i, s), ROWS), :].rearrange("(p j) f -> p j f", j=J)

        def pool_res3(g, s, h, x, own=None):
            if own:
                wait_own(g, *own, s)
                wait_xin(g, *own, s)
                g.wait_ge(gelu.sem, gelu.at(s, led.i))
                carry(g)
            else:
                g.wait_ge(z_act.sem, z_act.at((s, 2), led.i))
                carry(g)
                g.wait_ge(x_new.sem, x_new.at((s, 2), led.i))
                carry(g)
            g.tensor_tensor(Pb[s][:, :, :], x[:, :, :], h, ALU.add).then_inc(resid_p.sem, resid_p.counts((s, "part")))
            g.wait_ge(resid_p.sem, resid_p.at((s, "part"), led.i))
            carry(g)
            g.tensor_tensor(Pb[s][:, :, :], Pb[s][:, :, :], bcast(wide["L1_gnn_beta"][:, :]),
                                         ALU.add).then_inc(resid_p.sem, resid_p.counts((s, 3)))

        def pool_res5(g, s):
            g.wait_ge(x_new.sem, x_new.at((s, 3), led.i))
            carry(g)
            g.tensor_tensor(Pb[s][:, :, :], X[s][:, :, :], bcast(wide["L2_gnn_bias2"][:, :]),
                                         ALU.add).then_inc(resid_p.sem, resid_p.counts((s, 5)))

        def dve_res2(v, s):
            v.wait_ge(prod.sem, prod.at((s, 1), led.i))
            v.scalar_tensor_tensor(out=X[s][:, :, :], in0=O[s][:, :, 0:D], scalar=0.0,
                                              in1=xin[s][:, :, :], op0=ALU.max, op1=ALU.add).then_inc(x_new.sem, x_new.counts((s, 2)))
            v.wait_ge(x_new.sem, x_new.at((s, 2), led.i))
            dve_stats(v, s, 2, lambda j: X[s][:, j, :])

        def dve_mid(v, s):
            v.wait_ge(gelu.sem, gelu.at(s, led.i))
            dve_stats(v, s, "mid", lambda j: tmp[s][:, j, :])

        def dve_res3(v, s):
            dve_norm(v, s, "mid", lambda j: tmp[s][:, j, :], lambda j: tmp[s][:, j, :]).then_inc(vec.sem, vec.counts(("mid", s)))
            v.wait_ge(vec.sem, vec.at(("mid", s), led.i))
            v.tensor_tensor(tmp[s][:, :, :], tmp[s][:, :, :], bcast(wide["L1_gnn_gamma"][:, :]),
                                    ALU.mult).then_inc(vec.sem, vec.counts(("gamma", s)))
            v.wait_ge(vec.sem, vec.at(("gamma", s), led.i))
            v.wait_ge(resid_p.sem, resid_p.at((s, 3), led.i))
            v.tensor_tensor(X[s][:, :, :], tmp[s][:, :, :], Pb[s][:, :, :], ALU.add).then_inc(x_new.sem, x_new.counts((s, 3)))
            v.wait_ge(x_new.sem, x_new.at((s, 3), led.i))
            dve_stats(v, s, 3, lambda j: X[s][:, j, :])

        def dve_res5(v, s, gat):
            v.wait_ge(resid_p.sem, resid_p.at((s, 5), led.i))
            v.tensor_tensor(X[s][:, :, :], gat, Pb[s][:, :, :], ALU.add).then_inc(x_new.sem, x_new.counts((s, 5)))
            v.wait_ge(x_new.sem, x_new.at((s, 5), led.i))
            dve_stats(v, s, 5, lambda j: X[s][:, j, :])

        def own_w(r):
            return H2 if r >= 6 else D

        def z0_chunks(s, n):
            return [(lambda j, c=c: Z[s][0][:, j, c * D:(c + 1) * D]) for c in range(n)]

        def z1_chunks(s, n):
            return [(lambda j, c=c: Z[s][1][:, j, c * D:(c + 1) * D]) for c in range(n)]

        w = w128
        LAYERS = {
            0: [("a", z0_chunks, [w["w0l1"][:, 0, :], w["w0r1"][:, 0, :]], "L0_gnn_b1", D, None)],
            1: [("a", z0_chunks, [w["w0l2"][:, 0, :], w["w0r2"][:, 0, :]], "L0_gnn_b2", D, None)],
            2: [("a", z0_chunks, [w["w1l"][:, 0, :], w["w1r"][:, 0, :]], "L1_gnn_b_l", D, None),
                ("b", z1_chunks, W(wgat1), None, GAT1W, None)],
            3: [("a", z0_chunks, W(wgat2), None, GAT2W, "elu")],
            4: [],
            5: [("a", z0_chunks, W(w11), "L3_gnn_b1_1", H2, None), ("b", z1_chunks, W(w21), "L3_gnn_b2_1", H2, 0)],
            6: [("a", z0_chunks, W(w12), "L3_gnn_b1_2", H2, None), ("b", z1_chunks, W(w22), "L3_gnn_b2_2", H2, 4)],
            7: [("a", z0_chunks, W(w13), "L3_gnn_b1_3", H2, None), ("b", z1_chunks, W(w23), "L3_gnn_b2_3", D, 8)],
        }
        MSGW = [D, D, D, GAT1W, GAT2W, D, H2, H2]
        SUMW = [D, D, D, D + HEADS, D + 1, D, H2, H2]
        HN = {3: HEADS, 4: 1}
        SENT = {0: (z_act, "out", lambda s: Z[s][1], D), 1: (z_act, "out", lambda s: Z[s][1], D),
                2: (rows_a, "out", lambda s: row[s][0], GAT1W), 3: (rows_a, "out", lambda s: row[s][1], GAT2W),
                4: (z_act, "out", lambda s: Z[s][1], D), 5: (z_dve, "out", lambda s: Z[s][1], H2),
                6: (z_dve, "out", lambda s: Z[s][1], H2), 7: (done, "out", lambda s: fin[s], D)}
        OWN_SAVED = {0: D, 1: D, 2: D, 3: D, 4: D, 5: H2, 6: H2}
        RESID_READ, RESID_SAVED = (1, 2, 4, 7), (0, 1, 2, 4)

        def streams(i):
            return TAIL if isinstance(i, int) and i == SLOT_PASSES else range(NS)

        def tile0(i, s):
            return i * (J * NS) + s * J

        def in_round(r, eng, body):
            led.part(f"round{r}", SLOT_PASSES)
            with eng.Fori(0, SLOT_PASSES) as i:
                led.i = i
                body(i)
            led.part(f"round{r} tail", 1)
            led.i = 0
            body(SLOT_PASSES)

        def in_round_ahead(r, eng, first, body):
            led.part(f"round{r}", SLOT_PASSES)
            first()
            with eng.Fori(0, SLOT_PASSES - 1) as i:
                led.i = i
                body(i, range(NS))
            led.replay = True
            led.i = SLOT_PASSES - 1
            body(SLOT_PASSES - 1, TAIL)
            led.replay = False
            led.part(f"round{r} tail", 1)
            led.i = 0
            body(SLOT_PASSES, ())

        def fetched(eng, signal, s, before, r, i, per=1):
            n = before * (SLOT_PASSES + (s in TAIL))
            eng.wait_ge(signal.sem, (n + 1 + i) * per * 16)
            if eng is nc.sync or eng is nc.gpsimd:
                carry(eng)

        def group_rows(t, i, s, width):
            g0 = i * (NS * P) + s * P
            return t[bass.ds(g0, P), 0:J * width].rearrange("p (j f) -> p j f", j=J)

        msgs_before = lambda r: r
        owns_before = lambda r: r - 1
        resids_before = lambda r: sum(q < r for q in RESID_READ)
        XIN0 = PASSES

        def wait_msg(eng, r, i, s):
            fetched(eng, msg_in[s], s, msgs_before(r), r, i, J)

        def wait_own(eng, r, i, s):
            fetched(eng, own_in[s], s, owns_before(r), r, i)

        def wait_xin(eng, r, i, s):
            if r == 0:
                eng.wait_ge(x_got[s].sem, J * (i + 1) * 16)
            else:
                eng.wait_ge(x_in[s].sem, (XIN0 + resids_before(r) * (SLOT_PASSES + (s in TAIL)) + i + 1) * 16)
            if eng is nc.sync or eng is nc.gpsimd:
                carry(eng)

        def sp_round(sp, r):
            def load(i, s):
                if r >= 1:
                    w = own_w(r)
                    lo = D if r in (3, 4) else w
                    sp.dma_start(Z[s][0][:, :, lo:lo + w], group_rows(own, i, s, w)).then_inc(own_in[s].sem, 16)
                if r in RESID_READ:
                    sp.dma_start(xin[s][:, :, :], group_rows(resid, i, s, D)).then_inc(x_in[s].sem, 16)

            def free(i, s):
                if r == 3:
                    sp.wait_ge(z_dve.sem, z_dve.at((s, "a"), led.i))
                    carry(sp)
                elif r != 4 and r >= 1:
                    last = (len(LAYERS[r][0][2]) - 1) // 2 * 2
                    sp.wait_ge(turned.sem, turned.at((s, "a", last), led.i))
                    carry(sp)
                if r in (1, 4):
                    sp.wait_ge(x_new.sem, x_new.at((s, "x"), led.i))
                    carry(sp)
                if r == 2:
                    sp.wait_ge(resid_p.sem, resid_p.at((s, 3), led.i))
                    carry(sp)
                if r == 7:
                    sp.wait_ge(done.sem, done.at((s, "out"), led.i))
                    carry(sp)

            def first():
                for s in range(NS):
                    load(0, s)

            def body(i, ahead):
                here = streams(i)
                if r != 7:
                    for s in ahead:
                        free(i, s)
                        load(i + 1, s)
                for s in here:
                    if r in RESID_SAVED:
                        if r == 0:
                            wait_xin(sp, 0, i, s)
                        else:
                            sp.wait_ge(x_new.sem, x_new.at((s, 3 if r == 2 else "x"), led.i))
                            carry(sp)
                        buf = xin[s] if r == 0 else X[s]
                        sp.dma_start(group_rows(resid, i, s, D), buf[:, :, :]).then_inc(resid_out[s].sem, resid_out[s].counts(0))
                for s in here:
                    if r in OWN_SAVED:
                        sg, key, buf, _ = SENT[r]
                        sp.wait_ge(sg.sem, sg.at((s, key), led.i))
                        carry(sp)
                        sp.dma_start(group_rows(own, i, s, OWN_SAVED[r]),
                                                     buf(s)[:, :, 0:OWN_SAVED[r]]).then_inc(own_out[s].sem, own_out[s].counts(0))
                if r == 7:
                    for s in ahead:
                        free(i, s)
                        load(i + 1, s)
                for s in here:
                    if r in RESID_SAVED:
                        sp.wait_ge(resid_out[s].sem, resid_out[s].at(0, led.i))
                        carry(sp)
                    if r in OWN_SAVED:
                        sp.wait_ge(own_out[s].sem, own_out[s].at(0, led.i))
                        carry(sp)
                sp.nop().then_inc(saved.sem, saved.counts("pass"))

            in_round_ahead(r, sp, first, body)

        def pool_indices(g, s, k, source, i):
            g.tensor_copy(idx[s][:, k, :], source[:, bass.ds(tile0(i, s), J)]).then_inc(pool_c.sem, pool_c.counts((s, k)))
            g.wait_ge(pool_c.sem, pool_c.at((s, k), led.i))
            carry(g)

        def pool_gather(g, s, k, rows, buf, signal):
            for j in range(J):
                g.indirect_dma_start(buf(j), None, rows, bass.IndirectOffsetOnAxis(idx[s][:, k, j:j + 1], 0))\
                    .then_inc(signal.sem, 16)

        def pool_round(g, r):
            def fetch(i, s, c):
                for k, source in enumerate((src_i, self_i)[:2 if r == 0 else 1]):
                    g.tensor_copy(idx[s][:, k, :], source[:, bass.ds(tile0(i, s), J)]).then_inc(pool_c.sem, pool_c.counts((c, s, k)))
                    g.wait_ge(pool_c.sem, pool_c.at((c, s, k), led.i))
                    carry(g)
                if s not in streams(i):
                    return
                pool_gather(g, s, 0, T[r], lambda j: msg[s][:, j, 0:MSGW[r]], msg_in[s])
                if r == 0:
                    pool_gather(g, s, 1, d["x"], lambda j: xin[s][:, j, :], x_got[s])

            def first():
                pass

            def body(i, ahead):
                here = streams(i)
                for s in here:
                    if r == 2:
                        pool_res3(g, s, Z[s][0][:, :, D:2 * D], xin[s], own=(r, i))
                for s in range(NS) if ahead else ():
                    g.wait_ge(msg_used.sem, msg_used.at(s, led.i))
                    carry(g)
                    if r == 0:
                        g.wait_ge(z_act.sem, z_act.at((s, "a"), led.i))
                        carry(g)
                        g.wait_ge(resid_out[s].sem, resid_out[s].at(0, led.i))
                        carry(g)
                    fetch(i + 1, s, "ahead")
                for s in here:
                    sg, key, buf, width = SENT[r]
                    pool_indices(g, s, 2, put_i, i)
                    g.wait_ge(sg.sem, sg.at((s, key), led.i))
                    carry(g)
                    for j in range(J):
                        ins = g.indirect_dma_start(T[r + 1], bass.IndirectOffsetOnAxis(idx[s][:, 2, j:j + 1], 0),
                                                   buf(s)[:, j, 0:width], None,
                                                   bounds_check=N - 1, oob_is_err=False)
                        ins.then_inc(scatter_out[s].sem, scatter_out[s].counts(0))
                for s in here:
                    g.wait_ge(scatter_out[s].sem, scatter_out[s].at(0, led.i))
                    carry(g)
                g.nop().then_inc(scattered.sem, scattered.counts("pass"))

            led.part(f"round{r} first", 1)
            led.i = 0
            if r in HN:
                g.wait_ge(alpha_at.sem, led_total(alpha_at, r))
            for s in range(NS):
                fetch(0, s, "first")
            in_round_ahead(r, g, first, body)

        def column(t, i, s, j):
            return t[:, bass.ds(tile0(i, s) + j, 1)]

        def dve_sums(v, r, i, s):
            w = SUMW[r]
            if s == 1 and isinstance(i, int) and i == SLOT_PASSES:
                v.wait_ge(pe_c.sem, pe_c.at("joint"))
                v.tensor_tensor(acc[s][:, 0, 0:w], PT[s][:, 0, 0:w], joint[:, 0:w], ALU.add).then_inc(vec.sem, vec.counts(("joint", s)))
                v.wait_ge(vec.sem, vec.at(("joint", s), led.i))
                v.tensor_copy(acc[s][:, 1, 0:w], acc[s][:, 0, 0:w]).then_inc(msg_used.sem, msg_used.counts(s))
                v.wait_ge(msg_used.sem, msg_used.at(s, led.i))
                return
            for j in range(J):
                before = acc[s][:, 0, 0:w] if j else acc[(s - 1) % NS][:, 1, 0:w]
                v.scalar_tensor_tensor(out=acc[s][:, j, 0:w], in0=before, scalar=column(goes_on, i, s, j),
                                               in1=msg[s][:, j, 0:w], op0=ALU.mult, op1=ALU.add).then_inc(vec.sem, vec.counts(("acc", s, j)))
                v.wait_ge(vec.sem, vec.at(("acc", s, j), led.i))
                ins = v.scalar_tensor_tensor(out=joint[:, 0:w], in0=acc[s][:, j, 0:w], scalar=column(sel, i, s, j),
                                             in1=joint[:, 0:w], op0=ALU.mult, op1=ALU.add)
                if j == J - 1:
                    ins.then_inc(msg_used.sem, msg_used.counts(s))
                    v.wait_ge(msg_used.sem, msg_used.at(s, led.i))
                else:
                    ins.then_inc(vec.sem, vec.counts(("jacc", s, j)))
                    v.wait_ge(vec.sem, vec.at(("jacc", s, j), led.i))

        def dve_affine(v, s, what, view, g, b):
            v.tensor_tensor(view, view, bcast(wide2[g][:, :]), ALU.mult).then_inc(vec.sem, vec.counts((what, "g", s)))
            v.wait_ge(vec.sem, vec.at((what, "g", s), led.i))
            v.tensor_tensor(view, view, bcast(wide2[b][:, :]), ALU.add).then_inc(vec.sem, vec.counts((what, "b", s)))
            v.wait_ge(vec.sem, vec.at((what, "b", s), led.i))
            v.tensor_scalar(view, view, 0.0, None, ALU.max).then_inc(vec.sem, vec.counts((what, "r", s)))
            v.wait_ge(vec.sem, vec.at((what, "r", s), led.i))

        def heads(t, n):
            return t.unsqueeze(2).to_broadcast([P, n, D // n])

        def per_head(t, n):
            return t.rearrange("p (h c) -> p h c", h=n)

        def heads_at(t, i, s, j, n):
            return t[:, bass.ds(tile0(i, s) + j, 1), 0:n].rearrange("p t h -> p (t h)")

        def dve_round(v, r):
            n = HN.get(r)
            names = {6: ("L3_gnn_g2_1", "L3_gnn_bt2_1"), 7: ("L3_gnn_g2_2", "L3_gnn_bt2_2")}.get(r)

            def body(i):
                here = streams(i)
                tail = isinstance(i, int) and i == SLOT_PASSES
                for s in here:
                    wait_msg(v, r, i, s)
                    if names and not (tail and s == 1):
                        dve_affine(v, s, "msg", msg[s][:, :, :], *names)
                    if n and not (tail and s == 1):
                        for j in range(J):
                            p = heads_at(weight[0], i, s, j, n)
                            m = per_head(msg[s][:, j, 0:D], n)
                            v.tensor_tensor(m, m, heads(p, n), ALU.mult)
                            ins = v.tensor_copy(msg[s][:, j, D:D + n], p)
                        ins.then_inc(vec.sem, vec.counts(("weighted", s)))
                        v.wait_ge(vec.sem, vec.at(("weighted", s), led.i))
                    dve_sums(v, r, i, s)
                    if r == 0:
                        wait_xin(v, r, i, s)
                        dve_stats(v, s, "own", lambda j: xin[s][:, j, :])
                        dve_shift(v, s, "own")
                    if r >= 1:
                        wait_own(v, r, i, s)
                    if names:
                        dve_affine(v, s, "own", Z[s][0][:, :, H2:2 * H2], *names)
                    if r <= 2:
                        for j in range(J):
                            ins = v.tensor_scalar(Z[s][0][:, j, 0:D], acc[s][:, j, 0:D], column(rcount, i, s, j),
                                                  None, ALU.mult)
                        ins.then_inc(z_dve.sem, z_dve.counts((s, "a")))
                    elif r >= 5:
                        w = SUMW[r]
                        v.tensor_tensor(Z[s][0][:, :, 0:w], acc[s][:, :, 0:w], Z[s][0][:, :, w:2 * w],
                                                ALU.subtract).then_inc(vec.sem, vec.counts(("minus", s)))
                        v.wait_ge(vec.sem, vec.at(("minus", s), led.i))
                        for j in range(J):
                            ins = v.tensor_scalar(Z[s][0][:, j, 0:w], Z[s][0][:, j, 0:w], column(norm, i, s, j),
                                                  None, ALU.mult)
                        ins.then_inc(z_dve.sem, z_dve.counts((s, "a")))
                    else:
                        for j in range(J):
                            p = heads_at(weight[1], i, s, j, n)
                            v.tensor_tensor(per_head(tmp[s][:, j, :], n), per_head(Z[s][0][:, j, D:2 * D], n),
                                            heads(p, n), ALU.mult)
                            ins = v.scalar_tensor_tensor(out=den[s][:, j, 0:n], in0=p, scalar=1e-16,
                                                         in1=acc[s][:, j, D:D + n], op0=ALU.add, op1=ALU.add)
                        ins.then_inc(vec.sem, vec.counts(("den", s)))
                        v.wait_ge(vec.sem, vec.at(("den", s), led.i))
                        v.tensor_tensor(tmp[s][:, :, :], tmp[s][:, :, :], acc[s][:, :, 0:D], ALU.add)
                        v.reciprocal(den[s][:, :, 0:n], den[s][:, :, 0:n]).then_inc(vec.sem, vec.counts(("recip", s)))
                        v.wait_ge(vec.sem, vec.at(("recip", s), led.i))
                        for j in range(J):
                            ins = v.tensor_tensor(per_head(Z[s][0][:, j, 0:D], n), per_head(tmp[s][:, j, :], n),
                                                  heads(den[s][:, j, 0:n], n), ALU.mult)
                        ins.then_inc(z_dve.sem, z_dve.counts((s, "a")))
                if r in (1, 2, 4, 5, 6, 7):
                    v.wait_ge(scattered.sem, scattered.at("pass", led.i, back=1))
                    v.wait_ge(saved.sem, saved.at("pass", led.i, back=1))
                for s in here:
                    if r == 1:
                        v.wait_ge(prod.sem, prod.at((s, "a"), led.i))
                        wait_xin(v, r, i, s)
                        v.scalar_tensor_tensor(out=X[s][:, :, :], in0=O[s][:, :, 0:D], scalar=0.0,
                                                          in1=xin[s][:, :, :], op0=ALU.max, op1=ALU.add).then_inc(x_new.sem, x_new.counts((s, "x")))
                        v.wait_ge(x_new.sem, x_new.at((s, "x"), led.i))
                        dve_stats(v, s, "x", lambda j: X[s][:, j, :])
                        dve_shift(v, s, "x")
                    if r == 2:
                        dve_mid(v, s)
                    if r == 4:
                        wait_xin(v, r, i, s)
                        v.wait_ge(z_dve.sem, z_dve.at((s, "a"), led.i))
                        v.tensor_tensor(X[s][:, :, :], xin[s][:, :, :], Z[s][0][:, :, 0:D], ALU.add).then_inc(vec.sem, vec.counts(("x", s)))
                        v.wait_ge(vec.sem, vec.at(("x", s), led.i))
                        v.tensor_tensor(X[s][:, :, :], X[s][:, :, :], bcast(wide["L2_gnn_bias2"][:, :]),
                                                   ALU.add).then_inc(x_new.sem, x_new.counts((s, "x")))
                        v.wait_ge(x_new.sem, x_new.at((s, "x"), led.i))
                        dve_stats(v, s, "x", lambda j: X[s][:, j, :])
                        dve_shift(v, s, "x")
                    if r >= 5:
                        v.wait_ge(prod.sem, prod.at((s, "a"), led.i))
                        dve_stats(v, s, "b", lambda j: O[s][:, j, :])
                        dve_norm(v, s, "b", lambda j: O[s][:, j, :], zview(s, 1, 0, H2)).then_inc(z_dve.sem, z_dve.counts((s, "b")))
                for s in here:
                    if r == 2:
                        dve_res3(v, s)
                        dve_shift(v, s, 3)
                    if r == 3:
                        dve_elu(v, s, "a")
                    if r in (5, 6):
                        v.wait_ge(prod.sem, prod.at((s, "b"), led.i))
                        dve_stats(v, s, "out", lambda j: O[s][:, j, :])
                        dve_norm(v, s, "out", lambda j: O[s][:, j, :], zview(s, 1, 0, H2)).then_inc(z_dve.sem, z_dve.counts((s, "out")))
                    if r == 7:
                        v.wait_ge(prod.sem, prod.at((s, "b"), led.i))
                        wait_xin(v, r, i, s)
                        v.tensor_tensor(fin[s][:, :, :], xin[s][:, :, :], O[s][:, :, 0:D], ALU.add).then_inc(done.sem, done.counts((s, "out")))

            led.part(f"round{r} first", 1)
            led.i = 0
            v.memset(joint[:, :], 0.0)
            v.memset(acc[NS - 1][:, 1, :], 0.0).then_inc(vec.sem, vec.counts("zero"))
            v.wait_ge(vec.sem, vec.at("zero", led.i))
            in_round(r, v, body)

        def pe_round(t, r):
            def body(i):
                here = streams(i)
                if isinstance(i, int) and i == SLOT_PASSES:
                    t.wait_ge(vec.sem, vec.at(("acc", 0, 1), led.i))
                    t.matmul(PT[1][:, 0, 0:SUMW[r]], chain[:, :], acc[0][:, 1, 0:SUMW[r]],
                                       start=True, stop=True).then_inc(pe_c.sem, pe_c.counts("joint"))
                for key, rows, weights, bias, width, kind in LAYERS[r]:
                    made = z_dve if key == "a" or r >= 5 else z_act
                    for s in here:
                        if key == "a" and r >= 1 and r != 3:
                            wait_own(t, r, i, s)
                        if r == 0:
                            t.wait_ge(z_act.sem, z_act.at((s, "a"), led.i))
                        layer_pe(t, s, key, made, rows(s, len(weights)), weights, bias, width)
                        if len(weights) > 2:
                            layer_mm(t, s, key, weights, bias, width, elu=kind == "elu")
                        elif s:
                            layer_mm(t, s - 1, key, weights, bias, width, elu=kind == "elu")
                    if len(weights) <= 2:
                        layer_mm(t, list(here)[-1], key, weights, bias, width, elu=kind == "elu")

            in_round(r, t, body)

        def act_round(a, r):
            def body(i):
                here = streams(i)
                if r == 0:
                    for s in here:
                        act_rstd(a, s, "own")
                        a.wait_ge(shift.sem, shift.at((s, "own"), led.i))
                        for j in range(J):
                            ins = a.activation(Z[s][0][:, j, D:2 * D], xin[s][:, j, :], ACT.Relu,
                                               bias=nmean[s][:, j:j + 1], scale=rstd[s][:, j:j + 1])
                        ins.then_inc(z_act.sem, z_act.counts((s, "a")))
                for key, rows, weights, bias, width, kind in LAYERS[r]:
                    if r == 2 and key == "a":
                        for s in here:
                            act_flat(a, s, key, len(weights))
                        for s in here:
                            a.wait_ge(prod.sem, prod.at((s, "a"), led.i))
                            a.activation(tmp[s][:, :, :], O[s][:, :, 0:D], ACT.Gelu).then_inc(gelu.sem, gelu.counts(s))
                        a.preload_act_table_set("natural_log_exp_and_others")
                        for s in here:
                            act_rstd(a, s, "mid")
                        for s in here:
                            act_rstd(a, s, 3)
                            a.wait_ge(shift.sem, shift.at((s, 3), led.i))
                            for j in range(J):
                                ins = a.activation(Z[s][1][:, j, 0:D], X[s][:, j, :], ACT.Relu,
                                                   bias=nmean[s][:, j:j + 1], scale=rstd[s][:, j:j + 1])
                            ins.then_inc(z_act.sem, z_act.counts((s, "b")))
                        continue
                    for s in here:
                        if key == "b" and r >= 5:
                            act_rstd(a, s, "b")
                        act_flat(a, s, key, len(weights), affine=kind if isinstance(kind, int) else None,
                                 elu=kind == "elu")
                a.wait_ge(scattered.sem, scattered.at("pass", led.i, back=1))
                a.wait_ge(saved.sem, saved.at("pass", led.i, back=1))
                for s in here:
                    if r == 0:
                        a.wait_ge(prod.sem, prod.at((s, "a"), led.i))
                        a.activation(Z[s][1][:, :, 0:D], O[s][:, :, 0:D], ACT.Relu).then_inc(z_act.sem, z_act.counts((s, "out")))
                    if r in (1, 4):
                        act_rstd(a, s, "x")
                        a.wait_ge(shift.sem, shift.at((s, "x"), led.i))
                        for j in range(J):
                            ins = a.activation(Z[s][1][:, j, 0:D], X[s][:, j, :], ACT.Relu,
                                               bias=nmean[s][:, j:j + 1], scale=rstd[s][:, j:j + 1])
                        ins.then_inc(z_act.sem, z_act.counts((s, "out")))
                    if r == 2:
                        a.wait_ge(prod.sem, prod.at((s, "b"), led.i))
                        a.activation(row[s][0][:, :, :], O[s][:, :, 0:GAT1W], ACT.Copy).then_inc(rows_a.sem, rows_a.counts((s, "out")))
                    if r == 3:
                        a.wait_ge(prod.sem, prod.at((s, "a"), led.i))
                        a.activation(row[s][1][:, :, :], O[s][:, :, 0:GAT2W], ACT.Copy).then_inc(rows_a.sem, rows_a.counts((s, "out")))
                    if r in (5, 6):
                        act_rstd(a, s, "out")

            in_round(r, a, body)

        ALPHA_PASSES = TILES // (J * NS)

        def pool_alphas(g, r):
            k, w = r - 3, 2 * HN[r]
            rows = T[r].rearrange("n (a w) -> (n a) w", w=w)
            led.part(f"alphas{r}", ALPHA_PASSES)
            with g.Fori(0, ALPHA_PASSES) as i:
                led.i = i
                for s in range(NS):
                    g.wait_ge(alpha_at.sem, alpha_at.at(s, i, back=1))
                    carry(g)
                    for q in (0, 1):
                        pool_indices(g, s, q, alpha_i[k][q], i)
                        for j in range(J):
                            g.indirect_dma_start(abuf[s][:, q, j, 0:w], None, rows,
                                             bass.IndirectOffsetOnAxis(idx[s][:, q, j:j + 1], 0)).then_inc(alpha_in[s].sem, alpha_in[s].counts("in"))

        def act_alphas(a, r):
            w = 2 * HN[r]
            led.part(f"alphas{r}", ALPHA_PASSES)
            with a.Fori(0, ALPHA_PASSES) as i:
                led.i = i
                for s in range(NS):
                    a.wait_ge(alpha_in[s].sem, alpha_in[s].at("in", i))
                    for q in (0, 1):
                        ins = a.activation(alpha[q][:, bass.ds(tile0(i, s), J), 0:w], abuf[s][:, q, :, 0:w], ACT.Copy)
                    ins.then_inc(alpha_at.sem, alpha_at.counts(s))
            led.part(f"weights{r}", 1)
            led.i = 0
            n = HN[r]
            for q in (0, 1):
                a.wait_ge(vec.sem, vec.at(("minus max", q)))
                a.activation(weight[q][:, :, 0:n], weight[q][:, :, 0:n], ACT.Exp).then_inc(elu_e.sem, elu_e.counts(("weight", q)))

        def pe_weights(t, r):
            led.part(f"weights{r}", 1)
            led.i = 0
            for q in (0, 1):
                for h in range(HN[r]):
                    t.wait_ge(vec.sem, vec.at(("spread", q, h)))
                    ins = t.transpose(PT[q][:, h // 2, (h % 2) * P:(h % 2 + 1) * P], acc[h][:, q, 0:P], ident[:, :])
                ins.then_inc(tops.sem, tops.counts(q))

        def dve_weights(v, r):
            led.part(f"weights{r}", 1)
            led.i = 0
            n = HN[r]
            fwd, bwd, new = (t[:, :, 0:n] for t in top)
            w0, w1 = weight[0][:, :, 0:n], weight[1][:, :, 0:n]
            dst = dst_f[:, 0, :]
            over = lambda m, k: m.unsqueeze(2).to_broadcast([P, k, n])
            v.wait_ge(alpha_at.sem, led_total(alpha_at, r))
            v.tensor_tensor(w0, alpha[0][:, :, 0:n], alpha[1][:, :, n:2 * n], ALU.add)
            v.tensor_tensor(w1, alpha[1][:, :, 0:n], alpha[1][:, :, n:2 * n], ALU.add).then_inc(vec.sem, vec.counts("logits"))
            v.wait_ge(vec.sem, vec.at("logits", led.i))
            for q, w in enumerate((w0, w1)):
                ins = v.scalar_tensor_tensor(out=w, in0=w, scalar=0.2, in1=w, op0=ALU.mult, op1=ALU.max)
            ins.then_inc(vec.sem, vec.counts("leaky"))
            v.wait_ge(vec.sem, vec.at("leaky", led.i))
            v.tensor_copy(fwd, weight[0][:, 0:COLS, 0:n])
            v.tensor_copy(bwd, weight[0][:, 0:COLS, 0:n]).then_inc(vec.sem, vec.counts("start"))
            v.wait_ge(vec.sem, vec.at("start", led.i))
            step = 1
            while step < COLS:
                m = COLS - step
                v.tensor_tensor(same[0][:, 0:m], dst_f[:, 0, step:], dst_f[:, 0, 0:m], ALU.is_equal).then_inc(vec.sem, vec.counts(("eq", step)))
                v.wait_ge(vec.sem, vec.at(("eq", step), led.i))
                v.tensor_scalar(same[0][:, 0:m], same[0][:, 0:m], -1.0, FAR, ALU.add, ALU.mult).then_inc(vec.sem, vec.counts(("far", step)))
                v.wait_ge(vec.sem, vec.at(("far", step), led.i))
                v.tensor_tensor(new[:, 0:m, :], fwd[:, 0:m, :], over(same[0][:, 0:m], m), ALU.add).then_inc(vec.sem, vec.counts(("f1", step)))
                v.wait_ge(vec.sem, vec.at(("f1", step), led.i))
                v.tensor_tensor(new[:, 0:m, :], fwd[:, step:, :], new[:, 0:m, :], ALU.max).then_inc(vec.sem, vec.counts(("f2", step)))
                v.wait_ge(vec.sem, vec.at(("f2", step), led.i))
                v.tensor_copy(fwd[:, step:, :], new[:, 0:m, :]).then_inc(vec.sem, vec.counts(("f3", step)))
                v.wait_ge(vec.sem, vec.at(("f3", step), led.i))
                v.tensor_tensor(new[:, 0:m, :], bwd[:, step:, :], over(same[0][:, 0:m], m), ALU.add).then_inc(vec.sem, vec.counts(("b1", step)))
                v.wait_ge(vec.sem, vec.at(("b1", step), led.i))
                v.tensor_tensor(new[:, 0:m, :], bwd[:, 0:m, :], new[:, 0:m, :], ALU.max).then_inc(vec.sem, vec.counts(("b2", step)))
                v.wait_ge(vec.sem, vec.at(("b2", step), led.i))
                v.tensor_copy(bwd[:, 0:m, :], new[:, 0:m, :]).then_inc(vec.sem, vec.counts(("b3", step)))
                v.wait_ge(vec.sem, vec.at(("b3", step), led.i))
                step *= 2
            for q, (t, at) in enumerate(((fwd, COLS - 1), (bwd, 0))):
                for h in range(n):
                    v.tensor_scalar(acc[h][:, q, 0:P], ident[:, :], 0.0, t[:, at, h:h + 1], ALU.mult, ALU.add).then_inc(vec.sem, vec.counts(("spread", q, h)))
                    v.wait_ge(vec.sem, vec.at(("spread", q, h), led.i))
            v.tensor_tensor(fwd, fwd, bwd, ALU.max).then_inc(vec.sem, vec.counts("both"))
            v.wait_ge(vec.sem, vec.at("both", led.i))
            for q, (mask, start) in enumerate(((chain_t, dst_f[:, 0, 0:1]), (chain, dst_f[:, 0, COLS - 1:COLS]))):
                far = fin[0][:, 0, :]
                v.tensor_scalar(far, mask[:, :], -1.0, FAR, ALU.add, ALU.mult).then_inc(vec.sem, vec.counts(("mask", q)))
                v.wait_ge(vec.sem, vec.at(("mask", q), led.i))
                v.wait_ge(tops.sem, tops.at(q))
                for h in range(n):
                    v.tensor_tensor(fin[1][:, 0, :], PT[q][:, h // 2, (h % 2) * P:(h % 2 + 1) * P], far, ALU.add).then_inc(vec.sem, vec.counts(("masked", q, h)))
                    v.wait_ge(vec.sem, vec.at(("masked", q, h), led.i))
                    v.reduce_max(edge_top[:, q, h:h + 1], fin[1][:, 0, :], AX.X).then_inc(vec.sem, vec.counts(("edge", q, h)))
                    v.wait_ge(vec.sem, vec.at(("edge", q, h), led.i))
                v.tensor_scalar(same[0][:, :], dst, start, 1.0, ALU.is_equal, ALU.subtract).then_inc(vec.sem, vec.counts(("at", q)))
                v.wait_ge(vec.sem, vec.at(("at", q), led.i))
                v.tensor_scalar(same[0][:, :], same[0][:, :], FAR, None, ALU.mult).then_inc(vec.sem, vec.counts(("at far", q)))
                v.wait_ge(vec.sem, vec.at(("at far", q), led.i))
                v.tensor_tensor(new, over(same[0][:, :], COLS),
                                        edge_top[:, q, 0:n].unsqueeze(1).to_broadcast([P, COLS, n]), ALU.add).then_inc(vec.sem, vec.counts(("e1", q)))
                v.wait_ge(vec.sem, vec.at(("e1", q), led.i))
                v.tensor_tensor(fwd, fwd, new, ALU.max).then_inc(vec.sem, vec.counts(("e2", q)))
                v.wait_ge(vec.sem, vec.at(("e2", q), led.i))
            v.tensor_tensor(fwd, fwd, weight[1][:, 0:COLS, 0:n], ALU.max).then_inc(vec.sem, vec.counts("own too"))
            v.wait_ge(vec.sem, vec.at("own too", led.i))
            v.tensor_tensor(weight[1][:, COLS:TILES, 0:n], weight[1][:, COLS:TILES, 0:n],
                            fwd[:, 0:1, :].to_broadcast([P, TILES - COLS, n]), ALU.subtract)
            v.memset(weight[0][:, COLS:TILES, :], 0.0)
            v.tensor_tensor(weight[0][:, 0:COLS, 0:n], weight[0][:, 0:COLS, 0:n], fwd, ALU.subtract).then_inc(vec.sem, vec.counts(("minus max", 0)))
            v.tensor_tensor(weight[1][:, 0:COLS, 0:n], weight[1][:, 0:COLS, 0:n], fwd, ALU.subtract).then_inc(vec.sem, vec.counts(("minus max", 1)))
            v.wait_ge(elu_e.sem, elu_e.at(("weight", 1)))

        def led_total(signal, r):
            return (NS * (r - 2) * ALPHA_PASSES) + NS

        block = ctx.enter_context(nc.Block())
        from_dram = {}

        def loads():
            two = lambda n: d[n].rearrange("(c k) n -> k c n", k=P)
            one = lambda n: d[n].rearrange("(c k) n -> k c n", k=P)
            yield w128["w0l1"][:, :, :], one("L0_gnn_W1_l")
            yield w128["w0r1"][:, :, :], one("L0_gnn_W1_r")
            yield w128["w0l2"][:, :, :], one("L0_gnn_W2_l")
            yield w128["w0r2"][:, :, :], one("L0_gnn_W2_r")
            yield w128["w1l"][:, :, :], one("L1_gnn_W_l")
            yield w128["w1r"][:, :, :], one("L1_gnn_W_r")
            for t, n in ((w11, "L3_gnn_W1_1"), (w21, "L3_gnn_W2_1"), (w12, "L3_gnn_W1_2"),
                         (w22, "L3_gnn_W2_2"), (w13, "L3_gnn_W1_3"), (w23, "L3_gnn_W2_3")):
                yield t[:, :, :], two(n)
            yield Z[0][1][:, 0, 0:D], d["L2_gnn_W1"]
            yield Z[1][1][:, 0, 0:D], d["L2_gnn_W2"]
            yield bgat1[:, :], d["L2_gnn_bias1"].rearrange("(p a) -> p a", a=1)
            for k, n in enumerate(AFF):
                yield aff[:, k, :], d[n].rearrange("(c p) -> p c", p=P)
            for n in wide:
                yield wide[n][:, :], d[n].partition_broadcast(P)
            for n in wide2:
                yield wide2[n][:, :], d[n].partition_broadcast(P)
            for n, (lo, w) in BIAS_AT.items():
                for q in range(3):
                    yield bias_f[32 * q:32 * q + 1, lo:lo + w], d[n].rearrange("(a n) -> a n", a=1)

        def loads_small():
            for k, n in enumerate(("L2_gnn_att_src1", "L2_gnn_att_dst1")):
                for h in range(HEADS):
                    yield att[HC * h:HC * (h + 1), k * HEADS + h:k * HEADS + h + 1], \
                        d[n][h:h + 1, :].rearrange("a c -> c a")
            for k, n in enumerate(("L2_gnn_att_src2", "L2_gnn_att_dst2")):
                yield att[:, 2 * HEADS + k:2 * HEADS + k + 1], d[n].rearrange("a c -> c a")

        def loads_edges():
            cut = E - (P - 1) * COLS
            full = (P - 1) * COLS
            src, dst = d["src"], d["dst"]
            yield src_i[0:P - 1, 0:COLS], src[0:full].rearrange("(p t) -> p t", t=COLS)
            yield src_i[P - 1:P, 0:cut], src[full:E].rearrange("(p t) -> p t", p=1)
            yield dst_i[0:P - 1, 0, :], dst[0:full].rearrange("(p t) -> p t", t=COLS)
            yield dst_i[P - 1:P, 0, 0:cut], dst[full:E].rearrange("(p t) -> p t", p=1)
            yield dst_i[0:1, 1, 1:COLS], dst[0:COLS - 1].rearrange("(p t) -> p t", p=1)
            yield dst_i[1:P - 1, 1, :], dst[COLS - 1:full - 1].rearrange("(p t) -> p t", t=COLS)
            yield dst_i[P - 1:P, 1, 0:cut + 1], dst[full - 1:E].rearrange("(p t) -> p t", p=1)
            yield dst_i[0:P - 1, 2, :], dst[1:full + 1].rearrange("(p t) -> p t", t=COLS)
            yield dst_i[P - 1:P, 2, 0:cut - 1], dst[full + 1:E].rearrange("(p t) -> p t", p=1)

        def bcast(row_tile, j=J):
            return row_tile.unsqueeze(1).to_broadcast([P, j, row_tile.shape[1]])

        @block.sync
        def _(sp):
            led.i = 0
            led.part("setup", 1)
            sp.wait_ge(vec.sem, vec.at("cleared"))
            sp.wait_ge(pool_c.sem, pool_c.at("cleared"))
            for k, group in enumerate((loads(), loads_small(), loads_edges())):
                for dst, src in group:
                    with nc.allow_non_contiguous_dma(reason="small, once"):
                        sp.dma_start(dst, src).then_inc(weights_in[k].sem, weights_in[k].counts("last"))
                sp.wait_ge(weights_in[k].sem, weights_in[k].at("last"))
            sp.nop().then_inc(saved.sem, saved.counts("pass"))
            part_end(sp, 1)
            led.i = 0
            led.part("dense", PASSES)
            for s in range(NS):
                sp.dma_start(xin[s][:, :, :], rows_of(d["x"], 0, s)).then_inc(x_in[s].sem, 16)

            def store(i, s, k, key, ready, buf, target):
                sp.wait_ge(ready.sem, ready.at(key, i))
                carry(sp)
                if s == NS - 1:
                    sp.wait_ge(stored[k, s - 1].sem, stored[k, s - 1].at(0, i))
                    carry(sp)
                sp.dma_start(rows_of(target, i, s), buf).then_inc(stored[k, s].sem, stored[k, s].counts(0))

            def dense_sp(i, more):
                led.i = i
                for L in range(11):
                    for s in range(NS):
                        if L in KEPT:
                            sg, q = MADE[L]
                            w = WIDTH[KEPT[L]]
                            buf = row[s][0][:, :, :] if L == 4 else Z[s][q][:, :, 0:w]
                            store(i, s, KEPT[L], (s, L), sg, buf, T[KEPT[L]])
                        if L == 5:
                            store(i, s, 4, (s, "row2"), rows_a, row[s][1][:, :, :], T[4])
                            store(i, s, 5, (s, 5), z_act, Z[s][1][:, :, 0:D], T[5])
                        if L == 3 and more:
                            sp.wait_ge(x_new.sem, x_new.at((s, 2), i))
                            carry(sp)
                            sp.dma_start(xin[s][:, :, :], rows_of(d["x"], i + 1, s)).then_inc(x_in[s].sem, 16)
                for s in range(NS):
                    store(i, s, 8, (s, "out"), done, fin[s][:, :, :], out)
                for s in range(NS):
                    sp.wait_ge(stored[8, s].sem, stored[8, s].at(0, i))
                    carry(sp)
                sp.nop().then_inc(saved.sem, saved.counts("pass"))

            with sp.Fori(0, PASSES - 1) as i:
                dense_sp(i, True)
            led.replay = True
            dense_sp(PASSES - 1, False)
            led.replay = False
            part_end(sp, 2)
            for r in range(8):
                sp_round(sp, r)
                part_end(sp, 3 + r)

        @block.gpsimd
        def _(g):
            led.i = 0
            led.part("setup", 1)
            g.memset(ident[:, :], 0.0)
            g.memset(after[:, :], 1.0)
            g.memset(src_i[:, :], 0)
            g.memset(dst_i[:, :, :], N).then_inc(pool_c.sem, pool_c.counts("cleared0"))
            g.wait_ge(pool_c.sem, pool_c.at("cleared0"))
            g.affine_select(out=ident[:, :], in_=ident[:, :], compare_op=ALU.not_equal, fill=1.0,
                            base=0, pattern=[[-1, P]], channel_multiplier=1)
            g.affine_select(out=after[:, :], in_=after[:, :], compare_op=ALU.is_gt, fill=0.0,
                            base=0, pattern=[[1, P]], channel_multiplier=-1)
            g.memset(dst_i[0:1, 1, 0:1], -1).then_inc(pool_c.sem, pool_c.counts("cleared"))
            g.nop().then_inc(scattered.sem, scattered.counts("none yet"))
            part_end(g, 1)
            led.part("dense", PASSES)
            with g.Fori(0, PASSES) as i:
                led.i = i
                for s in range(NS):
                    pool_res3(g, s, Z[s][0][:, :, 0:D], X[s])
                for s in range(NS):
                    pool_res5(g, s)
            part_end(g, 2)
            for r in range(8):
                if r in HN:
                    pool_alphas(g, r)
                pool_round(g, r)
                part_end(g, 3 + r)

        @block.scalar
        def _(a):
            led.i = 0
            led.part("setup", 1)
            a.preload_act_table_set("natural_log_exp_and_others")
            a.wait_ge(vec.sem, vec.at("count"))
            a.activation(norm[:, :], count[:, :], ACT.Ln).then_inc(logvar.sem, logvar.counts("count"))
            a.wait_ge(logvar.sem, logvar.at("count"))
            a.activation(norm[:, :], norm[:, :], ACT.Exp, scale=-0.5).then_inc(rstds.sem, rstds.counts("count"))
            for s in range(NS):
                a.nop().then_inc(alpha_at.sem, alpha_at.counts(("none yet", s)))
            part_end(a, 1)
            led.part("dense", PASSES)
            with a.Fori(0, PASSES) as i:
                led.i = i
                for L in range(11):
                    for s in range(NS):
                        z0, z1 = zview(s, 0, 0, D), zview(s, 1, 0, D)
                        if L == 0:
                            act_rstd(a, s, 0)
                            act_norm_relu(a, s, 0, lambda j: xin[s][:, j, :], z0)
                        if L == 1:
                            a.wait_ge(prod.sem, prod.at((s, 0), i))
                            a.activation(Z[s][1][:, :, 0:D], O[s][:, :, 0:D], ACT.Relu).then_inc(z_act.sem, z_act.counts((s, 1)))
                        if L == 2:
                            act_rstd(a, s, 2)
                            a.wait_ge(stored[0, s].sem, stored[0, s].at(0, i))
                            act_norm_relu(a, s, 2, lambda j: X[s][:, j, :], z0)
                        if L == 3:
                            act_rstd(a, s, 3)
                            a.wait_ge(stored[1, s].sem, stored[1, s].at(0, i))
                            act_norm_relu(a, s, 3, lambda j: X[s][:, j, :], z1)
                        if L == 4:
                            a.wait_ge(prod.sem, prod.at((s, 3), i))
                            a.activation(row[s][0][:, :, :], O[s][:, :, 0:GAT1W], ACT.Copy).then_inc(rows_a.sem, rows_a.counts((s, 4)))
                        if L == 5:
                            a.wait_ge(prod.sem, prod.at((s, 4), i))
                            a.activation(row[s][1][:, :, :], O[s][:, :, 0:GAT2W], ACT.Copy).then_inc(rows_a.sem, rows_a.counts((s, "row2")))
                            act_rstd(a, s, 5)
                            act_norm_relu(a, s, 5, lambda j: X[s][:, j, :], z1)
                        if L >= 6:
                            act_rstd(a, s, L)
                        n, kind = len(DENSE[L][1]), DENSE[L][4]
                        act_flat(a, s, L, n, affine=kind if isinstance(kind, int) else None, elu=kind == "elu")
                    if L == 2:
                        for s in range(NS):
                            a.wait_ge(prod.sem, prod.at((s, 2), i))
                            a.activation(tmp[s][:, :, :], O[s][:, :, 0:D], ACT.Gelu).then_inc(gelu.sem, gelu.counts(s))
                        a.preload_act_table_set("natural_log_exp_and_others")
                        for s in range(NS):
                            act_rstd(a, s, "mid")
                for s in range(NS):
                    for k in (2, 3, 4, 5, 6, 7):
                        a.wait_ge(stored[k, s].sem, stored[k, s].at(0, i))
            part_end(a, 2)
            for r in range(8):
                if r in HN:
                    act_alphas(a, r)
                act_round(a, r)
                part_end(a, 3 + r)

        @block.vector
        def _(v):
            led.i = 0
            led.part("setup", 1)
            for tile, value in ((ones, 1.0), (brow, 0.0), (att, 0.0), (eps, EPS), (same[0], 0.0),
                                (same[1], 0.0), (joint, 0.0)):
                v.memset(tile[:, :], value)
            v.memset(put_i[:, :], NOWHERE).then_inc(vec.sem, vec.counts("cleared"))
            v.wait_ge(vec.sem, vec.at("cleared"))
            v.wait_ge(weights_in[0].sem, weights_in[0].at("last"))
            v.tensor_copy(brow[0:1, :], bias_f[0:1, :])
            for r in (32, 64):
                v.tensor_copy(bias_h[r:r + 1, :], bias_f[r:r + 1, :]).then_inc(vec.sem, vec.counts(("hi", r)))
                v.wait_ge(vec.sem, vec.at(("hi", r), led.i))
                v.tensor_tensor(bias_f[r:r + 1, :], bias_f[r:r + 1, :], bias_h[r:r + 1, :], ALU.subtract).then_inc(vec.sem, vec.counts(("rest", r)))
                v.wait_ge(vec.sem, vec.at(("rest", r), led.i))
            v.tensor_copy(bias_h[64:65, :], bias_f[64:65, :]).then_inc(vec.sem, vec.counts("mid"))
            v.wait_ge(vec.sem, vec.at("mid", led.i))
            v.tensor_tensor(bias_f[64:65, :], bias_f[64:65, :], bias_h[64:65, :], ALU.subtract).then_inc(vec.sem, vec.counts("rest2"))
            v.wait_ge(vec.sem, vec.at("rest2", led.i))
            v.tensor_copy(brow[32:33, :], bias_f[32:33, :])
            v.tensor_copy(brow[64:65, :], bias_f[64:65, :])
            v.tensor_tensor(c11[:, :, :], w11[:, 1:2, :], w11[:, 0:1, :], ALU.subtract)
            v.tensor_tensor(c12[:, :, :], w12[:, 2:4, :], w12[:, 0:2, :], ALU.subtract)
            v.tensor_tensor(c13[:, :, :], w13[:, 2:4, :], w13[:, 0:2, :], ALU.subtract)
            v.wait_ge(pe_c.sem, pe_c.at("gat"))
            v.tensor_copy(wgat1[:, 0, 0:D], PT[0][:, 0, 0:P])
            v.tensor_copy(wgat2[:, 0, 0:D], PT[1][:, 0, 0:P])
            v.tensor_copy(wgat1[:, 0, D:GAT1W], O[0][:, 0, 0:2 * HEADS])
            v.tensor_copy(wgat2[:, 0, D:GAT2W], O[1][:, 0, 0:2])
            v.wait_ge(weights_in[2].sem, weights_in[2].at("last"))
            v.tensor_copy(dst_f[:, :, :], dst_i[:, :, :]).then_inc(vec.sem, vec.counts("dst_f"))
            v.wait_ge(vec.sem, vec.at("dst_f", led.i))
            dst, first, final = dst_f[:, 0, :], dst_f[:, 0, 0:1], dst_f[:, 0, COLS - 1:COLS]
            v.tensor_tensor(goes_on[:, :], dst, dst_f[:, 1, :], ALU.is_equal).then_inc(vec.sem, vec.counts("on"))
            v.wait_ge(vec.sem, vec.at("on", led.i))
            v.tensor_copy(col[:, 0:1], goes_on[:, 0:1]).then_inc(vec.sem, vec.counts("linked"))
            v.wait_ge(vec.sem, vec.at("linked", led.i))
            v.memset(goes_on[:, 0:1], 0.0)
            v.tensor_scalar(sel[:, :], dst, first, col[:, 0:1], ALU.is_equal, ALU.mult).then_inc(vec.sem, vec.counts("first"))
            v.wait_ge(vec.sem, vec.at("first", led.i))
            v.tensor_tensor(same[0][:, :], dst, dst_f[:, 2, :], ALU.not_equal).then_inc(vec.sem, vec.counts("last"))
            v.wait_ge(vec.sem, vec.at("last", led.i))
            v.tensor_tensor(sel[:, :], sel[:, :], same[0][:, :], ALU.mult).then_inc(vec.sem, vec.counts("sel"))
            v.wait_ge(vec.sem, vec.at("sel", led.i))
            v.tensor_tensor(same[0][:, :], same[0][:, :], sel[:, :], ALU.subtract).then_inc(vec.sem, vec.counts("main"))
            v.wait_ge(vec.sem, vec.at("main", led.i))
            v.reduce_sum(col[:, 1:2], sel[:, :], AX.X).then_inc(vec.sem, vec.counts("has"))
            v.wait_ge(vec.sem, vec.at("has", led.i))
            v.tensor_scalar(cnt[0][:, :], dst, -float(NOWHERE), None, ALU.add).then_inc(vec.sem, vec.counts("off"))
            v.wait_ge(vec.sem, vec.at("off", led.i))
            v.tensor_tensor(cnt[1][:, :], cnt[0][:, :], same[0][:, :], ALU.mult).then_inc(vec.sem, vec.counts("off2"))
            v.wait_ge(vec.sem, vec.at("off2", led.i))
            v.tensor_scalar(put_i[:, 0:COLS], cnt[1][:, :], float(NOWHERE), None, ALU.add)
            v.tensor_tensor(col[:, 2:3], cnt[0][:, 0:1], col[:, 1:2], ALU.mult).then_inc(vec.sem, vec.counts("off3"))
            v.wait_ge(vec.sem, vec.at("off3", led.i))
            v.tensor_scalar(put_i[:, JOINT:JOINT + 1], col[:, 2:3], float(NOWHERE), None, ALU.add)
            v.tensor_scalar(self_i[:, 0:COLS], dst, float(N - 1), None, ALU.min)
            v.tensor_scalar(same[0][:, 0:TILES - COLS], dst_f[:, 0, 0:TILES - COLS], 0.0, first, ALU.mult, ALU.add).then_inc(vec.sem, vec.counts("fill"))
            v.wait_ge(vec.sem, vec.at("fill", led.i))
            v.tensor_scalar(self_i[:, COLS:TILES], same[0][:, 0:TILES - COLS], float(N - 1), None, ALU.min)
            v.memset(col[:, 3:4], 0.0).then_inc(vec.sem, vec.counts("self_i"))
            v.wait_ge(vec.sem, vec.at("self_i", led.i))
            for q, rows_i in enumerate((src_i, self_i)):
                for k, w in enumerate((GAT1W // (2 * HEADS), GAT2W // 2)):
                    v.tensor_scalar(alpha_i[k][q][:, :], rows_i[:, :], float(w), float(w - 1), ALU.mult, ALU.add)
            v.tensor_scalar(acc[0][:, 0, 0:P], ident[:, :], 0.0, first, ALU.mult, ALU.add).then_inc(vec.sem, vec.counts("wide first"))
            v.wait_ge(vec.sem, vec.at("wide first", led.i))
            v.wait_ge(pe_c.sem, pe_c.at("first"))
            v.scalar_tensor_tensor(out=chain[:, :], in0=PT[2][:, 0, 0:P], scalar=final, in1=after[:, :],
                                           op0=ALU.is_equal, op1=ALU.mult).then_inc(vec.sem, vec.counts("chain"))
            v.wait_ge(vec.sem, vec.at("chain", led.i))
            v.tensor_scalar(cnt[0][:, :], dst, 0.0, 1.0, ALU.mult, ALU.add).then_inc(vec.sem, vec.counts("one"))
            v.wait_ge(vec.sem, vec.at("one", led.i))
            step = 1
            while step < COLS:
                n = COLS - step
                v.tensor_tensor(same[0][:, 0:n], dst_f[:, 0, step:], dst_f[:, 0, 0:n], ALU.is_equal).then_inc(vec.sem, vec.counts(("eq", step)))
                v.wait_ge(vec.sem, vec.at(("eq", step), led.i))
                v.tensor_tensor(same[0][:, 0:n], same[0][:, 0:n], cnt[0][:, 0:n], ALU.mult).then_inc(vec.sem, vec.counts(("take", step)))
                v.wait_ge(vec.sem, vec.at(("take", step), led.i))
                v.tensor_tensor(cnt[1][:, step:], cnt[0][:, step:], same[0][:, 0:n], ALU.add).then_inc(vec.sem, vec.counts(("sum", step)))
                v.wait_ge(vec.sem, vec.at(("sum", step), led.i))
                v.tensor_copy(cnt[0][:, step:], cnt[1][:, step:]).then_inc(vec.sem, vec.counts(("back", step)))
                v.wait_ge(vec.sem, vec.at(("back", step), led.i))
                step *= 2
            v.tensor_copy(count[:, 0:COLS], cnt[0][:, :])
            v.tensor_tensor(cnt[1][:, :], cnt[0][:, :], sel[:, :], ALU.mult).then_inc(vec.sem, vec.counts("joint part"))
            v.wait_ge(vec.sem, vec.at("joint part", led.i))
            v.reduce_sum(col[:, 2:3], cnt[1][:, :], AX.X).then_inc(vec.sem, vec.counts("joint count"))
            v.wait_ge(vec.sem, vec.at("joint count", led.i))
            v.wait_ge(pe_c.sem, pe_c.at("count"))
            v.tensor_copy(chain_t[:, :], PT[3][:, 0, 0:P])
            v.tensor_tensor(col[:, 3:4], O[2][:, 0, 0:1], col[:, 2:3], ALU.add).then_inc(vec.sem, vec.counts("joint sum"))
            v.wait_ge(vec.sem, vec.at("joint sum", led.i))
            v.tensor_scalar(count[:, COLS:TILES], cnt[0][:, 0:TILES - COLS], 0.0, col[:, 3:4], ALU.mult, ALU.add).then_inc(vec.sem, vec.counts("fill2"))
            v.wait_ge(vec.sem, vec.at("fill2", led.i))
            v.tensor_scalar(count[:, :], count[:, :], 1.0, None, ALU.max).then_inc(vec.sem, vec.counts("count"))
            v.wait_ge(vec.sem, vec.at("count"))
            v.reciprocal(rcount[:, :], count[:, :])
            part_end(v, 1)
            led.part("dense", PASSES)
            with v.Fori(0, PASSES) as i:
                led.i = i
                for L in range(12):
                    if L == 3:
                        for s in range(NS):
                            dve_mid(v, s)
                    for s in range(NS):
                        if L == 0:
                            v.wait_ge(x_in[s].sem, 16 * (i + 1))
                            dve_stats(v, s, 0, lambda j: xin[s][:, j, :])
                            dve_shift(v, s, 0)
                        if L == 2:
                            dve_res2(v, s)
                            dve_shift(v, s, 2)
                        if L == 3:
                            dve_res3(v, s)
                            dve_shift(v, s, 3)
                        if L == 4:
                            dve_elu(v, s, 4)
                        if L == 5:
                            v.wait_ge(rows_a.sem, rows_a.at((s, "row2"), i))
                            dve_res5(v, s, row[s][1][:, :, 0:D])
                            dve_shift(v, s, 5)
                        if 6 <= L <= 10:
                            v.wait_ge(prod.sem, prod.at((s, L - 1), i))
                            q = MADE[L][1]
                            dve_stats(v, s, L, lambda j: O[s][:, j, :])
                            before = {6: 2, 7: 5, 9: 6}.get(L)
                            if before is not None:
                                v.wait_ge(stored[before, s].sem, stored[before, s].at(0, i))
                            dve_norm(v, s, L, lambda j: O[s][:, j, :], zview(s, q, 0, H2)).then_inc(z_dve.sem, z_dve.counts((s, L)))
                        if L == 11:
                            v.wait_ge(prod.sem, prod.at((s, 10), i))
                            v.wait_ge(saved.sem, saved.at("pass", i, back=1))
                            v.tensor_tensor(fin[s][:, :, :], X[s][:, :, :], O[s][:, :, 0:D], ALU.add).then_inc(done.sem, done.counts((s, "out")))
            part_end(v, 2)
            for r in range(8):
                if r in HN:
                    dve_weights(v, r)
                dve_round(v, r)
                part_end(v, 3 + r)

        @block.tensor
        def _(t):
            led.i = 0
            led.part("setup", 1)
            t.wait_ge(pool_c.sem, pool_c.at("cleared"))
            t.wait_ge(weights_in[0].sem, weights_in[0].at("last"))
            t.wait_ge(weights_in[1].sem, weights_in[1].at("last"))
            for k, o, width in ((0, 0, 2 * HEADS), (1, 2 * HEADS, 2)):
                t.transpose(PT[k][:, 0, 0:P], Z[k][1][:, 0, 0:P], ident[:, :])
                ins = t.matmul(O[k][:, 0, 0:width], Z[k][1][:, 0, 0:P], att[:, o:o + width], start=True, stop=True)
            ins.then_inc(pe_c.sem, pe_c.counts("gat"))
            t.wait_ge(vec.sem, vec.at("wide first"))
            t.transpose(PT[2][:, 0, 0:P], acc[0][:, 0, 0:P], ident[:, :]).then_inc(pe_c.sem, pe_c.counts("first"))
            t.wait_ge(vec.sem, vec.at("joint part"))
            t.transpose(PT[3][:, 0, 0:P], chain[:, :], ident[:, :])
            t.matmul(O[2][:, 0, 0:1], chain[:, :], count[:, COLS - 1:COLS], start=True, stop=True).then_inc(pe_c.sem, pe_c.counts("count"))
            part_end(t, 1)
            led.part("dense", PASSES)
            with t.Fori(0, PASSES) as i:
                led.i = i
                for L in range(11):
                    for s in range(NS):
                        layer_pe(t, s, L, MADE[L][0], chunk_rows(L, s), *DENSE[L][1:4])
                        if s:
                            layer_mm(t, s - 1, L, *DENSE[L][1:4], elu=L == 4)
                    layer_mm(t, NS - 1, L, *DENSE[L][1:4], elu=L == 4)
            part_end(t, 2)
            for r in range(8):
                if r in HN:
                    pe_weights(t, r)
                pe_round(t, r)
                part_end(t, 3 + r)
    return led.new


_INS = ["x", "src", "dst", "L0_gnn_W1_l", "L0_gnn_b1", "L0_gnn_W1_r", "L0_gnn_W2_l", "L0_gnn_b2",
        "L0_gnn_W2_r", "L1_gnn_W_l", "L1_gnn_b_l", "L1_gnn_W_r", "L1_gnn_gamma", "L1_gnn_beta",
        "L2_gnn_W1", "L2_gnn_att_src1", "L2_gnn_att_dst1", "L2_gnn_bias1", "L2_gnn_W2",
        "L2_gnn_att_src2", "L2_gnn_att_dst2", "L2_gnn_bias2", "L3_gnn_W1_1", "L3_gnn_b1_1",
        "L3_gnn_g1_1", "L3_gnn_bt1_1", "L3_gnn_W2_1", "L3_gnn_b2_1", "L3_gnn_g2_1", "L3_gnn_bt2_1",
        "L3_gnn_W1_2", "L3_gnn_b1_2", "L3_gnn_g1_2", "L3_gnn_bt1_2", "L3_gnn_W2_2", "L3_gnn_b2_2",
        "L3_gnn_g2_2", "L3_gnn_bt2_2", "L3_gnn_W1_3", "L3_gnn_b1_3", "L3_gnn_g1_3", "L3_gnn_bt1_3",
        "L3_gnn_W2_3", "L3_gnn_b2_3"]


def kernel(**inputs):
    import concourse.bacc as bacc
    from concourse.bass_utils import run_bass_kernel_spmd

    arrays = {n: np.ascontiguousarray(inputs[n]) for n in _INS}
    counts = {"event": {}, "total": {}}
    for _ in range(2):
        nc = bacc.Bacc("TRN2", target_bir_lowering=False, num_devices=1)
        d = {n: nc.dram_tensor("in_" + n, a.shape, mybir.dt.from_np(a.dtype), kind="ExternalInput").ap()
             for n, a in arrays.items()}
        out = nc.dram_tensor("out_0", (N, D), F32, kind="ExternalOutput").ap()
        counts = build(nc, d, out, counts)
    r = run_bass_kernel_spmd(nc, [{"in_" + n: a for n, a in arrays.items()}], core_ids=[0])
    return r.results[0]["out_0"]
```

```python
from contextlib import ExitStack

import numpy as np
import concourse.bass as bass
from concourse import mybir

F32 = mybir.dt.float32
BF16 = mybir.dt.bfloat16
I32 = mybir.dt.int32
ALU = mybir.AluOpType
ACT = mybir.ActivationFunctionType
AX = mybir.AxisListType

P = 128
D = 128
H2 = 256
N = 50000
E = 12500
HEADS = 4
HC = D // HEADS
COLS = -(-E // P)
JOINT = COLS
TILES = 104
J = 2
NS = 4
ROWS = P * J
PASS = ROWS * NS
PASSES = -(-N // PASS)
SHIFT = PASSES * PASS - N
SLOT_PASSES = COLS // (J * NS)
TAIL = (0, 1)
GROUPS = 52
PAIR_A, PAIR_B = (0, 1), (2, 3)
EARLY = (0, 1, 2, "gelu", 3, 4)
LATE = (5, 6, 7, 8, 9, 10)
QUICK = (0, 1, 2, 4)
NOWHERE = 60000
FAR = 1e30
EPS = 1e-5
GAT1W = D + 2 * HEADS
GAT2W = D + 2


class Ledger:

    def __init__(self, plan):
        self.old, self.new = plan, {"event": {}, "total": {}}
        self.replay, self.i, self.now, self.phase = False, 0, None, "early"
        self.parts = [("setup", 1), ("dense", PASSES)]
        for r in range(8):
            if r in (3, 4):
                self.parts += [(f"alphas{r}", TILES // (J * NS)), (f"weights{r}", 1)]
            self.parts += [(f"round{r} first", 1), (f"round{r}", SLOT_PASSES), (f"round{r} tail", 1)]

    def part(self, name, passes):
        assert (name, passes) in self.parts
        self.now, self.phase = name, "early"

    def go(self, i, phase):
        self.i, self.phase = i, phase

    def _total(self, part, phase, signal):
        return self.old["total"].get((part, phase, signal), 0)

    def fired(self, signal, key):
        if self.replay:
            return
        k = (self.now, self.phase, signal)
        n = self.new["total"].get(k, 0) + 1
        self.new["total"][k] = n
        self.new["event"][(self.now, signal, key)] = (self.phase, n)

    def value(self, signal, key, i, back=0):
        if not self.old["total"]:
            return 1
        base = 0
        for name, passes in self.parts:
            if name == self.now:
                break
            base += passes * (self._total(name, "early", signal) + self._total(name, "late", signal))
        early = self._total(self.now, "early", signal)
        per = early + self._total(self.now, "late", signal)
        phase, n = self.old["event"][(self.now, signal, key)]
        at = base + (early if phase == "late" else 0) + n - back * per
        return at + (i * per if not isinstance(i, int) or i else 0)


class Signal:

    def __init__(self, name, sem, ledger, inc=1):
        self.name, self.sem, self.ledger, self.inc = name, sem, ledger, inc

    def counts(self, key):
        self.ledger.fired(self.name, key)
        return self.inc

    def at(self, key, i=0, back=0):
        return self.ledger.value(self.name, key, i, back) * self.inc


def build(nc, d, out, plan):
    led = Ledger(plan)
    ctx = ExitStack()

    def sb(name, shape, dt=F32):
        return ctx.enter_context(nc.sbuf_tensor(name, shape, dt))

    def sig(name, inc=1):
        return Signal(name, ctx.enter_context(nc.semaphore(name)), led, inc)

    def pair(name):
        pairs = [sig(name + "_01"), sig(name + "_23")]
        return [pairs[s // 2] for s in range(NS)]

    def table(name, shape):
        return nc.dram_tensor(name, shape, F32).ap()

    with ctx:
        T = [table("t_h0", (N, D)), table("t_h1", (N, D)), table("t_h2", (N, D)),
             table("t_gat1", (N, GAT1W)), table("t_gat2", (N, GAT2W)), table("t_h5", (N, D)),
             table("t_z6", (N, H2)), table("t_z7", (N, H2)), out]
        WIDTH = [D, D, D, GAT1W, GAT2W, D, H2, H2, D]
        own = table("own", (GROUPS * P, J * H2))
        resid = table("resid", (GROUPS * P, J * D))

        w128 = {n: sb(n, [P, 1, D]) for n in ("w0l1", "w0r1", "w0l2", "w0r2", "w1l", "w1r")}
        wgat1, wgat2 = sb("wgat1", [P, 1, GAT1W]), sb("wgat2", [P, 1, GAT2W])
        w11, w21 = sb("w11", [P, 2, H2]), sb("w21", [P, 2, H2])
        w12, w22 = sb("w12", [P, 4, H2]), sb("w22", [P, 2, H2])
        w13, w23 = sb("w13", [P, 4, H2]), sb("w23", [P, 2, D])
        c11, c12, c13 = sb("c11", [P, 1, H2]), sb("c12", [P, 2, H2]), sb("c13", [P, 2, H2])
        BIASES = [("L0_gnn_b1", D), ("L0_gnn_b2", D), ("L1_gnn_b_l", D), ("L3_gnn_b1_1", H2),
                  ("L3_gnn_b2_1", H2), ("L3_gnn_b1_2", H2), ("L3_gnn_b2_2", H2),
                  ("L3_gnn_b1_3", H2), ("L3_gnn_b2_3", D)]
        at, BIAS_AT = 0, {}
        for name, w in BIASES:
            BIAS_AT[name] = (at, w)
            at += w
        NB = at
        brow = sb("brow", [P, NB], BF16)
        ones = sb("ones", [P, P], BF16)
        bgat1 = sb("bgat1", [P, 1])
        AFF = ["L3_gnn_g1_1", "L3_gnn_bt1_1", "L3_gnn_g2_1", "L3_gnn_bt2_1", "L3_gnn_g1_2",
               "L3_gnn_bt1_2", "L3_gnn_g2_2", "L3_gnn_bt2_2", "L3_gnn_g1_3", "L3_gnn_bt1_3"]
        aff = sb("aff", [P, len(AFF), 2])
        wide = {n: sb("wide_" + n, [P, D]) for n in ("L1_gnn_gamma", "L1_gnn_beta", "L2_gnn_bias2")}
        wide2 = {n: sb("wide_" + n, [P, H2]) for n in
                 ("L3_gnn_g2_1", "L3_gnn_bt2_1", "L3_gnn_g2_2", "L3_gnn_bt2_2")}
        ident = sb("ident", [P, P])
        after = sb("after", [P, P])
        eps = sb("eps", [P, 1])

        src_i, self_i, put_i = sb("src_i", [P, TILES], I32), sb("self_i", [P, TILES], I32), sb("put_i", [P, TILES], I32)
        dst_i = sb("dst_i", [P, 3, COLS], I32)
        dst_f = sb("dst_f", [P, 3, COLS])
        goes_on = sb("goes_on", [P, COLS])
        sel = sb("sel", [P, COLS])
        count = sb("count", [P, TILES])
        rcount, norm = sb("rcount", [P, TILES]), sb("norm", [P, TILES])
        chain = sb("chain", [P, P])
        chain_t = sb("chain_t", [P, P])

        xin = [sb(f"xin{s}", [P, J, D]) for s in range(NS)]
        X = [sb(f"x{s}", [P, J, D]) for s in range(NS)]
        fin = [sb(f"fin{s}", [P, J, D]) for s in range(NS)]
        tmp = [sb(f"tmp{s}", [P, J, D]) for s in range(NS)]
        Pb = [sb(f"pb{s}", [P, J, D]) for s in range(NS)]
        Z = [[sb(f"z{s}_{q}", [P, J, 2 * H2 if q == 0 else H2]) for q in (0, 1)] for s in range(NS)]
        row = [[sb(f"row{s}_{q}", [P, J, (GAT1W, GAT2W)[q]]) for q in (0, 1)] for s in range(NS)]
        hT = [sb(f"hT{s}", [P, 4, ROWS]) for s in range(NS)]
        eb = [sb(f"eb{s}", [P, ROWS]) for s in range(NS)]
        st = [sb(f"st{s}", [P, J, 6]) for s in range(NS)]
        mv = [sb(f"mv{s}", [P, J, 2]) for s in range(NS)]
        lnv = [sb(f"lnv{s}", [P, J]) for s in range(NS)]
        rstd = [sb(f"rstd{s}", [P, J]) for s in range(NS)]
        nmean = [sb(f"nmean{s}", [P, J]) for s in range(NS)]
        msg = [sb(f"msg{s}", [P, J, H2]) for s in range(NS)]
        acc = [sb(f"acc{s}", [P, J, H2]) for s in range(NS)]
        joint = [sb(f"joint{j}", [P, H2]) for j in range(J)]
        bias_f, bias_h = sb("bias_f", [P, NB]), sb("bias_h", [P, NB], BF16)
        att = sb("att", [P, 2 * HEADS + 2])
        same = [sb("same0", [P, COLS]), sb("same1", [P, COLS])]
        cnt = [sb("cnt0", [P, COLS]), sb("cnt1", [P, COLS])]
        col = sb("col", [P, 4])
        alpha = [sb("alpha_src", [P, TILES, 2 * HEADS]), sb("alpha_dst", [P, TILES, 2 * HEADS])]
        weight = [sb("weight_src", [P, TILES, HEADS]), sb("weight_own", [P, TILES, HEADS])]
        top = [sb("top_fwd", [P, COLS, HEADS]), sb("top_bwd", [P, COLS, HEADS]), sb("top_new", [P, COLS, HEADS])]
        edge_top = sb("edge_top", [P, 2, HEADS])
        abuf = [sb(f"abuf{s}", [P, 2, J, 2 * HEADS]) for s in range(NS)]
        den = [sb(f"den{s}", [P, J, HEADS]) for s in range(NS)]
        alpha_i = [[sb(f"alpha_i{k}{q}", [P, TILES], I32) for q in (0, 1)] for k in (0, 1)]
        idx = [sb(f"idx{s}", [P, 3, J], I32) for s in range(NS)]
        O = [ctx.enter_context(nc.psum_tensor(f"o{s}", [P, J, H2], F32)) for s in range(NS)]
        PT = [ctx.enter_context(nc.psum_tensor(f"pt{s}", [P, 2, ROWS], F32)) for s in range(NS)]

        weights_in = [sig(f"weights_in{k}", 16) for k in range(3)]
        x_in = [sig(f"x_in{s}", 16) for s in range(NS)]
        stored = {(k, s): sig(f"stored{k}_{s}", 16) for k in range(9) for s in range(NS)}
        saved = sig("saved")
        out_saved = pair("out_saved")
        means = pair("means")
        x_means, x_vec = pair("x_means"), pair("x_vec")
        logvar = pair("logvar")
        rstds = pair("rstds")
        shift = pair("shift")
        z_dve, z_act = pair("z_dve"), pair("z_act")
        turned = pair("turned")
        flat = pair("flat")
        elu_e = pair("elu_e")
        elu_d = pair("elu_d")
        prod = pair("prod")
        gelu = pair("gelu")
        rows_a = pair("rows_a")
        resid_p = pair("resid_p")
        pool_c = sig("pool_c")
        x_new = pair("x_new")
        done = pair("done")
        vec = pair("vec")
        pe_c = sig("pe_c")
        gate = sig("gate")
        passed = sig("passed")

        def carry(eng):
            if not isinstance(led.i, int):
                eng.sem_inc(passed.sem, 1)

        scattered = sig("scattered")
        msg_used = sig("msg_used")
        hnorm = pair("hnorm")
        joined = sig("joined")
        x_step = sig("x_step")
        x_got = sig("x_got", 16)
        x_kept = sig("x_kept", 16)
        msg_in = [sig(f"msg_in{s}", 16) for s in range(NS)]
        own_in = [sig(f"own_in{s}", 16) for s in range(NS)]
        own_ready = [sig(f"own_ready{s}") for s in range(NS)]
        scatter_out = [sig(f"scatter_out{s}", 16) for s in range(NS)]
        own_out = [sig(f"own_out{s}", 16) for s in range(NS)]
        resid_out = [sig(f"resid_out{s}", 16) for s in range(NS)]
        alpha_in = [sig(f"alpha_in{s}", 16) for s in range(NS)]
        alpha_at = sig("alpha_at")
        tops = sig("tops")


        def part_end(eng, k):
            eng.drain().then_inc(gate.sem, 1)
            eng.wait_ge(gate.sem, 5 * k)

        def dve_stats(v, s, key, view):
            for j in range(J):
                ins = v.bn_stats(st[s][:, j, :], view(j))
            ins.then_inc(vec[s].sem, vec[s].counts(("bn", s, key)))
            v.wait_ge(vec[s].sem, vec[s].at(("bn", s, key), led.i))
            if not isinstance(led.i, int):
                carry(v)
            for j in range(J):
                ins = v.bn_aggr(mv[s][:, j, :], st[s][:, j, :])
            ins.then_inc(means[s].sem, means[s].counts((s, key)))

        def act_rstd(a, s, key):
            of = x_means if key == 0 else means
            a.wait_ge(of[s].sem, of[s].at((s, key), led.i))
            a.activation(lnv[s][:, :], mv[s][:, :, 1], ACT.Ln, bias=eps[:, 0:1]).then_inc(logvar[s].sem, logvar[s].counts((s, key)))
            a.wait_ge(logvar[s].sem, logvar[s].at((s, key), led.i))
            a.activation(rstd[s][:, :], lnv[s][:, :], ACT.Exp, scale=-0.5).then_inc(rstds[s].sem, rstds[s].counts((s, key)))

        def dve_norm(v, s, key, view, dst):
            v.wait_ge(rstds[s].sem, rstds[s].at((s, key), led.i))
            for j in range(J):
                ins = v.tensor_scalar(dst(j), view(j), mv[s][:, j, 0:1], rstd[s][:, j:j + 1],
                                      ALU.subtract, ALU.mult)
            return ins

        def dve_shift(v, s, key):
            v.wait_ge(rstds[s].sem, rstds[s].at((s, key), led.i))
            of = x_means if key == 0 else means
            v.wait_ge(of[s].sem, of[s].at((s, key), led.i))
            v.scalar_tensor_tensor(out=nmean[s][:, :], in0=mv[s][:, :, 0], scalar=-1.0,
                                              in1=rstd[s][:, :], op0=ALU.mult, op1=ALU.mult).then_inc(shift[s].sem, shift[s].counts((s, key)))

        def act_norm_relu(a, s, key, view, dst):
            a.wait_ge(shift[s].sem, shift[s].at((s, key), led.i))
            for j in range(J):
                ins = a.activation(dst(j), view(j), ACT.Relu, bias=nmean[s][:, j:j + 1],
                                   scale=rstd[s][:, j:j + 1])
            ins.then_inc(z_act[s].sem, z_act[s].counts((s, key)))

        def zview(s, q, lo, hi):
            return lambda j: Z[s][q][:, j, lo:hi]

        def layer_pe(t, s, key, ready, chunks, weights, bias, width):
            t.wait_ge(ready[s].sem, ready[s].at((s, key), led.i))
            for h in range(0, len(chunks), 2):
                if h:
                    t.wait_ge(flat[s].sem, flat[s].at((s, key, h - 2), led.i))
                for c in range(h, min(h + 2, len(chunks))):
                    for j in range(J):
                        ins = t.transpose(PT[s][:, c - h, j * P:(j + 1) * P], chunks[c](j), ident[:, :])
                ins.then_inc(turned[s].sem, turned[s].counts((s, key, h)))

        def bias_mm(t, s, bias):
            lo, w = BIAS_AT[bias]
            t.matmul(O[s][:, :, 0:w], ones[:, :], bcast(brow[:, lo:lo + w]), start=True, stop=False)

        def layer_mm(t, s, key, weights, bias, width, elu=False, bias_done=False):
            h = (len(weights) - 1) // 2 * 2
            ready = elu_d if elu else flat
            t.wait_ge(ready[s].sem, ready[s].at((s, key, h), led.i))
            for j in range(J):
                o = O[s][:, j, 0:width]
                if bias and bias_done:
                    assert BIAS_AT[bias][1] == width
                elif bias:
                    lo, w = BIAS_AT[bias]
                    t.matmul(o, ones[:, :], brow[:, lo:lo + w], start=True, stop=False)
                for c, w in enumerate(weights):
                    ins = t.matmul(o, hT[s][:, c, j * P:(j + 1) * P], w[:, 0:width],
                                   start=(c == 0 and not bias),
                                   stop=(c == len(weights) - 1 and (j == J - 1 or not (bias and bias_done))))
            ins.then_inc(prod[s].sem, prod[s].counts((s, key)))

        def act_flat(a, s, key, n, affine=None, elu=False, relu_from=None):
            for h in range(0, n, 2):
                a.wait_ge(turned[s].sem, turned[s].at((s, key, h), led.i))
                if elu:
                    a.activation(eb[s][:, :], PT[s][:, 0, :], ACT.Exp, bias=bgat1[:, 0:1])
                    a.activation(hT[s][:, 0, :], PT[s][:, 0, :], ACT.Relu,
                                            bias=bgat1[:, 0:1]).then_inc(elu_e[s].sem, elu_e[s].counts((s, key, h)))
                elif affine is not None:
                    for c in range(h, min(h + 2, n)):
                        ins = a.activation(hT[s][:, c, :], PT[s][:, c - h, :], ACT.Relu,
                                           bias=aff[:, affine + 1, c:c + 1], scale=aff[:, affine, c:c + 1])
                    ins.then_inc(flat[s].sem, flat[s].counts((s, key, h)))
                else:
                    k = min(2, n - h)
                    a.activation(hT[s][:, h:h + k, :], PT[s][:, 0:k, :], ACT.Relu if relu_from == h else ACT.Copy).then_inc(flat[s].sem, flat[s].counts((s, key, h)))

        def dve_elu(v, s, key):
            v.wait_ge(elu_e[s].sem, elu_e[s].at((s, key, 0), led.i))
            v.tensor_scalar(eb[s][:, :], eb[s][:, :], 1.0, -1.0, ALU.min, ALU.add).then_inc(vec[s].sem, vec[s].counts(("elu", s, key)))
            v.wait_ge(vec[s].sem, vec[s].at(("elu", s, key), led.i))
            v.tensor_tensor(hT[s][:, 0, :], hT[s][:, 0, :], eb[s][:, :], ALU.add).then_inc(elu_d[s].sem, elu_d[s].counts((s, key, 0)))

        W = lambda t: [t[:, c, :] for c in range(t.shape[1])]
        DENSE = [
            (0, W(w128["w0r1"]), "L0_gnn_b1", D, None), (1, W(w128["w0r2"]), "L0_gnn_b2", D, None),
            (2, W(w128["w1r"]), "L1_gnn_b_l", D, None), (3, W(wgat1), None, GAT1W, None),
            (4, W(wgat2), None, GAT2W, "elu"), (5, W(c11), "L3_gnn_b1_1", H2, None),
            (6, W(w21), "L3_gnn_b2_1", H2, 0), (7, W(c12), "L3_gnn_b1_2", H2, 2),
            (8, W(w22), "L3_gnn_b2_2", H2, 4), (9, W(c13), "L3_gnn_b1_3", H2, 6),
            (10, W(w23), "L3_gnn_b2_3", D, 8),
        ]
        MADE = {0: (z_act, 0), 1: (z_act, 1), 2: (z_act, 0), 3: (z_act, 1), 4: (rows_a, None),
                5: (z_act, 1), 6: (z_dve, 0), 7: (z_dve, 1), 8: (z_dve, 0), 9: (z_dve, 1), 10: (z_dve, 0)}
        KEPT = {0: 0, 1: 1, 2: 2, 4: 3, 7: 6, 9: 7}

        def chunk_rows(L, s):
            q = MADE[L][1]
            n = len(DENSE[L][1])
            if L == 4:
                return [lambda j: row[s][0][:, j, 0:D]]
            return [(lambda j, c=c: Z[s][q][:, j, c * D:(c + 1) * D]) for c in range(n)]

        def node0(i, s):
            return i * PASS + s * ROWS - (SHIFT if s == NS - 1 and isinstance(i, int) and i == PASSES - 1 else 0)

        def rows_of(t, i, s):
            return t[bass.ds(node0(i, s), ROWS), :].rearrange("(p j) f -> p j f", j=J)

        def pool_res3(g, s, h, x, own=None):
            if own:
                wait_own(g, *own, s)
                wait_xin(g, *own, s)
                g.wait_ge(gelu[s].sem, gelu[s].at(s, led.i))
                carry(g)
            else:
                g.wait_ge(z_act[s].sem, z_act[s].at((s, 2), led.i))
                carry(g)
                g.wait_ge(x_new[s].sem, x_new[s].at((s, 2), led.i))
                carry(g)
            g.tensor_tensor(Pb[s][:, :, :], x[:, :, :], h, ALU.add).then_inc(resid_p[s].sem, resid_p[s].counts((s, "part")))
            g.wait_ge(resid_p[s].sem, resid_p[s].at((s, "part"), led.i))
            carry(g)
            g.tensor_tensor(Pb[s][:, :, :], Pb[s][:, :, :], bcast(wide["L1_gnn_beta"][:, :]),
                                         ALU.add).then_inc(resid_p[s].sem, resid_p[s].counts((s, 3)))

        def pool_res5(g, s):
            g.wait_ge(x_new[s].sem, x_new[s].at((s, 3), led.i))
            carry(g)
            g.tensor_tensor(Pb[s][:, :, :], X[s][:, :, :], bcast(wide["L2_gnn_bias2"][:, :]),
                                         ALU.add).then_inc(resid_p[s].sem, resid_p[s].counts((s, 5)))

        def dve_res2(v, s):
            v.wait_ge(prod[s].sem, prod[s].at((s, 1), led.i))
            v.scalar_tensor_tensor(out=X[s][:, :, :], in0=O[s][:, :, 0:D], scalar=0.0,
                                              in1=xin[s][:, :, :], op0=ALU.max, op1=ALU.add).then_inc(x_new[s].sem, x_new[s].counts((s, 2)))
            v.wait_ge(x_new[s].sem, x_new[s].at((s, 2), led.i))
            dve_stats(v, s, 2, lambda j: X[s][:, j, :])

        def dve_mid(v, s):
            v.wait_ge(gelu[s].sem, gelu[s].at(s, led.i))
            dve_stats(v, s, "mid", lambda j: tmp[s][:, j, :])

        def dve_res3(v, s):
            v.wait_ge(rstds[s].sem, rstds[s].at((s, "mid"), led.i))
            for j in range(J):
                ins = v.scalar_tensor_tensor(out=tmp[s][:, j, :], in0=tmp[s][:, j, :], scalar=mv[s][:, j, 0:1],
                                             in1=wide["L1_gnn_gamma"][:, :], op0=ALU.subtract, op1=ALU.mult)
            ins.then_inc(vec[s].sem, vec[s].counts(("gamma", s)))
            v.wait_ge(vec[s].sem, vec[s].at(("gamma", s), led.i))
            v.wait_ge(resid_p[s].sem, resid_p[s].at((s, 3), led.i))
            for j in range(J):
                ins = v.scalar_tensor_tensor(out=X[s][:, j, :], in0=tmp[s][:, j, :], scalar=rstd[s][:, j:j + 1],
                                             in1=Pb[s][:, j, :], op0=ALU.mult, op1=ALU.add)
            ins.then_inc(x_new[s].sem, x_new[s].counts((s, 3)))
            v.wait_ge(x_new[s].sem, x_new[s].at((s, 3), led.i))
            dve_stats(v, s, 3, lambda j: X[s][:, j, :])

        def dve_res5(v, s, gat):
            v.wait_ge(resid_p[s].sem, resid_p[s].at((s, 5), led.i))
            v.tensor_tensor(X[s][:, :, :], gat, Pb[s][:, :, :], ALU.add).then_inc(x_new[s].sem, x_new[s].counts((s, 5)))
            v.wait_ge(x_new[s].sem, x_new[s].at((s, 5), led.i))
            dve_stats(v, s, 5, lambda j: X[s][:, j, :])

        def own_w(r):
            return H2 if r >= 6 else D

        def z0_chunks(s, n):
            return [(lambda j, c=c: Z[s][0][:, j, c * D:(c + 1) * D]) for c in range(n)]

        def z1_chunks(s, n):
            return [(lambda j, c=c: Z[s][1][:, j, c * D:(c + 1) * D]) for c in range(n)]

        w = w128
        LAYERS = {
            0: [("a", z0_chunks, [w["w0l1"][:, 0, :], w["w0r1"][:, 0, :]], "L0_gnn_b1", D, None)],
            1: [("a", z0_chunks, [w["w0l2"][:, 0, :], w["w0r2"][:, 0, :]], "L0_gnn_b2", D, None)],
            2: [("a", z0_chunks, [w["w1l"][:, 0, :], w["w1r"][:, 0, :]], "L1_gnn_b_l", D, None),
                ("b", z1_chunks, W(wgat1), None, GAT1W, None)],
            3: [("a", z0_chunks, W(wgat2), None, GAT2W, "elu")],
            4: [],
            5: [("a", z0_chunks, W(w11), "L3_gnn_b1_1", H2, None), ("b", z1_chunks, W(w21), "L3_gnn_b2_1", H2, 0)],
            6: [("a", z0_chunks, W(w12), "L3_gnn_b1_2", H2, None), ("b", z1_chunks, W(w22), "L3_gnn_b2_2", H2, 4)],
            7: [("a", z0_chunks, W(w13), "L3_gnn_b1_3", H2, None), ("b", z1_chunks, W(w23), "L3_gnn_b2_3", D, 8)],
        }
        MSGW = [D, D, D, GAT1W, GAT2W, D, H2, H2]
        SUMW = [D, D, D, D + HEADS, D + 1, D, H2, H2]
        HN = {3: HEADS, 4: 1}
        SENT = {0: (z_act, "out", lambda s: Z[s][1], D), 1: (z_act, "out", lambda s: Z[s][1], D),
                2: (rows_a, "out", lambda s: row[s][0], GAT1W), 3: (rows_a, "out", lambda s: row[s][1], GAT2W),
                4: (z_act, "out", lambda s: Z[s][1], D), 5: (z_dve, "out", lambda s: Z[s][1], H2),
                6: (z_dve, "out", lambda s: Z[s][1], H2), 7: (done, "out", lambda s: fin[s], D)}
        OWN_SAVED = {0: D, 1: D, 2: D, 3: D, 4: D, 5: H2, 6: H2}
        AFFINE = {6: ("L3_gnn_g2_1", "L3_gnn_bt2_1"), 7: ("L3_gnn_g2_2", "L3_gnn_bt2_2")}
        RESID_READ, RESID_SAVED = (0, 1, 2, 4, 7), (1, 2, 4)

        def streams(i):
            return TAIL if isinstance(i, int) and i == SLOT_PASSES else range(NS)

        def tile0(i, s):
            return i * (J * NS) + s * J

        def in_round(r, eng, body):
            led.part(f"round{r}", SLOT_PASSES)
            with eng.Fori(0, SLOT_PASSES) as i:
                led.i = i
                body(i)
            led.part(f"round{r} tail", 1)
            led.i = 0
            body(SLOT_PASSES)

        def in_round_ahead(r, eng, first, body):
            led.part(f"round{r}", SLOT_PASSES)
            first()
            with eng.Fori(0, SLOT_PASSES - 1) as i:
                led.i = i
                body(i, range(NS))
            led.replay = True
            led.i = SLOT_PASSES - 1
            body(SLOT_PASSES - 1, TAIL)
            led.replay = False
            led.part(f"round{r} tail", 1)
            led.i = 0
            body(SLOT_PASSES, ())

        def fetched(eng, signal, s, before, r, i, per=1):
            n = before * (SLOT_PASSES + (s in TAIL))
            eng.wait_ge(signal.sem, (n + 1 + i) * per * 16)
            if eng is nc.sync or eng is nc.gpsimd:
                carry(eng)

        def group_rows(t, i, s, width):
            g0 = i * (NS * P) + s * P
            return t[bass.ds(g0, P), 0:J * width].rearrange("p (j f) -> p j f", j=J)

        msgs_before = lambda r: r
        owns_before = lambda r: r - 1
        resids_before = lambda r: sum(q < r for q in RESID_READ)
        XIN0 = PASSES

        def wait_msg(eng, r, i, s):
            fetched(eng, msg_in[s], s, msgs_before(r), r, i, J)

        def wait_own(eng, r, i, s):
            fetched(eng, own_in[s], s, owns_before(r), r, i)

        def wait_xin(eng, r, i, s):
            eng.wait_ge(x_in[s].sem, (XIN0 + resids_before(r) * (SLOT_PASSES + (s in TAIL)) + i + 1) * 16)
            if eng is nc.sync or eng is nc.gpsimd:
                carry(eng)

        def sp_round(sp, r):
            def load(i, s):
                if r >= 1:
                    w = own_w(r)
                    lo = D if r in (3, 4) else w
                    sp.dma_start(Z[s][0][:, :, lo:lo + w], group_rows(own, i, s, w)).then_inc(own_in[s].sem, 16)
                if r in RESID_READ and r != 7:
                    load_x(i, s)

            def load_x(i, s):
                sp.dma_start(xin[s][:, :, :], group_rows(resid, i, s, D)).then_inc(x_in[s].sem, 16)

            def free(i, s):
                if r == 0:
                    sp.wait_ge(z_act[s].sem, z_act[s].at((s, "a"), led.i))
                    carry(sp)
                if r == 3:
                    sp.wait_ge(z_dve[s].sem, z_dve[s].at((s, "a"), led.i))
                    carry(sp)
                elif r != 4 and r >= 1:
                    last = (len(LAYERS[r][0][2]) - 1) // 2 * 2
                    sp.wait_ge(turned[s].sem, turned[s].at((s, "a", last), led.i))
                    carry(sp)
                if r in (1, 4):
                    sp.wait_ge(x_new[s].sem, x_new[s].at((s, "x"), led.i))
                    carry(sp)
                if r == 2:
                    sp.wait_ge(resid_p[s].sem, resid_p[s].at((s, 3), led.i))
                    carry(sp)

            def first():
                for s in range(NS):
                    load(0, s)
                    if r == 7:
                        load_x(0, s)

            def body(i, ahead):
                here = streams(i)
                for s in ahead:
                    free(i, s)
                    load(i + 1, s)
                for s in here:
                    if r in RESID_SAVED:
                        sp.wait_ge(x_new[s].sem, x_new[s].at((s, 3 if r == 2 else "x"), led.i))
                        carry(sp)
                        sp.dma_start(group_rows(resid, i, s, D), X[s][:, :, :]).then_inc(resid_out[s].sem, resid_out[s].counts(0))
                for s in here:
                    if r in OWN_SAVED:
                        sg, key, buf, _ = SENT[r]
                        sp.wait_ge(sg[s].sem, sg[s].at((s, key), led.i))
                        carry(sp)
                        sp.dma_start(group_rows(own, i, s, OWN_SAVED[r]),
                                                     buf(s)[:, :, 0:OWN_SAVED[r]]).then_inc(own_out[s].sem, own_out[s].counts(0))
                if r == 7:
                    for s in ahead:
                        sp.wait_ge(done[s].sem, done[s].at((s, "out"), led.i))
                        carry(sp)
                        load_x(i + 1, s)
                for s in here:
                    if r in RESID_SAVED:
                        sp.wait_ge(resid_out[s].sem, resid_out[s].at(0, led.i))
                        carry(sp)
                    if r in OWN_SAVED:
                        sp.wait_ge(own_out[s].sem, own_out[s].at(0, led.i))
                        carry(sp)
                sp.nop().then_inc(saved.sem, saved.counts("pass"))

            in_round_ahead(r, sp, first, body)

        def pool_indices(g, s, k, source, i):
            g.tensor_copy(idx[s][:, k, :], source[:, bass.ds(tile0(i, s), J)]).then_inc(pool_c.sem, pool_c.counts((s, k)))
            g.wait_ge(pool_c.sem, pool_c.at((s, k), led.i))
            carry(g)

        def pool_gather(g, s, k, rows, buf, signal):
            for j in range(J):
                g.indirect_dma_start(buf(j), None, rows, bass.IndirectOffsetOnAxis(idx[s][:, k, j:j + 1], 0))\
                    .then_inc(signal.sem, 16)

        def pool_round(g, r):
            def fetch(i, s, c):
                g.tensor_copy(idx[s][:, 0, :], src_i[:, bass.ds(tile0(i, s), J)]).then_inc(pool_c.sem, pool_c.counts((c, s)))
                g.wait_ge(pool_c.sem, pool_c.at((c, s), led.i))
                carry(g)
                if s not in streams(i):
                    return
                pool_gather(g, s, 0, T[r], lambda j: msg[s][:, j, 0:MSGW[r]], msg_in[s])

            def body(i, ahead):
                here = streams(i)
                for s in here:
                    if r == 2:
                        pool_res3(g, s, Z[s][0][:, :, D:2 * D], xin[s], own=(r, i))
                for s in range(NS) if ahead else ():
                    g.wait_ge(msg_used.sem, msg_used.at(s, led.i))
                    carry(g)
                    fetch(i + 1, s, "ahead")
                if r in AFFINE:
                    for s in ahead:
                        pool_own(g, r, i + 1, s)
                for s in here:
                    sg, key, buf, width = SENT[r]
                    pool_indices(g, s, 2, put_i, i)
                    g.wait_ge(sg[s].sem, sg[s].at((s, key), led.i))
                    carry(g)
                    for j in range(J):
                        ins = g.indirect_dma_start(T[r + 1], bass.IndirectOffsetOnAxis(idx[s][:, 2, j:j + 1], 0),
                                                   buf(s)[:, j, 0:width], None,
                                                   bounds_check=N - 1, oob_is_err=False)
                        ins.then_inc(scatter_out[s].sem, scatter_out[s].counts(0))
                for s in here:
                    g.wait_ge(scatter_out[s].sem, scatter_out[s].at(0, led.i))
                    carry(g)
                g.nop().then_inc(scattered.sem, scattered.counts("pass"))

            led.part(f"round{r} first", 1)
            led.i = 0
            if r in HN:
                g.wait_ge(alpha_at.sem, led_total(alpha_at, r))
            for s in range(NS):
                fetch(0, s, "first")
            if r in AFFINE:
                for s in range(NS):
                    pool_own(g, r, 0, s)
            in_round_ahead(r, g, lambda: None, body)

        def own_rows_at(r, i, s):
            return 2 * ((r - 6) * (SLOT_PASSES + (s in TAIL)) + i + 1)

        def pool_own(g, r, i, s):
            own_rows = Z[s][0][:, :, H2:2 * H2]
            wait_own(g, r, i, s)
            g.tensor_tensor(own_rows, own_rows, bcast(wide2[AFFINE[r][0]][:, :]), ALU.mult).then_inc(own_ready[s].sem, 1)
            g.wait_ge(own_ready[s].sem, own_rows_at(r, i, s) - 1)
            carry(g)
            g.tensor_tensor(own_rows, own_rows, bcast(wide2[AFFINE[r][1]][:, :]), ALU.add).then_inc(own_ready[s].sem, 1)

        def column(t, i, s, j):
            return t[:, bass.ds(tile0(i, s) + j, 1)]

        def dve_sums(v, r, i, s):
            w = SUMW[r]
            if s == 1 and isinstance(i, int) and i == SLOT_PASSES:
                v.wait_ge(pe_c.sem, pe_c.at("joint"))
                v.wait_ge(joined.sem, joined.at(0, led.i))
                v.tensor_tensor(joint[0][:, 0:w], joint[0][:, 0:w], joint[1][:, 0:w], ALU.add).then_inc(vec[s].sem, vec[s].counts(("both", s)))
                v.wait_ge(vec[s].sem, vec[s].at(("both", s), led.i))
                v.tensor_tensor(acc[s][:, 0, 0:w], PT[s][:, 0, 0:w], joint[0][:, 0:w], ALU.add).then_inc(vec[s].sem, vec[s].counts(("joint", s)))
                v.wait_ge(vec[s].sem, vec[s].at(("joint", s), led.i))
                v.tensor_copy(acc[s][:, 1, 0:w], acc[s][:, 0, 0:w]).then_inc(msg_used.sem, msg_used.counts(s))
                v.wait_ge(msg_used.sem, msg_used.at(s, led.i))
                return
            def add(j, before):
                return v.scalar_tensor_tensor(out=acc[s][:, j, 0:w], in0=before, scalar=column(goes_on, i, s, j),
                                              in1=msg[s][:, j, 0:w], op0=ALU.mult, op1=ALU.add)

            def join(j):
                return v.scalar_tensor_tensor(out=joint[j][:, 0:w], in0=acc[s][:, j, 0:w], scalar=column(sel, i, s, j),
                                              in1=joint[j][:, 0:w], op0=ALU.mult, op1=ALU.add)

            add(0, acc[(s - 1) % NS][:, 1, 0:w]).then_inc(vec[s].sem, vec[s].counts(("acc", s, 0)))
            v.wait_ge(vec[s].sem, vec[s].at(("acc", s, 0), led.i))
            add(1, acc[s][:, 0, 0:w]).then_inc(msg_used.sem, msg_used.counts(s))
            v.wait_ge(joined.sem, joined.at(s, led.i) - 1)
            join(0)
            v.wait_ge(msg_used.sem, msg_used.at(s, led.i))
            join(1).then_inc(joined.sem, joined.counts(s))

        def dve_affine(v, s, what, view, g, b, relu=True):
            v.tensor_tensor(view, view, bcast(wide2[g][:, :]), ALU.mult).then_inc(vec[s].sem, vec[s].counts((what, "g", s)))
            v.wait_ge(vec[s].sem, vec[s].at((what, "g", s), led.i))
            v.tensor_tensor(view, view, bcast(wide2[b][:, :]), ALU.add).then_inc(vec[s].sem, vec[s].counts((what, "b", s)))
            v.wait_ge(vec[s].sem, vec[s].at((what, "b", s), led.i))
            if relu:
                v.tensor_scalar(view, view, 0.0, None, ALU.max).then_inc(vec[s].sem, vec[s].counts((what, "r", s)))
                v.wait_ge(vec[s].sem, vec[s].at((what, "r", s), led.i))

        def heads(t, n):
            return t.unsqueeze(2).to_broadcast([P, n, D // n])

        def per_head(t, n):
            return t.rearrange("p (h c) -> p h c", h=n)

        def heads_at(t, i, s, j, n):
            return t[:, bass.ds(tile0(i, s) + j, 1), 0:n].rearrange("p t h -> p (t h)")

        def dve_round(v, r):
            n = HN.get(r)

            def stats_of(s, key, layer):
                v.wait_ge(prod[s].sem, prod[s].at((s, layer), led.i))
                dve_stats(v, s, key, lambda j: O[s][:, j, :])

            names = AFFINE.get(r)

            def body(i):
                here = streams(i)
                tail = isinstance(i, int) and i == SLOT_PASSES
                for s in here:
                    wait_msg(v, r, i, s)
                    if names and not (tail and s == 1):
                        dve_affine(v, s, "msg", msg[s][:, :, :], *names)
                    if n and not (tail and s == 1):
                        for j in range(J):
                            p = heads_at(weight[0], i, s, j, n)
                            m = per_head(msg[s][:, j, 0:D], n)
                            v.tensor_tensor(m, m, heads(p, n), ALU.mult)
                            ins = v.tensor_copy(msg[s][:, j, D:D + n], p)
                        ins.then_inc(vec[s].sem, vec[s].counts(("weighted", s)))
                        v.wait_ge(vec[s].sem, vec[s].at(("weighted", s), led.i))
                    dve_sums(v, r, i, s)
                    if r == 0:
                        wait_xin(v, r, i, s)
                        dve_stats(v, s, "own", lambda j: xin[s][:, j, :])
                        dve_shift(v, s, "own")
                    if r >= 1:
                        wait_own(v, r, i, s)
                    if names:
                        v.wait_ge(own_ready[s].sem, own_rows_at(r, i, s))
                    if r <= 2:
                        for j in range(J):
                            ins = v.tensor_scalar(Z[s][0][:, j, 0:D], acc[s][:, j, 0:D], column(rcount, i, s, j),
                                                  None, ALU.mult)
                        ins.then_inc(z_dve[s].sem, z_dve[s].counts((s, "a")))
                    elif r >= 5:
                        w = SUMW[r]
                        v.wait_ge(hnorm[s].sem, hnorm[s].at(s, led.i))
                        for j in range(J):
                            ins = v.scalar_tensor_tensor(out=Z[s][0][:, j, 0:w], in0=acc[s][:, j, 0:w],
                                                         scalar=column(norm, i, s, j), in1=Z[s][0][:, j, 0:w],
                                                         op0=ALU.mult, op1=ALU.subtract)
                        ins.then_inc(z_dve[s].sem, z_dve[s].counts((s, "a")))
                    else:
                        for j in range(J):
                            p = heads_at(weight[1], i, s, j, n)
                            v.tensor_tensor(per_head(tmp[s][:, j, :], n), per_head(Z[s][0][:, j, D:2 * D], n),
                                            heads(p, n), ALU.mult)
                            ins = v.scalar_tensor_tensor(out=den[s][:, j, 0:n], in0=p, scalar=1e-16,
                                                         in1=acc[s][:, j, D:D + n], op0=ALU.add, op1=ALU.add)
                        ins.then_inc(vec[s].sem, vec[s].counts(("den", s)))
                        v.wait_ge(vec[s].sem, vec[s].at(("den", s), led.i))
                        v.tensor_tensor(tmp[s][:, :, :], tmp[s][:, :, :], acc[s][:, :, 0:D], ALU.add)
                        v.reciprocal(den[s][:, :, 0:n], den[s][:, :, 0:n]).then_inc(vec[s].sem, vec[s].counts(("recip", s)))
                        v.wait_ge(vec[s].sem, vec[s].at(("recip", s), led.i))
                        for j in range(J):
                            ins = v.tensor_tensor(per_head(Z[s][0][:, j, 0:D], n), per_head(tmp[s][:, j, :], n),
                                                  heads(den[s][:, j, 0:n], n), ALU.mult)
                        ins.then_inc(z_dve[s].sem, z_dve[s].counts((s, "a")))
                if r in (1, 2, 4, 5, 6, 7):
                    v.wait_ge(scattered.sem, scattered.at("pass", led.i, back=1))
                    v.wait_ge(saved.sem, saved.at("pass", led.i, back=1))
                for s in here:
                    if r == 1:
                        v.wait_ge(prod[s].sem, prod[s].at((s, "a"), led.i))
                        wait_xin(v, r, i, s)
                        v.scalar_tensor_tensor(out=X[s][:, :, :], in0=O[s][:, :, 0:D], scalar=0.0,
                                                          in1=xin[s][:, :, :], op0=ALU.max, op1=ALU.add).then_inc(x_new[s].sem, x_new[s].counts((s, "x")))
                        v.wait_ge(x_new[s].sem, x_new[s].at((s, "x"), led.i))
                        dve_stats(v, s, "x", lambda j: X[s][:, j, :])
                        if s != here[0]:
                            dve_shift(v, s - 1, "x")
                        if s == here[-1]:
                            dve_shift(v, s, "x")
                    if r == 2:
                        dve_mid(v, s)
                    if r == 4:
                        wait_xin(v, r, i, s)
                        v.wait_ge(z_dve[s].sem, z_dve[s].at((s, "a"), led.i))
                        v.tensor_tensor(X[s][:, :, :], xin[s][:, :, :], Z[s][0][:, :, 0:D], ALU.add).then_inc(vec[s].sem, vec[s].counts(("x", s)))
                        v.wait_ge(vec[s].sem, vec[s].at(("x", s), led.i))
                        v.tensor_tensor(X[s][:, :, :], X[s][:, :, :], bcast(wide["L2_gnn_bias2"][:, :]),
                                                   ALU.add).then_inc(x_new[s].sem, x_new[s].counts((s, "x")))
                        v.wait_ge(x_new[s].sem, x_new[s].at((s, "x"), led.i))
                        dve_stats(v, s, "x", lambda j: X[s][:, j, :])
                        if s != here[0]:
                            dve_shift(v, s - 1, "x")
                        if s == here[-1]:
                            dve_shift(v, s, "x")
                    if r >= 5:
                        if s == here[0]:
                            stats_of(s, "b", "a")
                        if s != here[-1]:
                            stats_of(s + 1, "b", "a")
                        dve_norm(v, s, "b", lambda j: O[s][:, j, :], zview(s, 1, 0, H2)).then_inc(z_dve[s].sem, z_dve[s].counts((s, "b")))
                for s in here:
                    if r == 2:
                        dve_res3(v, s)
                        if s != here[0]:
                            dve_shift(v, s - 1, 3)
                        if s == here[-1]:
                            dve_shift(v, s, 3)
                    if r == 3:
                        dve_elu(v, s, "a")
                    if r in (5, 6):
                        if s == here[0]:
                            stats_of(s, "out", "b")
                        if s != here[-1]:
                            stats_of(s + 1, "out", "b")
                        dve_norm(v, s, "out", lambda j: O[s][:, j, :], zview(s, 1, 0, H2)).then_inc(z_dve[s].sem, z_dve[s].counts((s, "out")))
                    if r == 7:
                        v.wait_ge(prod[s].sem, prod[s].at((s, "b"), led.i))
                        wait_xin(v, r, i, s)
                        v.tensor_tensor(fin[s][:, :, :], xin[s][:, :, :], O[s][:, :, 0:D], ALU.add).then_inc(done[s].sem, done[s].counts((s, "out")))

            led.part(f"round{r} first", 1)
            led.i = 0
            v.memset(joint[1][:, :], 0.0)
            v.memset(joint[0][:, :], 0.0).then_inc(joined.sem, joined.counts("cleared"))
            v.memset(acc[NS - 1][:, 1, :], 0.0).then_inc(vec[0].sem, vec[0].counts("zero"))
            v.wait_ge(vec[0].sem, vec[0].at("zero", led.i))
            in_round(r, v, body)

        def pe_round(t, r):
            def body(i):
                here = streams(i)
                if isinstance(i, int) and i == SLOT_PASSES:
                    t.wait_ge(msg_used.sem, msg_used.at(0, led.i))
                    t.matmul(PT[1][:, 0, 0:SUMW[r]], chain[:, :], acc[0][:, 1, 0:SUMW[r]],
                                       start=True, stop=True).then_inc(pe_c.sem, pe_c.counts("joint"))
                for key, rows, weights, bias, width, kind in LAYERS[r]:
                    made = z_dve if key == "a" or r >= 5 else z_act
                    for s in here:
                        if key == "a" and r >= 1 and r != 3:
                            wait_own(t, r, i, s)
                        if r == 0:
                            t.wait_ge(z_act[s].sem, z_act[s].at((s, "a"), led.i))
                        layer_pe(t, s, key, made, rows(s, len(weights)), weights, bias, width)
                        if len(weights) > 2:
                            layer_mm(t, s, key, weights, bias, width, elu=kind == "elu")
                        elif s:
                            layer_mm(t, s - 1, key, weights, bias, width, elu=kind == "elu")
                    if len(weights) <= 2:
                        layer_mm(t, list(here)[-1], key, weights, bias, width, elu=kind == "elu")

            in_round(r, t, body)

        def act_round(a, r):
            def body(i):
                here = streams(i)
                for s in here if r >= 5 else ():
                    w = SUMW[r]
                    if r in AFFINE:
                        a.wait_ge(own_ready[s].sem, own_rows_at(r, i, s))
                    else:
                        wait_own(a, r, i, s)
                    for j in range(J):
                        ins = a.activation(Z[s][0][:, j, 0:w], Z[s][0][:, j, w:2 * w], ACT.Relu,
                                           scale=column(norm, i, s, j))
                    ins.then_inc(hnorm[s].sem, hnorm[s].counts(s))
                if r == 0:
                    for s in here:
                        act_rstd(a, s, "own")
                        a.wait_ge(shift[s].sem, shift[s].at((s, "own"), led.i))
                        for j in range(J):
                            ins = a.activation(Z[s][0][:, j, D:2 * D], xin[s][:, j, :], ACT.Relu,
                                               bias=nmean[s][:, j:j + 1], scale=rstd[s][:, j:j + 1])
                        ins.then_inc(z_act[s].sem, z_act[s].counts((s, "a")))
                for key, rows, weights, bias, width, kind in LAYERS[r]:
                    if r == 2 and key == "a":
                        for s in here:
                            act_flat(a, s, key, len(weights))
                        for s in here:
                            a.wait_ge(prod[s].sem, prod[s].at((s, "a"), led.i))
                            a.activation(tmp[s][:, :, :], O[s][:, :, 0:D], ACT.Gelu).then_inc(gelu[s].sem, gelu[s].counts(s))
                        a.preload_act_table_set("natural_log_exp_and_others")
                        for s in here:
                            act_rstd(a, s, "mid")
                        for s in here:
                            if s == here[0]:
                                act_rstd(a, s, 3)
                            if s != here[-1]:
                                act_rstd(a, s + 1, 3)
                            a.wait_ge(shift[s].sem, shift[s].at((s, 3), led.i))
                            for j in range(J):
                                ins = a.activation(Z[s][1][:, j, 0:D], X[s][:, j, :], ACT.Relu,
                                                   bias=nmean[s][:, j:j + 1], scale=rstd[s][:, j:j + 1])
                            ins.then_inc(z_act[s].sem, z_act[s].counts((s, "b")))
                        continue
                    for s in here:
                        if key == "b" and r >= 5:
                            if s == here[0]:
                                act_rstd(a, s, "b")
                            if s != here[-1]:
                                act_rstd(a, s + 1, "b")
                        act_flat(a, s, key, len(weights), affine=kind if isinstance(kind, int) else None,
                                 elu=kind == "elu", relu_from=2 if key == "a" and r >= 6 else None)
                a.wait_ge(scattered.sem, scattered.at("pass", led.i, back=1))
                a.wait_ge(saved.sem, saved.at("pass", led.i, back=1))
                for s in here:
                    if r == 0:
                        a.wait_ge(prod[s].sem, prod[s].at((s, "a"), led.i))
                        a.activation(Z[s][1][:, :, 0:D], O[s][:, :, 0:D], ACT.Relu).then_inc(z_act[s].sem, z_act[s].counts((s, "out")))
                    if r in (1, 4):
                        if s == here[0]:
                            act_rstd(a, s, "x")
                        if s != here[-1]:
                            act_rstd(a, s + 1, "x")
                        a.wait_ge(shift[s].sem, shift[s].at((s, "x"), led.i))
                        for j in range(J):
                            ins = a.activation(Z[s][1][:, j, 0:D], X[s][:, j, :], ACT.Relu,
                                               bias=nmean[s][:, j:j + 1], scale=rstd[s][:, j:j + 1])
                        ins.then_inc(z_act[s].sem, z_act[s].counts((s, "out")))
                    if r == 2:
                        a.wait_ge(prod[s].sem, prod[s].at((s, "b"), led.i))
                        a.activation(row[s][0][:, :, :], O[s][:, :, 0:GAT1W], ACT.Copy).then_inc(rows_a[s].sem, rows_a[s].counts((s, "out")))
                    if r == 3:
                        a.wait_ge(prod[s].sem, prod[s].at((s, "a"), led.i))
                        a.activation(row[s][1][:, :, :], O[s][:, :, 0:GAT2W], ACT.Copy).then_inc(rows_a[s].sem, rows_a[s].counts((s, "out")))
                    if r in (5, 6):
                        act_rstd(a, s, "out")

            in_round(r, a, body)

        ALPHA_PASSES = TILES // (J * NS)

        def pool_alphas(g, r):
            k, w = r - 3, 2 * HN[r]
            rows = T[r].rearrange("n (a w) -> (n a) w", w=w)
            led.part(f"alphas{r}", ALPHA_PASSES)
            with g.Fori(0, ALPHA_PASSES) as i:
                led.i = i
                for s in range(NS):
                    g.wait_ge(alpha_at.sem, alpha_at.at(s, i, back=1))
                    carry(g)
                    for q in (0, 1):
                        pool_indices(g, s, q, alpha_i[k][q], i)
                        for j in range(J):
                            g.indirect_dma_start(abuf[s][:, q, j, 0:w], None, rows,
                                             bass.IndirectOffsetOnAxis(idx[s][:, q, j:j + 1], 0)).then_inc(alpha_in[s].sem, alpha_in[s].counts("in"))

        def act_alphas(a, r):
            w = 2 * HN[r]
            led.part(f"alphas{r}", ALPHA_PASSES)
            with a.Fori(0, ALPHA_PASSES) as i:
                led.i = i
                for s in range(NS):
                    a.wait_ge(alpha_in[s].sem, alpha_in[s].at("in", i))
                    for q in (0, 1):
                        ins = a.activation(alpha[q][:, bass.ds(tile0(i, s), J), 0:w], abuf[s][:, q, :, 0:w], ACT.Copy)
                    ins.then_inc(alpha_at.sem, alpha_at.counts(s))
            led.part(f"weights{r}", 1)
            led.i = 0
            n = HN[r]
            for q in (0, 1):
                a.wait_ge(vec[0].sem, vec[0].at(("minus max", q)))
                a.activation(weight[q][:, :, 0:n], weight[q][:, :, 0:n], ACT.Exp).then_inc(elu_e[0].sem, elu_e[0].counts(("weight", q)))

        def pe_weights(t, r):
            led.part(f"weights{r}", 1)
            led.i = 0
            for q in (0, 1):
                for h in range(HN[r]):
                    t.wait_ge(vec[0].sem, vec[0].at(("spread", q, h)))
                    ins = t.transpose(PT[q][:, h // 2, (h % 2) * P:(h % 2 + 1) * P], acc[h][:, q, 0:P], ident[:, :])
                ins.then_inc(tops.sem, tops.counts(q))

        def dve_weights(v, r):
            led.part(f"weights{r}", 1)
            led.i = 0
            n = HN[r]
            fwd, bwd, new = (t[:, :, 0:n] for t in top)
            w0, w1 = weight[0][:, :, 0:n], weight[1][:, :, 0:n]
            dst = dst_f[:, 0, :]
            over = lambda m, k: m.unsqueeze(2).to_broadcast([P, k, n])
            v.wait_ge(alpha_at.sem, led_total(alpha_at, r))
            v.tensor_tensor(w0, alpha[0][:, :, 0:n], alpha[1][:, :, n:2 * n], ALU.add)
            v.tensor_tensor(w1, alpha[1][:, :, 0:n], alpha[1][:, :, n:2 * n], ALU.add).then_inc(vec[0].sem, vec[0].counts("logits"))
            v.wait_ge(vec[0].sem, vec[0].at("logits", led.i))
            for q, w in enumerate((w0, w1)):
                ins = v.scalar_tensor_tensor(out=w, in0=w, scalar=0.2, in1=w, op0=ALU.mult, op1=ALU.max)
            ins.then_inc(vec[0].sem, vec[0].counts("leaky"))
            v.wait_ge(vec[0].sem, vec[0].at("leaky", led.i))
            v.tensor_copy(fwd, weight[0][:, 0:COLS, 0:n])
            v.tensor_copy(bwd, weight[0][:, 0:COLS, 0:n]).then_inc(vec[0].sem, vec[0].counts("start"))
            v.wait_ge(vec[0].sem, vec[0].at("start", led.i))
            step = 1
            while step < COLS:
                m = COLS - step
                v.tensor_tensor(same[0][:, 0:m], dst_f[:, 0, step:], dst_f[:, 0, 0:m], ALU.is_equal).then_inc(vec[0].sem, vec[0].counts(("eq", step)))
                v.wait_ge(vec[0].sem, vec[0].at(("eq", step), led.i))
                v.tensor_scalar(same[0][:, 0:m], same[0][:, 0:m], -1.0, FAR, ALU.add, ALU.mult).then_inc(vec[0].sem, vec[0].counts(("far", step)))
                v.wait_ge(vec[0].sem, vec[0].at(("far", step), led.i))
                v.tensor_tensor(new[:, 0:m, :], fwd[:, 0:m, :], over(same[0][:, 0:m], m), ALU.add).then_inc(vec[0].sem, vec[0].counts(("f1", step)))
                v.wait_ge(vec[0].sem, vec[0].at(("f1", step), led.i))
                v.tensor_tensor(new[:, 0:m, :], fwd[:, step:, :], new[:, 0:m, :], ALU.max).then_inc(vec[0].sem, vec[0].counts(("f2", step)))
                v.wait_ge(vec[0].sem, vec[0].at(("f2", step), led.i))
                v.tensor_copy(fwd[:, step:, :], new[:, 0:m, :]).then_inc(vec[0].sem, vec[0].counts(("f3", step)))
                v.wait_ge(vec[0].sem, vec[0].at(("f3", step), led.i))
                v.tensor_tensor(new[:, 0:m, :], bwd[:, step:, :], over(same[0][:, 0:m], m), ALU.add).then_inc(vec[0].sem, vec[0].counts(("b1", step)))
                v.wait_ge(vec[0].sem, vec[0].at(("b1", step), led.i))
                v.tensor_tensor(new[:, 0:m, :], bwd[:, 0:m, :], new[:, 0:m, :], ALU.max).then_inc(vec[0].sem, vec[0].counts(("b2", step)))
                v.wait_ge(vec[0].sem, vec[0].at(("b2", step), led.i))
                v.tensor_copy(bwd[:, 0:m, :], new[:, 0:m, :]).then_inc(vec[0].sem, vec[0].counts(("b3", step)))
                v.wait_ge(vec[0].sem, vec[0].at(("b3", step), led.i))
                step *= 2
            for q, (t, at) in enumerate(((fwd, COLS - 1), (bwd, 0))):
                for h in range(n):
                    v.tensor_scalar(acc[h][:, q, 0:P], ident[:, :], 0.0, t[:, at, h:h + 1], ALU.mult, ALU.add).then_inc(vec[0].sem, vec[0].counts(("spread", q, h)))
                    v.wait_ge(vec[0].sem, vec[0].at(("spread", q, h), led.i))
            v.tensor_tensor(fwd, fwd, bwd, ALU.max).then_inc(vec[0].sem, vec[0].counts("both"))
            v.wait_ge(vec[0].sem, vec[0].at("both", led.i))
            for q, (mask, start) in enumerate(((chain_t, dst_f[:, 0, 0:1]), (chain, dst_f[:, 0, COLS - 1:COLS]))):
                far = fin[0][:, 0, :]
                v.tensor_scalar(far, mask[:, :], -1.0, FAR, ALU.add, ALU.mult).then_inc(vec[0].sem, vec[0].counts(("mask", q)))
                v.wait_ge(vec[0].sem, vec[0].at(("mask", q), led.i))
                v.wait_ge(tops.sem, tops.at(q))
                for h in range(n):
                    v.tensor_tensor(fin[1][:, 0, :], PT[q][:, h // 2, (h % 2) * P:(h % 2 + 1) * P], far, ALU.add).then_inc(vec[0].sem, vec[0].counts(("masked", q, h)))
                    v.wait_ge(vec[0].sem, vec[0].at(("masked", q, h), led.i))
                    v.reduce_max(edge_top[:, q, h:h + 1], fin[1][:, 0, :], AX.X).then_inc(vec[0].sem, vec[0].counts(("edge", q, h)))
                    v.wait_ge(vec[0].sem, vec[0].at(("edge", q, h), led.i))
                v.tensor_scalar(same[0][:, :], dst, start, 1.0, ALU.is_equal, ALU.subtract).then_inc(vec[0].sem, vec[0].counts(("at", q)))
                v.wait_ge(vec[0].sem, vec[0].at(("at", q), led.i))
                v.tensor_scalar(same[0][:, :], same[0][:, :], FAR, None, ALU.mult).then_inc(vec[0].sem, vec[0].counts(("at far", q)))
                v.wait_ge(vec[0].sem, vec[0].at(("at far", q), led.i))
                v.tensor_tensor(new, over(same[0][:, :], COLS),
                                        edge_top[:, q, 0:n].unsqueeze(1).to_broadcast([P, COLS, n]), ALU.add).then_inc(vec[0].sem, vec[0].counts(("e1", q)))
                v.wait_ge(vec[0].sem, vec[0].at(("e1", q), led.i))
                v.tensor_tensor(fwd, fwd, new, ALU.max).then_inc(vec[0].sem, vec[0].counts(("e2", q)))
                v.wait_ge(vec[0].sem, vec[0].at(("e2", q), led.i))
            v.tensor_tensor(fwd, fwd, weight[1][:, 0:COLS, 0:n], ALU.max).then_inc(vec[0].sem, vec[0].counts("own too"))
            v.wait_ge(vec[0].sem, vec[0].at("own too", led.i))
            v.tensor_tensor(weight[1][:, COLS:TILES, 0:n], weight[1][:, COLS:TILES, 0:n],
                            fwd[:, 0:1, :].to_broadcast([P, TILES - COLS, n]), ALU.subtract)
            v.memset(weight[0][:, COLS:TILES, :], 0.0)
            v.tensor_tensor(weight[0][:, 0:COLS, 0:n], weight[0][:, 0:COLS, 0:n], fwd, ALU.subtract).then_inc(vec[0].sem, vec[0].counts(("minus max", 0)))
            v.tensor_tensor(weight[1][:, 0:COLS, 0:n], weight[1][:, 0:COLS, 0:n], fwd, ALU.subtract).then_inc(vec[0].sem, vec[0].counts(("minus max", 1)))
            v.wait_ge(elu_e[0].sem, elu_e[0].at(("weight", 1)))

        def led_total(signal, r):
            return (NS * (r - 2) * ALPHA_PASSES) + NS

        block = ctx.enter_context(nc.Block())
        from_dram = {}

        def loads():
            two = lambda n: d[n].rearrange("(c k) n -> k c n", k=P)
            one = lambda n: d[n].rearrange("(c k) n -> k c n", k=P)
            yield w128["w0l1"][:, :, :], one("L0_gnn_W1_l")
            yield w128["w0r1"][:, :, :], one("L0_gnn_W1_r")
            yield w128["w0l2"][:, :, :], one("L0_gnn_W2_l")
            yield w128["w0r2"][:, :, :], one("L0_gnn_W2_r")
            yield w128["w1l"][:, :, :], one("L1_gnn_W_l")
            yield w128["w1r"][:, :, :], one("L1_gnn_W_r")
            for t, n in ((w11, "L3_gnn_W1_1"), (w21, "L3_gnn_W2_1"), (w12, "L3_gnn_W1_2"),
                         (w22, "L3_gnn_W2_2"), (w13, "L3_gnn_W1_3"), (w23, "L3_gnn_W2_3")):
                yield t[:, :, :], two(n)
            yield Z[0][1][:, 0, 0:D], d["L2_gnn_W1"]
            yield Z[1][1][:, 0, 0:D], d["L2_gnn_W2"]
            yield bgat1[:, :], d["L2_gnn_bias1"].rearrange("(p a) -> p a", a=1)
            for k, n in enumerate(AFF):
                yield aff[:, k, :], d[n].rearrange("(c p) -> p c", p=P)
            for n in wide:
                yield wide[n][:, :], d[n].partition_broadcast(P)
            for n in wide2:
                yield wide2[n][:, :], d[n].partition_broadcast(P)
            for n, (lo, w) in BIAS_AT.items():
                for q in range(3):
                    yield bias_f[32 * q:32 * q + 1, lo:lo + w], d[n].rearrange("(a n) -> a n", a=1)

        def loads_small():
            for k, n in enumerate(("L2_gnn_att_src1", "L2_gnn_att_dst1")):
                for h in range(HEADS):
                    yield att[HC * h:HC * (h + 1), k * HEADS + h:k * HEADS + h + 1], \
                        d[n][h:h + 1, :].rearrange("a c -> c a")
            for k, n in enumerate(("L2_gnn_att_src2", "L2_gnn_att_dst2")):
                yield att[:, 2 * HEADS + k:2 * HEADS + k + 1], d[n].rearrange("a c -> c a")

        def loads_edges():
            cut = E - (P - 1) * COLS
            full = (P - 1) * COLS
            src, dst = d["src"], d["dst"]
            yield src_i[0:P - 1, 0:COLS], src[0:full].rearrange("(p t) -> p t", t=COLS)
            yield src_i[P - 1:P, 0:cut], src[full:E].rearrange("(p t) -> p t", p=1)
            yield dst_i[0:P - 1, 0, :], dst[0:full].rearrange("(p t) -> p t", t=COLS)
            yield dst_i[P - 1:P, 0, 0:cut], dst[full:E].rearrange("(p t) -> p t", p=1)
            yield dst_i[0:1, 1, 1:COLS], dst[0:COLS - 1].rearrange("(p t) -> p t", p=1)
            yield dst_i[1:P - 1, 1, :], dst[COLS - 1:full - 1].rearrange("(p t) -> p t", t=COLS)
            yield dst_i[P - 1:P, 1, 0:cut + 1], dst[full - 1:E].rearrange("(p t) -> p t", p=1)
            yield dst_i[0:P - 1, 2, :], dst[1:full + 1].rearrange("(p t) -> p t", t=COLS)
            yield dst_i[P - 1:P, 2, 0:cut - 1], dst[full + 1:E].rearrange("(p t) -> p t", p=1)

        def bcast(row_tile, j=J):
            return row_tile.unsqueeze(1).to_broadcast([P, j, row_tile.shape[1]])

        @block.sync
        def _(sp):
            led.i = 0
            led.part("setup", 1)
            sp.wait_ge(vec[0].sem, vec[0].at("cleared"))
            sp.wait_ge(pool_c.sem, pool_c.at("cleared"))
            for k, group in enumerate((loads(), loads_small(), loads_edges())):
                for dst, src in group:
                    with nc.allow_non_contiguous_dma(reason="small, once"):
                        sp.dma_start(dst, src).then_inc(weights_in[k].sem, weights_in[k].counts("last"))
                sp.wait_ge(weights_in[k].sem, weights_in[k].at("last"))
            sp.nop().then_inc(saved.sem, saved.counts("pass"))
            part_end(sp, 1)
            led.i = 0
            led.part("dense", PASSES)
            for s in range(NS):
                sp.dma_start(xin[s][:, :, :], rows_of(d["x"], 0, s)).then_inc(x_in[s].sem, 16)

            def store(s, k, key, ready, buf, target):
                sp.wait_ge(ready[s].sem, ready[s].at(key, led.i))
                carry(sp)
                if s == NS - 1 and isinstance(led.i, int) and led.i == PASSES - 1:
                    sp.wait_ge(stored[k, s - 1].sem, stored[k, s - 1].at(0, led.i))
                sp.dma_start(rows_of(target, led.i, s), buf).then_inc(stored[k, s].sem, stored[k, s].counts(0))

            def store_rows(s, L):
                sg, q = MADE[L]
                w = WIDTH[KEPT[L]]
                store(s, KEPT[L], (s, L), sg, row[s][0][:, :, :] if L == 4 else Z[s][q][:, :, 0:w], T[KEPT[L]])

            def last(s, i):
                led.go(i, "late")
                store(s, 8, (s, "out"), done, fin[s][:, :, :], out)

            def last_saved(s, i):
                led.go(i, "late")
                sp.wait_ge(stored[8, s].sem, stored[8, s].at(0, i))
                carry(sp)
                sp.nop().then_inc(out_saved[s].sem, out_saved[s].counts(s))

            def keep_x(q):
                sp.wait_ge(x_got.sem, J * 16 * (q + 1))
                carry(sp)
                sp.dma_start(group_rows(resid, 0, q, D), msg[0][:, :, 0:D]).then_inc(x_kept.sem, 16)

            def half(early, ei, late, li, more=True, ended=True):
                for s in early if ended else ():
                    last(s, ei - 1)
                for E_, L in zip(EARLY, LATE):
                    if E_ == 1 and early == PAIR_A:
                        keep_x(ei)
                    for s in early if ended and E_ == 2 else ():
                        last_saved(s, ei - 1)
                    led.go(li, "late")
                    for s in late:
                        if L == 5:
                            store(s, 4, (s, "row2"), rows_a, row[s][1][:, :, :], T[4])
                            store(s, 5, (s, 5), z_act, Z[s][1][:, :, 0:D], T[5])
                        if L in (7, 9):
                            store_rows(s, L)
                    led.go(ei, "early")
                    for s in early:
                        if E_ in (0, 1, 2, 4):
                            store_rows(s, E_)
                        if E_ == "gelu" and more:
                            sp.wait_ge(x_new[s].sem, x_new[s].at((s, 2), ei))
                            carry(sp)
                            sp.dma_start(xin[s][:, :, :], rows_of(d["x"], ei + 1, s)).then_inc(x_in[s].sem, 16)
            led.replay = True
            half(PAIR_A, 0, (), 0, ended=False)
            half(PAIR_B, 0, PAIR_A, 0, ended=False)
            half(PAIR_A, 1, PAIR_B, 0)
            led.replay = False
            with sp.Fori(1, PASSES - 2) as i:
                half(PAIR_B, i, PAIR_A, i)
                half(PAIR_A, i + 1, PAIR_B, i)
            led.replay = True
            half(PAIR_B, PASSES - 2, PAIR_A, PASSES - 2)
            half(PAIR_A, PASSES - 1, PAIR_B, PASSES - 2, more=False)
            half(PAIR_B, PASSES - 1, PAIR_A, PASSES - 1, more=False)
            for s in PAIR_A:
                last(s, PASSES - 1)
            half((), 0, PAIR_B, PASSES - 1)
            for s in PAIR_B:
                last(s, PASSES - 1)
            for s in range(NS):
                last_saved(s, PASSES - 1)
            keep_x(PASSES)
            sp.wait_ge(x_kept.sem, 16 * (PASSES + 1))
            led.replay = False
            part_end(sp, 2)
            for r in range(8):
                sp_round(sp, r)
                part_end(sp, 3 + r)

        @block.gpsimd
        def _(g):
            led.i = 0
            led.part("setup", 1)
            g.memset(ident[:, :], 0.0)
            g.memset(after[:, :], 1.0)
            g.memset(src_i[:, :], 0)
            g.memset(dst_i[:, :, :], N).then_inc(pool_c.sem, pool_c.counts("cleared0"))
            g.wait_ge(pool_c.sem, pool_c.at("cleared0"))
            g.affine_select(out=ident[:, :], in_=ident[:, :], compare_op=ALU.not_equal, fill=1.0,
                            base=0, pattern=[[-1, P]], channel_multiplier=1)
            g.affine_select(out=after[:, :], in_=after[:, :], compare_op=ALU.is_gt, fill=0.0,
                            base=0, pattern=[[1, P]], channel_multiplier=-1)
            g.memset(dst_i[0:1, 1, 0:1], -1).then_inc(pool_c.sem, pool_c.counts("cleared"))
            g.nop().then_inc(scattered.sem, scattered.counts("none yet"))
            part_end(g, 1)
            led.part("dense", PASSES)

            def gather_x(q):
                g.tensor_copy(idx[0][:, 1, :], self_i[:, bass.ds(q * J, J)]).then_inc(x_step.sem, 1)
                g.wait_ge(x_step.sem, q + 1)
                carry(g)
                pool_gather(g, 0, 1, d["x"], lambda j: msg[0][:, j, 0:D], x_got)

            gather_x(0)
            with g.Fori(0, PASSES) as i:
                led.i = i
                for streams_of in (PAIR_A, PAIR_B):
                    for s in streams_of:
                        pool_res3(g, s, Z[s][0][:, :, 0:D], X[s])
                    for s in streams_of:
                        pool_res5(g, s)
                g.wait_ge(x_kept.sem, 16 * (i + 1))
                carry(g)
                gather_x(i + 1)
            part_end(g, 2)
            for r in range(8):
                if r in HN:
                    pool_alphas(g, r)
                pool_round(g, r)
                part_end(g, 3 + r)

        @block.scalar
        def _(a):
            led.i = 0
            led.part("setup", 1)
            a.preload_act_table_set("natural_log_exp_and_others")
            a.wait_ge(vec[0].sem, vec[0].at("count"))
            a.activation(norm[:, :], count[:, :], ACT.Ln).then_inc(logvar[0].sem, logvar[0].counts("count"))
            a.wait_ge(logvar[0].sem, logvar[0].at("count"))
            a.activation(norm[:, :], norm[:, :], ACT.Exp, scale=-0.5).then_inc(rstds[0].sem, rstds[0].counts("count"))
            for s in range(NS):
                a.nop().then_inc(alpha_at.sem, alpha_at.counts(("none yet", s)))
            part_end(a, 1)
            led.part("dense", PASSES)

            def back(s, L):
                n, kind = len(DENSE[L][1]), DENSE[L][4]
                act_flat(a, s, L, n, affine=kind if isinstance(kind, int) else None, elu=kind == "elu")

            def row2(s):
                a.wait_ge(prod[s].sem, prod[s].at((s, 4), led.i))
                a.activation(row[s][1][:, :, :], O[s][:, :, 0:GAT2W], ACT.Copy).then_inc(rows_a[s].sem, rows_a[s].counts((s, "row2")))

            def half(early, ei, late, li):
                late_turn, ahead = None, False
                led.go(ei, "early")
                for s in early:
                    act_rstd(a, s, 0)
                led.go(li, "late")
                for s in late[0:1]:
                    row2(s)
                led.go(ei, "early")
                for s in early:
                    act_norm_relu(a, s, 0, lambda j: xin[s][:, j, :], zview(s, 0, 0, D))
                led.go(li, "late")
                for s in late[1:2]:
                    row2(s)
                led.go(ei, "early")
                for s in early:
                    back(s, 0)
                led.go(li, "late")
                for s in late:
                    act_rstd(a, s, 5)
                    act_norm_relu(a, s, 5, lambda j: X[s][:, j, :], zview(s, 1, 0, D))
                for s in late:
                    back(s, 5)
                for E_, L in zip(EARLY[1:], LATE[1:]):
                    for k in (0, 1):
                        l, e = late[k:k + 1], early[k:k + 1]
                        led.go(li, "late")
                        for s in l if not ahead else ():
                            act_rstd(a, s, L)
                        ahead = False
                        if late_turn is not None:
                            led.go(ei, "early")
                            back(late_turn, 3)
                            late_turn = None
                        led.go(ei, "early")
                        for s in e:
                            z0 = zview(s, 0, 0, D)
                            if E_ == 1:
                                a.wait_ge(prod[s].sem, prod[s].at((s, 0), led.i))
                                a.activation(Z[s][1][:, :, 0:D], O[s][:, :, 0:D], ACT.Relu).then_inc(z_act[s].sem, z_act[s].counts((s, 1)))
                            if E_ == 2:
                                act_rstd(a, s, 2)
                                a.wait_ge(stored[0, s].sem, stored[0, s].at(0, led.i))
                                act_norm_relu(a, s, 2, lambda j: X[s][:, j, :], z0)
                            if E_ == 4:
                                a.wait_ge(prod[s].sem, prod[s].at((s, 3), led.i))
                                a.activation(row[s][0][:, :, :], O[s][:, :, 0:GAT1W], ACT.Copy).then_inc(rows_a[s].sem, rows_a[s].counts((s, 4)))
                        if E_ == "gelu" and k == 1 and early:
                            for s in early:
                                a.wait_ge(prod[s].sem, prod[s].at((s, 2), led.i))
                                a.activation(tmp[s][:, :, :], O[s][:, :, 0:D], ACT.Gelu).then_inc(gelu[s].sem, gelu[s].counts(s))
                            a.preload_act_table_set("natural_log_exp_and_others")
                        led.go(li, "late")
                        for s in l:
                            back(s, L)
                        led.go(ei, "early")
                        if E_ == "gelu" and k == 1 and late:
                            led.go(li, "late")
                            act_rstd(a, late[0], L + 1)
                            ahead = True
                            led.go(ei, "early")
                        if E_ == "gelu" and k == 1:
                            for s in early:
                                act_rstd(a, s, "mid")
                        if E_ == 3 and late:
                            led.go(li, "late")
                            act_rstd(a, late[1 - k], L + k)
                            ahead = True
                            led.go(ei, "early")
                        for s in e:
                            if E_ == 3:
                                act_rstd(a, s, 3)
                                a.wait_ge(stored[1, s].sem, stored[1, s].at(0, led.i))
                                act_norm_relu(a, s, 3, lambda j: X[s][:, j, :], zview(s, 1, 0, D))
                            if E_ == 3:
                                late_turn = s
                            elif E_ != "gelu":
                                back(s, E_)
                led.go(li, "late")
                for s in late:
                    for k in (2, 3, 4, 5, 6, 7):
                        a.wait_ge(stored[k, s].sem, stored[k, s].at(0, led.i))

            led.replay = True
            half(PAIR_A, 0, (), 0)
            led.replay = False
            with a.Fori(0, PASSES - 1) as i:
                half(PAIR_B, i, PAIR_A, i)
                half(PAIR_A, i + 1, PAIR_B, i)
            led.replay = True
            half(PAIR_B, PASSES - 1, PAIR_A, PASSES - 1)
            half((), 0, PAIR_B, PASSES - 1)
            led.replay = False
            part_end(a, 2)
            for r in range(8):
                if r in HN:
                    act_alphas(a, r)
                act_round(a, r)
                part_end(a, 3 + r)

        @block.vector
        def _(v):
            led.i = 0
            led.part("setup", 1)
            for s in range(NS):
                v.nop().then_inc(out_saved[s].sem, out_saved[s].counts(("none yet", s)))
            for tile, value in ((ones, 1.0), (brow, 0.0), (att, 0.0), (eps, EPS), (same[0], 0.0),
                                (same[1], 0.0)):
                v.memset(tile[:, :], value)
            v.memset(put_i[:, :], NOWHERE).then_inc(vec[0].sem, vec[0].counts("cleared"))
            v.wait_ge(vec[0].sem, vec[0].at("cleared"))
            v.wait_ge(weights_in[0].sem, weights_in[0].at("last"))
            v.tensor_copy(brow[0:1, :], bias_f[0:1, :])
            for r in (32, 64):
                v.tensor_copy(bias_h[r:r + 1, :], bias_f[r:r + 1, :]).then_inc(vec[0].sem, vec[0].counts(("hi", r)))
                v.wait_ge(vec[0].sem, vec[0].at(("hi", r), led.i))
                v.tensor_tensor(bias_f[r:r + 1, :], bias_f[r:r + 1, :], bias_h[r:r + 1, :], ALU.subtract).then_inc(vec[0].sem, vec[0].counts(("rest", r)))
                v.wait_ge(vec[0].sem, vec[0].at(("rest", r), led.i))
            v.tensor_copy(bias_h[64:65, :], bias_f[64:65, :]).then_inc(vec[0].sem, vec[0].counts("mid"))
            v.wait_ge(vec[0].sem, vec[0].at("mid", led.i))
            v.tensor_tensor(bias_f[64:65, :], bias_f[64:65, :], bias_h[64:65, :], ALU.subtract).then_inc(vec[0].sem, vec[0].counts("rest2"))
            v.wait_ge(vec[0].sem, vec[0].at("rest2", led.i))
            v.tensor_copy(brow[32:33, :], bias_f[32:33, :])
            v.tensor_copy(brow[64:65, :], bias_f[64:65, :])
            v.tensor_tensor(c11[:, :, :], w11[:, 1:2, :], w11[:, 0:1, :], ALU.subtract)
            v.tensor_tensor(c12[:, :, :], w12[:, 2:4, :], w12[:, 0:2, :], ALU.subtract)
            v.tensor_tensor(c13[:, :, :], w13[:, 2:4, :], w13[:, 0:2, :], ALU.subtract)
            v.wait_ge(pe_c.sem, pe_c.at("gat"))
            v.tensor_copy(wgat1[:, 0, 0:D], PT[0][:, 0, 0:P])
            v.tensor_copy(wgat2[:, 0, 0:D], PT[1][:, 0, 0:P])
            v.tensor_copy(wgat1[:, 0, D:GAT1W], O[0][:, 0, 0:2 * HEADS])
            v.tensor_copy(wgat2[:, 0, D:GAT2W], O[1][:, 0, 0:2])
            v.wait_ge(weights_in[2].sem, weights_in[2].at("last"))
            v.tensor_copy(dst_f[:, :, :], dst_i[:, :, :]).then_inc(vec[0].sem, vec[0].counts("dst_f"))
            v.wait_ge(vec[0].sem, vec[0].at("dst_f", led.i))
            dst, first, final = dst_f[:, 0, :], dst_f[:, 0, 0:1], dst_f[:, 0, COLS - 1:COLS]
            v.tensor_tensor(goes_on[:, :], dst, dst_f[:, 1, :], ALU.is_equal).then_inc(vec[0].sem, vec[0].counts("on"))
            v.wait_ge(vec[0].sem, vec[0].at("on", led.i))
            v.tensor_copy(col[:, 0:1], goes_on[:, 0:1]).then_inc(vec[0].sem, vec[0].counts("linked"))
            v.wait_ge(vec[0].sem, vec[0].at("linked", led.i))
            v.memset(goes_on[:, 0:1], 0.0)
            v.tensor_scalar(sel[:, :], dst, first, col[:, 0:1], ALU.is_equal, ALU.mult).then_inc(vec[0].sem, vec[0].counts("first"))
            v.wait_ge(vec[0].sem, vec[0].at("first", led.i))
            v.tensor_tensor(same[0][:, :], dst, dst_f[:, 2, :], ALU.not_equal).then_inc(vec[0].sem, vec[0].counts("last"))
            v.wait_ge(vec[0].sem, vec[0].at("last", led.i))
            v.tensor_tensor(sel[:, :], sel[:, :], same[0][:, :], ALU.mult).then_inc(vec[0].sem, vec[0].counts("sel"))
            v.wait_ge(vec[0].sem, vec[0].at("sel", led.i))
            v.tensor_tensor(same[0][:, :], same[0][:, :], sel[:, :], ALU.subtract).then_inc(vec[0].sem, vec[0].counts("main"))
            v.wait_ge(vec[0].sem, vec[0].at("main", led.i))
            v.reduce_sum(col[:, 1:2], sel[:, :], AX.X).then_inc(vec[0].sem, vec[0].counts("has"))
            v.wait_ge(vec[0].sem, vec[0].at("has", led.i))
            v.tensor_scalar(cnt[0][:, :], dst, -float(NOWHERE), None, ALU.add).then_inc(vec[0].sem, vec[0].counts("off"))
            v.wait_ge(vec[0].sem, vec[0].at("off", led.i))
            v.tensor_tensor(cnt[1][:, :], cnt[0][:, :], same[0][:, :], ALU.mult).then_inc(vec[0].sem, vec[0].counts("off2"))
            v.wait_ge(vec[0].sem, vec[0].at("off2", led.i))
            v.tensor_scalar(put_i[:, 0:COLS], cnt[1][:, :], float(NOWHERE), None, ALU.add)
            v.tensor_tensor(col[:, 2:3], cnt[0][:, 0:1], col[:, 1:2], ALU.mult).then_inc(vec[0].sem, vec[0].counts("off3"))
            v.wait_ge(vec[0].sem, vec[0].at("off3", led.i))
            v.tensor_scalar(put_i[:, JOINT:JOINT + 1], col[:, 2:3], float(NOWHERE), None, ALU.add)
            v.tensor_scalar(self_i[:, 0:COLS], dst, float(N - 1), None, ALU.min)
            v.tensor_scalar(same[0][:, 0:TILES - COLS], dst_f[:, 0, 0:TILES - COLS], 0.0, first, ALU.mult, ALU.add).then_inc(vec[0].sem, vec[0].counts("fill"))
            v.wait_ge(vec[0].sem, vec[0].at("fill", led.i))
            v.tensor_scalar(self_i[:, COLS:TILES], same[0][:, 0:TILES - COLS], float(N - 1), None, ALU.min)
            v.memset(col[:, 3:4], 0.0).then_inc(vec[0].sem, vec[0].counts("self_i"))
            v.wait_ge(vec[0].sem, vec[0].at("self_i", led.i))
            for q, rows_i in enumerate((src_i, self_i)):
                for k, w in enumerate((GAT1W // (2 * HEADS), GAT2W // 2)):
                    v.tensor_scalar(alpha_i[k][q][:, :], rows_i[:, :], float(w), float(w - 1), ALU.mult, ALU.add)
            v.tensor_scalar(acc[0][:, 0, 0:P], ident[:, :], 0.0, first, ALU.mult, ALU.add).then_inc(vec[0].sem, vec[0].counts("wide first"))
            v.wait_ge(vec[0].sem, vec[0].at("wide first", led.i))
            v.wait_ge(pe_c.sem, pe_c.at("first"))
            v.scalar_tensor_tensor(out=chain[:, :], in0=PT[2][:, 0, 0:P], scalar=final, in1=after[:, :],
                                           op0=ALU.is_equal, op1=ALU.mult).then_inc(vec[0].sem, vec[0].counts("chain"))
            v.wait_ge(vec[0].sem, vec[0].at("chain", led.i))
            v.tensor_scalar(cnt[0][:, :], dst, 0.0, 1.0, ALU.mult, ALU.add).then_inc(vec[0].sem, vec[0].counts("one"))
            v.wait_ge(vec[0].sem, vec[0].at("one", led.i))
            step = 1
            while step < COLS:
                n = COLS - step
                v.tensor_tensor(same[0][:, 0:n], dst_f[:, 0, step:], dst_f[:, 0, 0:n], ALU.is_equal).then_inc(vec[0].sem, vec[0].counts(("eq", step)))
                v.wait_ge(vec[0].sem, vec[0].at(("eq", step), led.i))
                v.tensor_tensor(same[0][:, 0:n], same[0][:, 0:n], cnt[0][:, 0:n], ALU.mult).then_inc(vec[0].sem, vec[0].counts(("take", step)))
                v.wait_ge(vec[0].sem, vec[0].at(("take", step), led.i))
                v.tensor_tensor(cnt[1][:, step:], cnt[0][:, step:], same[0][:, 0:n], ALU.add).then_inc(vec[0].sem, vec[0].counts(("sum", step)))
                v.wait_ge(vec[0].sem, vec[0].at(("sum", step), led.i))
                v.tensor_copy(cnt[0][:, step:], cnt[1][:, step:]).then_inc(vec[0].sem, vec[0].counts(("back", step)))
                v.wait_ge(vec[0].sem, vec[0].at(("back", step), led.i))
                step *= 2
            v.tensor_copy(count[:, 0:COLS], cnt[0][:, :])
            v.tensor_tensor(cnt[1][:, :], cnt[0][:, :], sel[:, :], ALU.mult).then_inc(vec[0].sem, vec[0].counts("joint part"))
            v.wait_ge(vec[0].sem, vec[0].at("joint part", led.i))
            v.reduce_sum(col[:, 2:3], cnt[1][:, :], AX.X).then_inc(vec[0].sem, vec[0].counts("joint count"))
            v.wait_ge(vec[0].sem, vec[0].at("joint count", led.i))
            v.wait_ge(pe_c.sem, pe_c.at("count"))
            v.tensor_copy(chain_t[:, :], PT[3][:, 0, 0:P])
            v.tensor_tensor(col[:, 3:4], O[2][:, 0, 0:1], col[:, 2:3], ALU.add).then_inc(vec[0].sem, vec[0].counts("joint sum"))
            v.wait_ge(vec[0].sem, vec[0].at("joint sum", led.i))
            v.tensor_scalar(count[:, COLS:TILES], cnt[0][:, 0:TILES - COLS], 0.0, col[:, 3:4], ALU.mult, ALU.add).then_inc(vec[0].sem, vec[0].counts("fill2"))
            v.wait_ge(vec[0].sem, vec[0].at("fill2", led.i))
            v.tensor_scalar(count[:, :], count[:, :], 1.0, None, ALU.max).then_inc(vec[0].sem, vec[0].counts("count"))
            v.wait_ge(vec[0].sem, vec[0].at("count"))
            v.reciprocal(rcount[:, :], count[:, :])
            part_end(v, 1)
            led.part("dense", PASSES)

            def last(s, i):
                led.go(i, "late")
                v.wait_ge(prod[s].sem, prod[s].at((s, 10), led.i))
                v.wait_ge(out_saved[s].sem, out_saved[s].at(s, led.i, back=1))
                v.tensor_tensor(fin[s][:, :, :], X[s][:, :, :], O[s][:, :, 0:D], ALU.add).then_inc(done[s].sem, done[s].counts((s, "out")))

            def x_stats(s, i):
                led.go(i, "early")
                v.wait_ge(x_in[s].sem, 16 * (led.i + 1))
                for j in range(J):
                    ins = v.bn_stats(st[s][:, j, :], xin[s][:, j, :])
                ins.then_inc(x_vec[s].sem, x_vec[s].counts(s))
                v.wait_ge(x_vec[s].sem, x_vec[s].at(s, led.i))
                carry(v)
                for j in range(J):
                    ins = v.bn_aggr(mv[s][:, j, :], st[s][:, j, :])
                ins.then_inc(x_means[s].sem, x_means[s].counts((s, 0)))

            def late_stats(s, L):
                v.wait_ge(prod[s].sem, prod[s].at((s, L - 1), led.i))
                dve_stats(v, s, L, lambda j: O[s][:, j, :])

            def half(early, ei, late, li, ended=True):
                ahead = False
                for s in early if ended else ():
                    last(s, ei - 1)
                led.go(ei, "early")
                for s in early:
                    dve_shift(v, s, 0)
                led.go(li, "late")
                for s in late:
                    v.wait_ge(rows_a[s].sem, rows_a[s].at((s, "row2"), led.i))
                    dve_res5(v, s, row[s][1][:, :, 0:D])
                for s in late:
                    dve_shift(v, s, 5)
                for E_, L in zip(EARLY[1:], LATE[1:]):
                    for k in (0, 1):
                        l, e = late[k:k + 1], early[k:k + 1]
                        led.go(li, "late")
                        for s in l:
                            if not ahead:
                                late_stats(s, L)
                        ahead = False
                        led.go(ei, "early")
                        for s in e:
                            if E_ == 2:
                                dve_res2(v, s)
                        led.go(li, "late")
                        for s in l if L > 5 else ():
                            before = {6: 2, 7: 5, 9: 6}.get(L)
                            if before is not None:
                                v.wait_ge(stored[before, s].sem, stored[before, s].at(0, led.i))
                            dve_norm(v, s, L, lambda j: O[s][:, j, :], zview(s, MADE[L][1], 0, H2)).then_inc(z_dve[s].sem, z_dve[s].counts((s, L)))
                        if (E_, k) == (4, 1) and not (isinstance(li, int) and li == PASSES - 1):
                            for s in late:
                                x_stats(s, li + 1)
                        if (E_ in (3, 4) and (E_, k) != (4, 1) or (E_, k) == ("gelu", 1)) and late:
                            late_stats(late[1 - k], L + k)
                            ahead = True
                        led.go(ei, "early")
                        for s in e:
                            if E_ == 3:
                                dve_res3(v, s)
                            if E_ == 4:
                                dve_elu(v, s, 4)
                            if E_ in (2, 3):
                                dve_shift(v, s, E_)
                        if E_ == "gelu" and k == 1:
                            for s in early:
                                dve_mid(v, s)

            led.replay = True
            for s in range(NS):
                x_stats(s, 0)
            half(PAIR_A, 0, (), 0, ended=False)
            half(PAIR_B, 0, PAIR_A, 0, ended=False)
            half(PAIR_A, 1, PAIR_B, 0)
            led.replay = False
            with v.Fori(1, PASSES - 1) as i:
                half(PAIR_B, i, PAIR_A, i)
                half(PAIR_A, i + 1, PAIR_B, i)
            led.replay = True
            half(PAIR_B, PASSES - 1, PAIR_A, PASSES - 1)
            for s in PAIR_A:
                last(s, PASSES - 1)
            half((), 0, PAIR_B, PASSES - 1)
            for s in PAIR_B:
                last(s, PASSES - 1)
            led.replay = False
            part_end(v, 2)
            for r in range(8):
                if r in HN:
                    dve_weights(v, r)
                dve_round(v, r)
                part_end(v, 3 + r)

        @block.tensor
        def _(t):
            led.i = 0
            led.part("setup", 1)
            t.wait_ge(pool_c.sem, pool_c.at("cleared"))
            t.wait_ge(weights_in[0].sem, weights_in[0].at("last"))
            t.wait_ge(weights_in[1].sem, weights_in[1].at("last"))
            for k, o, width in ((0, 0, 2 * HEADS), (1, 2 * HEADS, 2)):
                t.transpose(PT[k][:, 0, 0:P], Z[k][1][:, 0, 0:P], ident[:, :])
                ins = t.matmul(O[k][:, 0, 0:width], Z[k][1][:, 0, 0:P], att[:, o:o + width], start=True, stop=True)
            ins.then_inc(pe_c.sem, pe_c.counts("gat"))
            t.wait_ge(vec[0].sem, vec[0].at("wide first"))
            t.transpose(PT[2][:, 0, 0:P], acc[0][:, 0, 0:P], ident[:, :]).then_inc(pe_c.sem, pe_c.counts("first"))
            t.wait_ge(vec[0].sem, vec[0].at("joint part"))
            t.transpose(PT[3][:, 0, 0:P], chain[:, :], ident[:, :])
            t.matmul(O[2][:, 0, 0:1], chain[:, :], count[:, COLS - 1:COLS], start=True, stop=True).then_inc(pe_c.sem, pe_c.counts("count"))
            part_end(t, 1)
            led.part("dense", PASSES)

            def mm(s, i, phase, L):
                led.go(i, phase)
                layer_mm(t, s, L, *DENSE[L][1:4], elu=L == 4, bias_done=True)

            def turn(s, i, phase, L):
                led.go(i, phase)
                layer_pe(t, s, L, MADE[L][0], chunk_rows(L, s), *DENSE[L][1:4])
                if DENSE[L][2]:
                    bias_mm(t, s, DENSE[L][2])

            def half(early, ei, late, li):
                for s in early:
                    turn(s, ei, "early", 0)
                for s in early:
                    mm(s, ei, "early", 0)
                for s in late:
                    turn(s, li, "late", 5)
                    mm(s, li, "late", 5)
                before = None
                for E_, L in zip(EARLY[1:], LATE[1:]):
                    for k in (0, 1):
                        l, e = late[k:k + 1], early[k:k + 1]
                        for s in l:
                            turn(s, li, "late", L)
                        if before:
                            mm(*before)
                        if E_ in QUICK and e:
                            turn(e[0], ei, "early", E_)
                        for s in l:
                            mm(s, li, "late", L)
                        if E_ not in QUICK and E_ != "gelu" and e:
                            turn(e[0], ei, "early", E_)
                        before = (e[0], ei, "early", E_) if e and E_ != "gelu" else None
                if before:
                    mm(*before)

            led.replay = True
            half(PAIR_A, 0, (), 0)
            led.replay = False
            with t.Fori(0, PASSES - 1) as i:
                half(PAIR_B, i, PAIR_A, i)
                half(PAIR_A, i + 1, PAIR_B, i)
            led.replay = True
            half(PAIR_B, PASSES - 1, PAIR_A, PASSES - 1)
            half((), 0, PAIR_B, PASSES - 1)
            led.replay = False
            part_end(t, 2)
            for r in range(8):
                if r in HN:
                    pe_weights(t, r)
                pe_round(t, r)
                part_end(t, 3 + r)
    return led.new


_INS = ["x", "src", "dst", "L0_gnn_W1_l", "L0_gnn_b1", "L0_gnn_W1_r", "L0_gnn_W2_l", "L0_gnn_b2",
        "L0_gnn_W2_r", "L1_gnn_W_l", "L1_gnn_b_l", "L1_gnn_W_r", "L1_gnn_gamma", "L1_gnn_beta",
        "L2_gnn_W1", "L2_gnn_att_src1", "L2_gnn_att_dst1", "L2_gnn_bias1", "L2_gnn_W2",
        "L2_gnn_att_src2", "L2_gnn_att_dst2", "L2_gnn_bias2", "L3_gnn_W1_1", "L3_gnn_b1_1",
        "L3_gnn_g1_1", "L3_gnn_bt1_1", "L3_gnn_W2_1", "L3_gnn_b2_1", "L3_gnn_g2_1", "L3_gnn_bt2_1",
        "L3_gnn_W1_2", "L3_gnn_b1_2", "L3_gnn_g1_2", "L3_gnn_bt1_2", "L3_gnn_W2_2", "L3_gnn_b2_2",
        "L3_gnn_g2_2", "L3_gnn_bt2_2", "L3_gnn_W1_3", "L3_gnn_b1_3", "L3_gnn_g1_3", "L3_gnn_bt1_3",
        "L3_gnn_W2_3", "L3_gnn_b2_3"]


def kernel(**inputs):
    import concourse.bacc as bacc
    from concourse.bass_utils import run_bass_kernel_spmd

    arrays = {n: np.ascontiguousarray(inputs[n]) for n in _INS}
    counts = {"event": {}, "total": {}}
    for _ in range(2):
        nc = bacc.Bacc("TRN2", target_bir_lowering=False, num_devices=1)
        d = {n: nc.dram_tensor("in_" + n, a.shape, mybir.dt.from_np(a.dtype), kind="ExternalInput").ap()
             for n, a in arrays.items()}
        out = nc.dram_tensor("out_0", (N, D), F32, kind="ExternalOutput").ap()
        counts = build(nc, d, out, counts)
    r = run_bass_kernel_spmd(nc, [{"in_" + n: a for n, a in arrays.items()}], core_ids=[0])
    return r.results[0]["out_0"]
```
